# Optimizing a Trainium2 kernel written in Bass

```python
import numpy as np
import jax
import jax.numpy as jnp

def _softmax(x, axis=-1):
    return jax.nn.softmax(x, axis=axis)

def _gelu(x):
    return jax.nn.gelu(x, approximate=True)

def _silu(x):
    return jax.nn.silu(x)

def _sigmoid(x):
    return jax.nn.sigmoid(x)

def _layernorm(x, axis=-1, eps=1e-05):
    m = jnp.mean(x, axis=axis, keepdims=True)
    v = jnp.var(x, axis=axis, keepdims=True)
    return (x - m) / jnp.sqrt(v + eps)

def _scatter_add(tgt, idx, src, axis=0):
    return tgt.at[idx].add(src)

def _segment_sum(src, seg, n):
    return jax.ops.segment_sum(src, seg, n)
kernel_name = 'mk_conv_seq_d2_conv_nhwc768_r4_d220d0'

def setup_inputs(seed: int=0):
    np.random.seed(seed)
    _w = jnp.asarray

    def _rec_inputs():
        import jax
        import jax.numpy as jnp
        _gk = jax.random.key(seed)
        x = -0.0004039 + 1 * jax.random.normal(jax.random.fold_in(_gk, 1), (4, 16, 16, 192), jnp.float32)
        return x
    x = _rec_inputs()

    def _L0_conv_setup():
        import jax, jax.numpy as jnp
        import numpy as np
        B, H, W, C = (4, 16, 16, 192)
        NH = 12
        HD = C // NH
        WS = 14
        MLP = 768
        SCALE = HD ** (-0.5)
        EPS = 1e-06

        def _layernorm(x, g, b):
            m = jnp.mean(x, axis=-1, keepdims=True)
            v = jnp.var(x, axis=-1, keepdims=True)
            return (x - m) * jax.lax.rsqrt(v + EPS) * g + b
        key = jax.random.key(seed)
        ks = jax.random.split(key, 8)
        p = lambda k, shape: jax.random.normal(k, shape, jnp.float32) * 0.02
        return {'x': jax.random.normal(ks[0], (B, H, W, C), jnp.float32), 'ln1_g': jnp.ones((C,), jnp.float32), 'ln1_b': jnp.zeros((C,), jnp.float32), 'qkv_w': p(ks[1], (C, 3 * C)), 'qkv_b': jnp.zeros((3 * C,), jnp.float32), 'proj_w': p(ks[2], (C, C)), 'proj_b': jnp.zeros((C,), jnp.float32), 'rel_pos_h': p(ks[3], (2 * WS - 1, HD)), 'rel_pos_w': p(ks[4], (2 * WS - 1, HD)), 'ln2_g': jnp.ones((C,), jnp.float32), 'ln2_b': jnp.zeros((C,), jnp.float32), 'fc1_w': p(ks[5], (C, MLP)), 'fc1_b': jnp.zeros((MLP,), jnp.float32), 'fc2_w': p(ks[6], (MLP, C)), 'fc2_b': jnp.zeros((C,), jnp.float32)}
    _L0_conv_all = _L0_conv_setup()
    _L0_conv_in = {k: v for k, v in _L0_conv_all.items() if k in ('ln1_g', 'ln1_b', 'qkv_w', 'qkv_b', 'proj_w', 'proj_b', 'rel_pos_h', 'rel_pos_w', 'ln2_g', 'ln2_b', 'fc1_w', 'fc1_b', 'fc2_w', 'fc2_b')}
    del _L0_conv_all

    def _L1_conv_setup():
        import jax, jax.numpy as jnp
        import numpy as np

        def _dht(x):
            f = jnp.fft.fftn(x)
            return f.real + f.imag
        key = jax.random.key(seed)
        ks = jax.random.split(key, 5)
        B, H, W, C = (2, 32, 64, 192)
        nb, fac = (8, 1)
        bs = C // nb
        scale = 0.02
        x = jax.random.normal(ks[0], (B, H, W, C), dtype=jnp.float32)
        w1 = scale * jax.random.normal(ks[1], (2, nb, bs, bs * fac), dtype=jnp.float32)
        b1 = scale * jax.random.normal(ks[2], (2, nb, bs * fac), dtype=jnp.float32)
        w2 = scale * jax.random.normal(ks[3], (2, nb, bs * fac, bs), dtype=jnp.float32)
        b2 = scale * jax.random.normal(ks[4], (2, nb, bs), dtype=jnp.float32)
        return {'x': x, 'w1': w1, 'b1': b1, 'w2': w2, 'b2': b2}
    _L1_conv_all = _L1_conv_setup()
    _L1_conv_in = {k: v for k, v in _L1_conv_all.items() if k in ('w1', 'b1', 'w2', 'b2')}
    del _L1_conv_all
    return {'x': x, 'L0_conv_ln1_g': _L0_conv_in['ln1_g'], 'L0_conv_ln1_b': _L0_conv_in['ln1_b'], 'L0_conv_qkv_w': _L0_conv_in['qkv_w'], 'L0_conv_qkv_b': _L0_conv_in['qkv_b'], 'L0_conv_proj_w': _L0_conv_in['proj_w'], 'L0_conv_proj_b': _L0_conv_in['proj_b'], 'L0_conv_rel_pos_h': _L0_conv_in['rel_pos_h'], 'L0_conv_rel_pos_w': _L0_conv_in['rel_pos_w'], 'L0_conv_ln2_g': _L0_conv_in['ln2_g'], 'L0_conv_ln2_b': _L0_conv_in['ln2_b'], 'L0_conv_fc1_w': _L0_conv_in['fc1_w'], 'L0_conv_fc1_b': _L0_conv_in['fc1_b'], 'L0_conv_fc2_w': _L0_conv_in['fc2_w'], 'L0_conv_fc2_b': _L0_conv_in['fc2_b'], 'L1_conv_w1': _L1_conv_in['w1'], 'L1_conv_b1': _L1_conv_in['b1'], 'L1_conv_w2': _L1_conv_in['w2'], 'L1_conv_b2': _L1_conv_in['b2']}

def reference(x, L0_conv_ln1_g, L0_conv_ln1_b, L0_conv_qkv_w, L0_conv_qkv_b, L0_conv_proj_w, L0_conv_proj_b, L0_conv_rel_pos_h, L0_conv_rel_pos_w, L0_conv_ln2_g, L0_conv_ln2_b, L0_conv_fc1_w, L0_conv_fc1_b, L0_conv_fc2_w, L0_conv_fc2_b, L1_conv_w1, L1_conv_b1, L1_conv_w2, L1_conv_b2):
    import jax
    import jax.numpy as jnp

    def _L0_conv_ref(x, ln1_g, ln1_b, qkv_w, qkv_b, proj_w, proj_b, rel_pos_h, rel_pos_w, ln2_g, ln2_b, fc1_w, fc1_b, fc2_w, fc2_b):
        import jax, jax.numpy as jnp
        import numpy as np
        B, H, W, C = (4, 16, 16, 192)
        NH = 12
        HD = C // NH
        WS = 14
        MLP = 768
        SCALE = HD ** (-0.5)
        EPS = 1e-06

        def _layernorm(x, g, b):
            m = jnp.mean(x, axis=-1, keepdims=True)
            v = jnp.var(x, axis=-1, keepdims=True)
            return (x - m) * jax.lax.rsqrt(v + EPS) * g + b
        shortcut = x
        h = _layernorm(x, ln1_g, ln1_b)
        pad_h = -H % WS
        pad_w = -W % WS
        Hp, Wp = (H + pad_h, W + pad_w)
        nwh, nww = (Hp // WS, Wp // WS)
        h = jnp.pad(h, ((0, 0), (0, pad_h), (0, pad_w), (0, 0)))
        xw = h.reshape(B, nwh, WS, nww, WS, C).transpose(0, 1, 3, 2, 4, 5)
        xw = xw.reshape(-1, WS * WS, C)
        Bw = B * nwh * nww
        N = WS * WS
        qkv = xw @ qkv_w + qkv_b
        qkv = qkv.reshape(Bw, N, 3, NH, HD).transpose(2, 0, 3, 1, 4)
        qkv = qkv.reshape(3, Bw * NH, N, HD)
        q, k, v = (qkv[0], qkv[1], qkv[2])
        coords = jnp.arange(WS)[:, None] - jnp.arange(WS)[None, :] + (WS - 1)
        Rh = rel_pos_h[coords]
        Rw = rel_pos_w[coords]
        rq = q.reshape(Bw * NH, WS, WS, HD)
        rel_h = jnp.einsum('bhwc,hkc->bhwk', rq, Rh)
        rel_w = jnp.einsum('bhwc,wkc->bhwk', rq, Rw)
        bias = (rel_h[:, :, :, :, None] + rel_w[:, :, :, None, :]).reshape(Bw * NH, N, N)
        scores = jnp.einsum('bqd,bkd->bqk', q, k) * SCALE + bias
        attn = jax.nn.softmax(scores, axis=-1)
        o = jnp.einsum('bqk,bkd->bqd', attn, v)
        o = o.reshape(Bw, NH, WS, WS, HD).transpose(0, 2, 3, 1, 4).reshape(Bw, WS, WS, C)
        o = o @ proj_w + proj_b
        o = o.reshape(B, nwh, nww, WS, WS, C).transpose(0, 1, 3, 2, 4, 5)
        o = o.reshape(B, Hp, Wp, C)[:, :H, :W, :]
        x1 = shortcut + o
        m = _layernorm(x1, ln2_g, ln2_b)
        m = jax.nn.gelu(m @ fc1_w + fc1_b, approximate=False)
        out = x1 + m @ fc2_w + fc2_b
        return out

    def _L1_conv_ref(x, w1, b1, w2, b2):
        import jax, jax.numpy as jnp
        import numpy as np

        def _dht(x):
            f = jnp.fft.fftn(x)
            return f.real + f.imag
        SPARSITY = 0.01
        FRAC = 1.0
        bias = x
        B, H, W, C = x.shape
        nb = w1.shape[1]
        bs = C // nb
        xf = x.astype(jnp.float32)
        X_k = _dht(xf).reshape(B, H, W, nb, bs)
        X_nk = jnp.roll(jnp.flip(xf, axis=(1, 2)), shift=(1, 1), axis=(1, 2)).reshape(B, H, W, nb, bs)
        total = H // 2 + 1
        kept = int(total * FRAC)
        r0, r1 = (total - kept, min(total + kept, H))
        a = X_k[:, r0:r1, :kept]
        an = X_nk[:, r0:r1, :kept]
        ein = lambda t, w: jnp.einsum('bhwni,nio->bhwno', t, w)
        o1_k = jax.nn.relu(0.5 * (ein(a, w1[0]) - ein(an, w1[1]) + ein(a, w1[1]) + ein(an, w1[0])) + b1[0])
        o1_nk = jax.nn.relu(0.5 * (ein(an, w1[0]) - ein(a, w1[1]) + ein(an, w1[1]) + ein(a, w1[0])) + b1[1])
        o2_k = 0.5 * (ein(o1_k, w2[0]) - ein(o1_nk, w2[1]) + ein(o1_k, w2[1]) + ein(o1_nk, w2[0])) + b2[0]
        o2_nk = 0.5 * (ein(o1_nk, w2[0]) - ein(o2_k, w2[1]) + ein(o1_nk, w2[1]) + ein(o2_k, w2[0])) + b2[1]
        s = o2_k + o2_nk
        s = jnp.sign(s) * jnp.maximum(jnp.abs(s) - SPARSITY, 0.0)
        full = jnp.zeros((B, H, W, nb, bs), jnp.float32).at[:, r0:r1, :kept].set(s)
        full = full.reshape(B, H, W, C)
        out = _dht(full) / full.size
        return out.astype(x.dtype) + bias

    def _gn(v, G=32, eps=1e-05):
        B_, H_, W_, C_ = v.shape
        g = v.reshape(B_, H_, W_, G, C_ // G)
        m = jnp.mean(g, axis=(1, 2, 4), keepdims=True)
        s = jnp.var(g, axis=(1, 2, 4), keepdims=True)
        return ((g - m) / jnp.sqrt(s + eps)).reshape(v.shape)

    def _ln_c(v, eps=1e-06):
        m = jnp.mean(v, axis=-1, keepdims=True)
        s = jnp.var(v, axis=-1, keepdims=True)
        return (v - m) / jnp.sqrt(s + eps)

    def _ln_t(v, eps=1e-05):
        m = jnp.mean(v, axis=-1, keepdims=True)
        s = jnp.var(v, axis=-1, keepdims=True)
        return (v - m) / jnp.sqrt(s + eps)

    def _to_tokens(v):
        B_, H_, W_, C_ = v.shape
        return v.reshape(B_, H_ * W_, C_)

    def _from_tokens(t, like):
        return t.reshape(like.shape)
    x = _L0_conv_ref(x, L0_conv_ln1_g, L0_conv_ln1_b, L0_conv_qkv_w, L0_conv_qkv_b, L0_conv_proj_w, L0_conv_proj_b, L0_conv_rel_pos_h, L0_conv_rel_pos_w, L0_conv_ln2_g, L0_conv_ln2_b, L0_conv_fc1_w, L0_conv_fc1_b, L0_conv_fc2_w, L0_conv_fc2_b)
    x = _L1_conv_ref(x, L1_conv_w1, L1_conv_b1, L1_conv_w2, L1_conv_b2)
    return x

_drawn_inputs = setup_inputs


def setup_inputs(seed=0):
    import zlib

    import numpy as np

    out = dict(_drawn_inputs(seed))
    spreads = {'L0_conv_ln1_g': (1.0, 0.6),
     'L0_conv_ln1_b': (0.0, 0.8),
     'L0_conv_qkv_b': (0.0, 0.283),
     'L0_conv_proj_b': (0.0, 0.1),
     'L0_conv_ln2_g': (1.0, 0.6),
     'L0_conv_ln2_b': (0.0, 0.8),
     'L0_conv_fc1_b': (0.0, 0.285),
     'L0_conv_fc2_b': (0.0, 0.1)}
    factors = {'L0_conv_qkv_w': 6.804,
     'L0_conv_rel_pos_h': 8.0,
     'L0_conv_rel_pos_w': 8.0,
     'L1_conv_w1': 8.0,
     'L1_conv_b1': 64.0,
     'L1_conv_w2': 8.0,
     'L1_conv_b2': 64.0}
    for name, (base, spread) in spreads.items():
        noise = np.random.default_rng([zlib.crc32(name.encode()), seed]).standard_normal(out[name].shape)
        drawn = base * np.exp(spread * noise) if base else spread * noise
        out[name] = jnp.asarray(drawn.astype(out[name].dtype))
    for name, factor in factors.items():
        out[name] = (out[name] * factor).astype(out[name].dtype)
    return out
```

```python
from contextlib import ExitStack

import concourse.bass as bass
from concourse import mybir
import numpy as np

F32 = mybir.dt.float32
F32R = mybir.dt.float32r
ALU = mybir.AluOpType
ACT = mybir.ActivationFunctionType
AX = mybir.AxisListType

B, H, W, C = 4, 16, 16, 192
NH, HD, WS = 12, 16, 14
MLP = 768
EPS = 1e-6
CF = C // 2
NT = B * H * W // 128
HH = NH // 2
WIN = WS * WS
HWIN = WIN // 2
GC = B * WIN
QB, QR, QN = GC, GC + 128, GC + 256
PADB = (WS - 2) * WS
PADR = WS * (WS - 2) + (WS - 2) * 2
KB, KPB = GC, GC + 112
KR = KPB + PADB
KPR = KR + 128
KN = KPR + PADR
BIG = 1e30
NB = 8
BS = C // NB
SHRINK = 0.01
NW = 9
CAS = C + 2


def tables():
    t = {}
    t["ident"] = np.eye(128)
    t["mask6"] = np.repeat(np.eye(HH), HD, axis=0)
    t["half4"] = 0.5 * np.repeat(np.eye(NB // 2), BS, axis=0)
    q = np.zeros((128, QN))
    k = np.zeros((128, KN))

    def key(col, kh, kw):
        for part in range(2):
            k[64 + 2 * kh + part, col] = 1
            k[96 + 2 * kw + part, col] = 1

    k[126:128] = 1
    for b in range(B):
        others = [92 + i for i in range(B) if i != b]
        for h in range(H):
            for w in range(W):
                if h < WS and w < WS:
                    key(b * WIN + h * WS + w, h, w)
                elif w < WS:
                    col = b * 28 + (h - WS) * WS + w
                    key(KB + col, h - WS, w)
                    k[others, KB + col] = -BIG
                    q[92 + b, QB + col] = 1
                else:
                    col = b * 32 + h * 2 + w - WS
                    corner = h >= WS
                    key(KR + col, h % WS, w - WS)
                    k[others, KR + col] = -BIG
                    k[124 if corner else 125, KR + col] = -BIG
                    q[92 + b, QR + col] = 1
                    q[125 if corner else 124, QR + col] = 1
    n = KPB
    for kh in range(2, WS):
        for kw in range(WS):
            key(n, kh, kw)
            n += 1
    n = KPR
    for kh in range(WS):
        for kw in range(2, WS):
            key(n, kh, kw)
            n += 1
    for kh in range(2, WS):
        for kw in range(2):
            key(n, kh, kw)
            k[124, n] = -BIG
            n += 1
    t["qrows"], t["krows"] = q, k
    w = np.arange(W)
    tw = np.zeros((W, 8, 2))
    tw[:, 0, 0] = 1
    tw[:, 0, 1] = np.cos(np.pi * w)
    for j in range(1, 8):
        tw[:, j, 0] = np.cos(2 * np.pi * j * w / W)
        tw[:, j, 1] = np.sin(2 * np.pi * j * w / W)
    fw = np.zeros((8, W, 8, 2, 8))
    for h in range(8):
        fw[h, :, :, :, h] = tw
    kept = [0, 8] + list(range(1, 8))
    flip = np.zeros((8, W, NW, 8))
    for h in range(8):
        for v, f in enumerate(kept):
            flip[h, (-f) % W, v, 7 - h] = 1
    t["fw"] = np.concatenate([fw.reshape(128, 128), flip.reshape(128, NW * 8)], 1)
    c, f = np.meshgrid(np.arange(C), np.arange(CAS) % C, indexing="ij")
    a = 2 * np.pi * ((c * f) % C) / C
    t["cas"] = (np.cos(a) - np.sin(a)).reshape(2, CF, CAS).transpose(1, 0, 2)
    b, h = np.meshgrid(np.arange(B), np.arange(H), indexing="ij")
    b, h = b.ravel(), h.ravel()
    u = (h + 9) % H
    g = 2 * np.pi * ((b[:, None] * b[None] * 4 + h[:, None] * u[None]) % 16) / 16
    cg, sg = np.cos(g), np.sin(g)
    z = np.zeros((64, 64))
    t["fg"] = np.concatenate([np.block([[cg, z], [z, cg]]), np.block([[-sg, z], [z, -sg]]),
                              np.concatenate([cg, -sg]), np.concatenate([-sg, -cg])], 1)
    cg, sg = cg.T, sg.T
    t["ig"] = np.concatenate([np.block([[cg, z], [z, cg]]), np.block([[-sg, z], [z, -sg]]),
                              np.block([[cg, cg], [-sg, sg]]), np.block([[-sg, -sg], [-cg, cg]])], 1)
    for name, m in (("iw14", 14), ("iw8", 8)):
        iw = np.zeros((NW, m, 8, 2, m))
        for v, f in enumerate(kept):
            for x in range(m):
                iw[v, x, :, :, x] = tw[f]
        t[name] = iw.reshape(NW * m, 16 * m)
    return {n: np.ascontiguousarray(v, np.float32) for n, v in t.items()}


def bank_order():
    count, place = [0] * 8, {}

    def add(key, bank):
        place[key] = (bank, count[bank])
        count[bank] += 1

    turn = [0]

    def rotate(keys):
        for key in keys:
            add(key, turn[0] % 8)
            turn[0] += 1

    rotate([("relp", a) for a in range(2)])
    rotate([("hT", bp, f) for bp in range(2) for f in range(2)])
    for f in range(2):
        rotate([("q", f, g) for g in range(3)])
        rotate([("k", f, g) for g in range(3)])
        rotate([("rel", f, a, p) for a in range(2) for p in range(2)])
    rotate([("v", n) for n in range(6)])
    for h in range(NH):
        for u in range(6):
            add(("S", h, u), u % 2)
            add(("E", h, u), 2 + u % 2)
        add(("pvg", h), 4 + h % 2)
        if h % 2 == 0:
            add(("pvw", h // 2), 6)
        add(("mx", h), 7)
    turn[0] = 0
    rotate([("eT", u, n) for u in range(2) for n in range(3)] + [("wT", n) for n in range(2)])
    rotate([("oT", f, bp) for bp in range(3) for f in range(2)])
    rotate([("pr", n) for n in range(4)])
    rotate([("mT", bp, f) for bp in range(2) for f in range(2)])
    rotate(["w2T", "w2p", "b2w"])
    rotate([("f1", n, m) for n in range(2) for m in range(6)])
    rotate([("f2", n) for n in range(4)])
    rotate([("fa", n, f) for n in range(4) for f in range(2)])
    rotate([("fb", n) for n in range(4)])
    rotate([("fc", f, p) for f in range(2) for p in range(2)])
    rotate([("m1", f, x, p) for f in range(2) for x in range(2) for p in range(2)])
    rotate([("m2", n) for n in range(3)])
    rotate([("ia", f, n) for n in range(3) for f in range(2)])
    rotate([("ib", n) for n in range(4)])
    rotate([("ic", n) for n in range(4)])
    return place


def build(nc, a):
    place = bank_order()
    ctx = ExitStack()
    with ctx:
        def sb(name, shape, dt=F32):
            return ctx.enter_context(nc.sbuf_tensor(name, shape, dt))

        def sem(name):
            return ctx.enter_context(nc.semaphore(name))

        bank = [ctx.enter_context(nc.psum_tensor(f"bank{i}", [128, 512], F32)) for i in range(8)]
        bank_full = [sem(f"bank_full{i}") for i in range(8)]
        bank_free = [sem(f"bank_free{i}") for i in range(8)]

        def ps(key):
            return bank[place[key][0]]

        def filled(key):
            return bank_full[place[key][0]]

        def emptied(key):
            return bank_free[place[key][0]]

        def is_full(key):
            return bank_full[place[key][0]], place[key][1] + 1

        def is_read(key):
            return bank_free[place[key][0]], place[key][1] + 1

        def is_free(key):
            return bank_free[place[key][0]], place[key][1]

        ident = sb("ident", [128, 128])
        mask6 = sb("mask6", [CF, HH])
        xt = sb("xt", [128, NT, C])
        wqkv = sb("wqkv", [CF, 2, 3 * C])
        ln1 = sb("ln1", [CF, 2, 2])
        ln2 = sb("ln2", [CF, 2, 2])
        bqkv = sb("bqkv", [CF, 6])
        bk4 = sb("bk4", [CF, 2])
        bv = sb("bv", [128, C])
        pb = sb("pb", [128, C])
        f2b = sb("f2b", [128, C])
        f1b = sb("f1b", [128, 6])
        relpos = sb("relpos", [2 * WS - 1, 2, HH, HD])
        stats = sb("stats", [128, 2, NT, 6])
        mv = sb("mv", [128, 2, NT, 2])
        veps = sb("veps", [128, 2, NT])
        rstd = sb("rstd", [128, 2, NT])
        mhalf = sb("mhalf", [128, NT])
        wproj = sb("wproj", [CF, 2, C])
        wf1 = sb("wf1", [CF, 2, MLP])
        wf2 = sb("wf2", [128, 6, C])
        half4 = sb("half4", [CF, NB // 2])
        w12 = sb("w12", [CF, 2, 2, 2, BS])
        b1c = sb("b1c", [CF, 2, 2])
        b20c = sb("b20c", [CF, 2])
        b2r = sb("b2r", [128, 2, C])
        NOP = 4
        qop = sb("qop", [128, NOP, QN], F32R)
        kop = sb("kop", [128, NOP, KN], F32R)
        negmax = sb("negmax", [128, 2, 10])
        negmax2 = sb("negmax2", [128, 2, 20])
        maxg = sb("maxg", [16, 2, HWIN], F32R)
        maxw = sb("maxw", [4, 2, 128], F32R)

        ARENA = 34200
        arena = sb("arena", [128, ARENA])

        def layout(*items):
            views, at = [], 0
            for rows, dims, dt in items:
                n = int(np.prod(dims))
                v = arena[0:rows, at:at + n]
                if dt is not F32:
                    v = v.bitcast(dt)
                names = "abcdefg"[:len(dims)]
                if len(dims) > 1:
                    v = v.rearrange(f"p ({' '.join(names)}) -> p {' '.join(names)}",
                                    **{names[i]: dims[i] for i in range(len(dims))})
                views.append(v)
                at += n
            assert at <= ARENA, at
            return views

        (relc, q2, k2, relw, qf, h1t, vaug, ev, evw, pg, pwb, pwr) = layout(
            (84, (2, 2, 2, QN), F32R),
            (CF, (2, 2, QN), F32R),
            (CF, (2, 2, KN), F32R),
            (CF, (2, WS, 84), F32),
            (CF, (2, 1024), F32),
            (CF, (2, QN), F32),
            (128, (11, NH, 32), F32),
            (128, (NH, WIN), F32),
            (128, (NH // 2, 128), F32),
            (HWIN, (B, 2 * WIN), F32),
            (112, (3 * 128,), F32),
            (128, (3 * 128,), F32))
        xn_at = 2 * 2 * 2 * QN + 2 * 2 * QN + 2 * 2 * KN + 2 * WS * 84 + 2 * 1024 + 2 * QN + 11 * NH * 32
        xn = arena[:, xn_at:xn_at + NT * C].rearrange("p (t c) -> p t c", t=NT)
        rows_at = xn_at + NT * C
        rows_k = arena[64:128, rows_at:rows_at + KN]
        rows_q = arena[64:128, rows_at + KN:rows_at + KN + QN]

        (on, onw, rden, rdenw, ot, x1, x1b, x1n, h2t, gl, y, consts) = layout(
            (HWIN, (2, B, C), F32),
            (128, (2, C), F32),
            (HWIN, (2, NH, B), F32),
            (128, (NH, 2), F32),
            (CF, (2, 1024), F32),
            (128, (NT, C), F32),
            (128, (NT, C), F32),
            (128, (NT, C), F32),
            (CF, (2, 1024), F32),
            (128, (6, 1024), F32),
            (128, (NT, C), F32),
            (128, (200 + 2 * CAS + 384 + 512 + 224 + 128,), F32))
        at = 0

        def take(rows, n):
            nonlocal at
            at += n
            return consts[0:rows, at - n:at]

        fw = take(128, 200)
        cas = take(CF, 2 * CAS).rearrange("p (f c) -> p f c", f=2)
        fg = take(128, 384)
        ig = take(128, 512)
        iw14 = take(NW * 14, 224)
        iw8 = take(NW * 8, 128)
        x1_at = 2 * B * C + 2 * C + 2 * NH * B + NH // 2 * 4 + 2 * 1024
        gl_at = x1_at + 3 * NT * C + 2 * 1024
        tail = gl_at + 6 * 1024 + NT * C + at

        def behind(rows, dims):
            nonlocal tail
            n = int(np.prod(dims))
            v = arena[0:rows, tail:tail + n]
            tail += n
            assert tail <= ARENA, tail
            names = "abcdefg"[:len(dims)]
            return v.rearrange(f"p ({' '.join(names)}) -> p {' '.join(names)}",
                               **{names[i]: dims[i] for i in range(len(dims))}) if len(dims) > 1 else v

        wsum = behind(CF, (2, 2, 2, BS))
        wbd = behind(CF, (2, 2, 2, CF))
        w2t = behind(CF, (2, 2, CF))
        wps = behind(CF, (2, CF))
        wab = behind(CF, (2, 2, CF))
        bsum = behind(128, (C,))
        bs = behind(128, (C,))
        ya = behind(CF, (2, 1024))
        an = behind(CF, (2, NW * 64))
        fbp = behind(128, (8, C))
        fbf = behind(128, (8, C))
        dk = behind(CF, (2, NW * 64))
        o1 = behind(CF, (2, 2, NW * 64))
        sm, sc, ss = (arena[0:126, gl_at + i * 5 * C:gl_at + (i + 1) * 5 * C].rearrange("p (t c) -> p t c", t=5)
                      for i in range(3))
        iv = arena[0:CF, gl_at + 15 * C:gl_at + 15 * C + 2048].rearrange("p (f n) -> p f n", f=2)
        ibq = arena[:, x1_at:x1_at + 8 * CAS].rearrange("p (j c) -> p j c", j=8)
        y2 = xt
        res = x1n

        x_in = [sem(f"x_in{i}") for i in range(2)]
        small_in = sem("small_in")
        bqkv_in = sem("bqkv_in")
        weights_in = sem("weights_in")
        rel_in = sem("rel_in")
        wqkv_in = sem("wqkv_in")
        bv_in = sem("bv_in")
        rows_in = sem("rows_in")
        late_in = sem("late_in")
        tables_in = sem("tables_in")
        rows_set = sem("rows_set")
        rows_copied = sem("rows_copied")
        set_up = sem("set_up")
        stats_done = sem("stats_done")
        mean_done = sem("mean_done")
        veps_done = sem("veps_done")
        rstd_done = sem("rstd_done")
        xn_done = sem("xn_done")
        k_scaled = sem("k_scaled")
        q_high = sem("q_high")
        k_high = sem("k_high")
        r_high = sem("r_high")
        k_padded = sem("k_padded")
        v_padded = sem("v_padded")
        q_loaded = [sem(f"q_loaded{i}") for i in range(NOP)]
        k_loaded = [sem(f"k_loaded{i}") for i in range(NOP)]
        r_loaded = [sem(f"r_loaded{i}") for i in range(NOP)]
        max_found = sem("max_found")
        max_high = sem("max_high")
        max_split = sem("max_split")
        max_loaded = [sem(f"max_loaded{i}") for i in range(2)]
        pvw_even = sem("pvw_even")
        xpb_done = sem("xpb_done")
        rden_done = sem("rden_done")
        x1n_done = sem("x1n_done")
        x1b_done = sem("x1b_done")
        y_stored = sem("y_stored")
        y2_in = sem("y2_in")
        wsum_done = sem("wsum_done")
        wbd_done = sem("wbd_done")
        wps_done = sem("wps_done")
        bsum_done = sem("bsum_done")
        wab_half = sem("wab_half")
        fb_kept = sem("fb_kept")
        ib_kept = sem("ib_kept")
        clipped = sem("clipped")
        shrunk = sem("shrunk")
        out_stored = sem("out_stored")

        xd = a["x"].rearrange("b (t h) w c -> (h w) (b t) c", t=2)
        scratch = a["scratch"]
        sd = scratch.rearrange("b (t h) w c -> (h w) (b t) c", t=2)

        GROUPS = [(0, 2 * WIN), (2 * WIN, 4 * WIN), (GC, QN)]

        def win(t, piece, b0, nb):
            if piece == "G":
                return t[:, b0 * WIN:(b0 + nb) * WIN].rearrange("p (b h w) -> p b h w", b=nb, h=WS)
            if piece == "B":
                return t[:, QB + b0 * 28:QB + (b0 + nb) * 28].rearrange("p (b h w) -> p b h w", b=nb, h=2)
            return t[:, QR + b0 * 32:QR + (b0 + nb) * 32].rearrange("p (b h w) -> p b h w", b=nb, h=H)

        def nat(t, piece, nb):
            v = t.rearrange("p (b h w) -> p b h w", b=nb, h=H)
            return {"G": v[:, :, 0:WS, 0:WS], "B": v[:, :, WS:H, 0:WS], "R": v[:, :, :, WS:W]}[piece]

        def raw(t):
            return t.bitcast(F32)

        def rel_pieces(axis, part, p, t):
            lo, n = 8 * p, min(8, WS - 8 * p)
            g = t[:, 0:GC].rearrange("p (b h w) -> p b h w", b=B, h=WS)
            bt = t[:, QB:QB + 112].rearrange("p (b h w) -> p b h w", b=B, h=2)
            r = t[:, QR:QN].rearrange("p (b h w) -> p b h w", b=B, h=H)
            s = part.rearrange("p (l b m) -> p l b m", l=8, b=B)
            if axis == 0:
                out = [(s[:, 0:n, :, 0:WS], g[:, :, lo:lo + n].rearrange("p b h w -> p h b w")),
                       (s[:, :, :, WS:W], r[:, :, lo:lo + 8].rearrange("p b h w -> p h b w"))]
                if p == 1:
                    out.append((s[:, 6:8, :, 0:WS], bt.rearrange("p b h w -> p h b w")))
            else:
                out = [(s[:, 0:n, :, 0:WS], g[:, :, :, lo:lo + n].rearrange("p b h w -> p w b h")),
                       (s[:, 0:n, :, WS:H], bt[:, :, :, lo:lo + n].rearrange("p b h w -> p w b h"))]
                if p == 1:
                    out.append((s[:, 6:8], r.rearrange("p b h w -> p w b h")))
            return out

        block = ctx.enter_context(nc.Block())

        @block.sync
        def _(sp):
            for i in range(2):
                sp.dma_start(xt[:, 4 * i:4 * i + 4], xd[:, 4 * i:4 * i + 4]).then_inc(x_in[i], 16)
            sp.dma_start(wqkv[:], a["qkv_w"].rearrange("(f p) n -> p f n", f=2)).then_inc(wqkv_in, 16)
            sp.dma_start(rows_k, a["krows"][64:128, :]).then_inc(rows_in, 16)
            sp.dma_start(rows_q, a["qrows"][64:128, :]).then_inc(rows_in, 16)
            sp.dma_start(wproj[:], a["proj_w"].rearrange("(f p) n -> p f n", f=2)).then_inc(weights_in, 16)
            sp.dma_start(wf1[:], a["fc1_w"].rearrange("(f p) n -> p f n", f=2)).then_inc(weights_in, 16)
            sp.dma_start(wf2[:], a["fc2_w"].rearrange("(m p) n -> p m n", m=6)).then_inc(weights_in, 16)
            sp.wait_ge(rows_set, 2)
            for i in range(1, NOP):
                sp.dma_start(raw(kop[64:128, i]), raw(kop[64:128, 0])).then_inc(rows_copied, 16)
                sp.dma_start(raw(qop[64:128, i]), raw(qop[64:128, 0])).then_inc(rows_copied, 16)
            for h in range(NH):
                f, j, o = h // HH, h % HH, h % NOP
                if h >= NOP:
                    sp.wait_ge(*is_full(("E", h - NOP, 4)))
                    sp.wait_ge(*is_full(("E", h - NOP, 5)))
                p0, p1 = HD * j, HD * (j + 1)
                for g in range(3):
                    sp.wait_ge(*is_read(("q", f, g)))
                for part in range(2):
                    src = q2[p0:p1, f, part, None, :].to_broadcast([HD, 2, QN])
                    sp.dma_start(raw(qop[32 * part:32 * part + 32, o]), raw(src)).then_inc(q_loaded[o], 16)
                for g in range(3):
                    sp.wait_ge(*is_read(("k", f, g)))
                sp.wait_ge(k_padded, 2 * (f + 1))
                for copy in range(2):
                    sp.dma_start(raw(kop[32 * copy:32 * copy + 32, o]), raw(k2[p0:p1, f])).then_inc(k_loaded[o], 16)
                if h == 1:
                    sp.wait_ge(*is_full(("rel", 1, 1, 1)))
                    for dst, src in ((fw, a["fw"]), (cas, a["cas"]), (fg, a["fg"]), (ig, a["ig"]),
                                     (iw14, a["iw14"]), (iw8, a["iw8"])):
                        sp.dma_start(dst, src).then_inc(tables_in, 16)
            for n in range(4):
                sp.wait_ge(*is_read(("f2", n)))
                sp.dma_start(sd[:, 2 * n:2 * n + 2], y[:, 2 * n:2 * n + 2]).then_inc(y_stored, 16)
            sp.wait_ge(y_stored, 64)
            sw = scratch.rearrange("b h w c -> (b h) w c")
            sp.dma_start(y2[0:64, :, :], sw[:, 0:8, :]).then_inc(y2_in, 16)
            sp.dma_start(y2[64:128, 0, :], sw[:, 8, :]).then_inc(y2_in, 16)
            for j in range(1, 8):
                sp.dma_start(y2[64:128, j, :], sw[:, W - j, :]).then_inc(y2_in, 16)
            od = a["out"].rearrange("b h w c -> (b h) w c")
            for n in range(4):
                sp.wait_ge(*is_read(("ic", n)))
                sp.dma_start(od[:, 2 * n:2 * n + 2, :], res[0:64, 2 * n:2 * n + 2, :]).then_inc(out_stored, 16)
                for j in (2 * n, 2 * n + 1):
                    sp.dma_start(od[:, W - j if j else 8, :], res[64:128, j, :]).then_inc(out_stored, 16)
            sp.wait_ge(out_stored, 16 * 12)

        @block.gpsimd
        def _(pool):
            pool.dma_start(bqkv[:], a["qkv_b"].rearrange("(f p) -> p f", p=CF), allow_slow_non_contiguous=True).then_inc(bqkv_in, 16)
            pool.dma_start(bv[:], a["qkv_b"][2 * C:3 * C].partition_broadcast(128)).then_inc(bv_in, 16)
            nc.gpsimd.memset(mhalf[:], -0.5).then_inc(set_up, 1)
            nc.gpsimd.memset(h1t[:, :, QB + 112:QR], 0.0).then_inc(set_up, 1)
            for f in range(2):
                nc.gpsimd.memset(raw(relc[:, f, :, :, QB + 112:QR]), 0.0).then_inc(set_up, 1)
            nc.gpsimd.memset(negmax[:], 0.0).then_inc(set_up, 1)
            pool.wait_ge(set_up, 5)
            for i in range(2):
                pool.wait_ge(veps_done, i + 1)
                nc.gpsimd.tensor_tensor(rstd[:, 0, 4 * i:4 * i + 4], veps[:, 0, 4 * i:4 * i + 4],
                                        mhalf[:, 0:4], ALU.pow).then_inc(rstd_done, 1)
            nc.gpsimd.memset(vaug[:, :, :, HD:2 * HD], 1.0).then_inc(set_up, 1)

            def halves(row):
                return row.rearrange("n o -> (n o)").rearrange("(f p) -> p f", p=CF)

            for dst, src in (
                    (pb[:], a["proj_b"].partition_broadcast(128)),
                    (f2b[:], a["fc2_b"].partition_broadcast(128)),
                    (f1b[:], a["fc1_b"].rearrange("(m p) -> p m", p=128)),
                    (ln2[:, :, 0], a["ln2_g"].rearrange("(f p) -> p f", p=CF)),
                    (ln2[:, :, 1], a["ln2_b"].rearrange("(f p) -> p f", p=CF)),
                    (half4[:], a["half4"]),
                    (b20c[:], halves(a["b2"][0])),
                    (b2r[:, 0], a["b2"][0].rearrange("n o -> (n o)").partition_broadcast(128)),
                    (b2r[:, 1], a["b2"][1].rearrange("n o -> (n o)").partition_broadcast(128)),
                    (b1c[:, 0], halves(a["b1"][0])),
                    (b1c[:, 1], halves(a["b1"][1])),
                    (w12[:, 0, 0], a["w1"][0].rearrange("(f n) i o -> (n i) f o", f=2)),
                    (w12[:, 0, 1], a["w1"][1].rearrange("(f n) i o -> (n i) f o", f=2)),
                    (w12[:, 1, 0], a["w2"][0].rearrange("(f n) i o -> (n i) f o", f=2)),
                    (w12[:, 1, 1], a["w2"][1].rearrange("(f n) i o -> (n i) f o", f=2))):
                pool.dma_start(dst, src, allow_slow_non_contiguous=True).then_inc(late_in, 16)
            for f in range(2):
                pool.wait_ge(*is_read(("k", f, 2)))
                for at, n in ((KPB + 16, PADB - 16), (KPR, PADR)):
                    nc.gpsimd.tensor_copy(k2[:, f, :, at:at + n],
                                          k2[:, f, :, KPB:KPB + 1].to_broadcast([CF, 2, n])).then_inc(k_padded, 1)
                for j in range(HH):
                    h = f * HH + j
                    o = h % NOP
                    if h == 0:
                        pool.wait_ge(rows_copied, 16 * 2 * (NOP - 1))
                    if h >= NOP:
                        pool.wait_ge(*is_full(("E", h - NOP, 4)))
                        pool.wait_ge(*is_full(("E", h - NOP, 5)))
                    for axis in range(2):
                        for p in range(2):
                            pool.wait_ge(*is_read(("rel", f, axis, p)))
                        pool.dma_start(raw(qop[64 + 32 * axis:92 + 32 * axis, o]),
                                       raw(relc[WS * j:WS * (j + 1), f, axis])).then_inc(r_loaded[o], 16)
            pool.wait_ge(late_in, 15 * 16)
            for t in range(NT):
                nc.gpsimd.tensor_tensor(xt[:, t], xt[:, t], pb[:], ALU.add).then_inc(xpb_done, 1)
            for i in range(2):
                pool.wait_ge(veps_done, 3 + i)
                nc.gpsimd.tensor_tensor(rstd[:, 1, 4 * i:4 * i + 4], veps[:, 1, 4 * i:4 * i + 4],
                                        mhalf[:, 0:4], ALU.pow).then_inc(rstd_done, 1)
            for n in range(4):
                pool.wait_ge(*is_read(("pr", n)))
                for t in (2 * n, 2 * n + 1):
                    nc.gpsimd.tensor_tensor(x1b[:, t], x1[:, t], f2b[:], ALU.add).then_inc(x1b_done, 1)

        def normalised(eng, key, f, bp, into):
            eng.wait_ge(*is_full(key))
            for piece in "GBR":
                ins = into(win(h1t[:, f], piece, 2 * bp, 2), nat(ps(key)[0:CF, :], piece, 2))
            ins.then_inc(emptied(key), 1)

        def outputs_read(eng, copy, f, bp):
            key = ("oT", f, bp)
            eng.wait_ge(*is_full(key))
            if bp < 2:
                ins = copy(nat(ot[:, f, 512 * bp:512 * bp + 512], "G", 2),
                           ps(key)[0:CF, 0:2 * WIN].rearrange("p (b h w) -> p b h w", b=2, h=WS))
            else:
                copy(nat(ot[:, f], "B", B), ps(key)[0:CF, 0:112].rearrange("p (b h w) -> p b h w", b=B, h=2))
                ins = copy(nat(ot[:, f], "R", B),
                           ps(key)[0:CF, 128:256].rearrange("p (b h w) -> p b h w", b=B, h=H))
            ins.then_inc(emptied(key), 1)

        def fa_read(eng, copy, n, f):
            key = ("fa", n, f)
            eng.wait_ge(*is_full(key))
            src = ps(key)[0:CF, 0:400].rearrange("p (t m) -> p t m", t=2)
            dst = ya[:, f].rearrange("p (m g) -> p m g", m=16)[:, :, 16 * n:16 * n + 16]
            copy(dst.rearrange("p m (t h) -> p t m h", t=2),
                 src[:, :, 0:128].rearrange("p t (m h) -> p t m h", m=16))
            dst = an[:, f].rearrange("p (v g) -> p v g", v=NW)[:, :, 16 * n:16 * n + 16]
            copy(dst.rearrange("p v (t h) -> p t v h", t=2),
                 src[:, :, 128:200].rearrange("p t (v h) -> p t v h", v=NW)).then_inc(emptied(key), 1)

        def ia_read(eng, copy, n, f):
            key = ("ia", f, n)
            eng.wait_ge(*is_full(key))
            dst = iv[:, f].rearrange("p (m g) -> p m g", m=16)
            if n < 2:
                copy(dst[:, :, 28 * n:28 * n + 28].rearrange("p m (t g) -> p t m g", t=2),
                     ps(key)[0:CF, 0:448].rearrange("p (t m g) -> p t m g", t=2, m=16)).then_inc(emptied(key), 1)
            else:
                copy(dst[:, :, 56:64],
                     ps(key)[0:CF, 0:128].rearrange("p (m g) -> p m g", m=16)).then_inc(emptied(key), 1)

        def pair(key):
            return ps(key)[:, 0:2 * CAS].rearrange("p (j c) -> p j c", j=2)

        def k_places(key, f, g, part):
            c0, c1 = GROUPS[g]
            src = ps(key)[0:CF, 0:c1 - c0]
            if g < 2:
                return k2[:, f, part, c0:c1], src
            dst = k2[:, f, part, KB:KB + 2 * (KR - KB)].rearrange("p (g c) -> p g c", g=2)[:, :, 0:128]
            return dst, src.rearrange("p (g c) -> p g c", g=2)

        @block.scalar
        def _(act):
            act.dma_start(ident[:], a["ident"]).then_inc(small_in, 16)
            act.dma_start(ln1[:, :, 0], a["ln1_g"].rearrange("(f p) -> p f", p=CF),
                          allow_slow_non_contiguous=True).then_inc(small_in, 16)
            act.dma_start(ln1[:, :, 1], a["ln1_b"].rearrange("(f p) -> p f", p=CF),
                          allow_slow_non_contiguous=True).then_inc(small_in, 16)
            act.dma_start(relpos[:, 0], a["rel_pos_h"][:, None].to_broadcast([2 * WS - 1, HH, HD])).then_inc(rel_in, 16)
            act.dma_start(relpos[:, 1], a["rel_pos_w"][:, None].to_broadcast([2 * WS - 1, HH, HD])).then_inc(rel_in, 16)
            act.dma_start(mask6[:], a["mask6"]).then_inc(rel_in, 16)
            act.wait_ge(rows_in, 32)
            nc.scalar.copy(kop[64:128, 0], rows_k).then_inc(rows_set, 1)
            nc.scalar.copy(qop[64:128, 0], rows_q).then_inc(rows_set, 1)
            act.wait_ge(small_in, 48)
            for bp in range(2):
                normalised(act, ("hT", bp, 0), 0, bp, lambda dst, src: nc.scalar.activation(
                    dst, src, ACT.Identity, scale=ln1[:, 0, 0:1], bias=ln1[:, 0, 1:2]))
            act.wait_ge(k_scaled, 3)
            for f in range(2):
                bq = bqkv[:, f:f + 1]
                for g, (c0, c1) in enumerate(GROUPS):
                    key = ("q", f, g)
                    act.wait_ge(*is_full(key))
                    src = ps(key)[0:CF, 0:c1 - c0]
                    if g < 2:
                        nc.scalar.activation(nat(qf[:, f, 512 * g:512 * g + 512], "G", 2),
                                             src.rearrange("p (b h w) -> p b h w", b=2, h=WS),
                                             ACT.Identity, bias=bq)
                    else:
                        nc.scalar.activation(nat(qf[:, f], "B", B),
                                             src[:, 0:112].rearrange("p (b h w) -> p b h w", b=B, h=2),
                                             ACT.Identity, bias=bq)
                        nc.scalar.activation(nat(qf[:, f], "R", B),
                                             src[:, 128:256].rearrange("p (b h w) -> p b h w", b=B, h=H),
                                             ACT.Identity, bias=bq)
                    nc.scalar.activation(q2[:, f, 0, c0:c1], src, ACT.Identity, bias=bq).then_inc(q_high, 1)
                for g in range(3):
                    key = ("k", f, g)
                    act.wait_ge(*is_full(key))
                    dst, src = k_places(key, f, g, 0)
                    nc.scalar.activation(dst, src, ACT.Identity, bias=bk4[:, f:f + 1]).then_inc(k_high, 1)
                for axis in range(2):
                    for p in range(2):
                        key = ("rel", f, axis, p)
                        act.wait_ge(*is_full(key))
                        for src, dst in rel_pieces(axis, ps(key)[0:84, :], p, relc[:, f, axis, 0]):
                            ins = nc.scalar.copy(dst, src)
                        ins.then_inc(r_high, 1)
            for n in range(NH + 3):
                m = n - 2
                for u in range(6):
                    if u == 3 and 1 <= n <= NH:
                        h = n - 1
                        key = ("mx", h)
                        act.wait_ge(*is_full(key))
                        if h >= 2:
                            act.wait_ge(max_loaded[h % 2], 32 * (h // 2))
                        nc.scalar.copy(maxg[:, h % 2], ps(key)[0:16, 0:HWIN])
                        nc.scalar.copy(maxw[:, h % 2], ps(key)[0:4, 128:256]).then_inc(emptied(key), 1)
                        act.wait_ge(*is_read(key))
                        act.dma_start(raw(qop[126:128, h % NOP, 0:GC]), raw(maxg[:, h % 2])).then_inc(max_loaded[h % 2], 16)
                        act.dma_start(raw(qop[126:128, h % NOP, QB:QN]), raw(maxw[:, h % 2])).then_inc(max_loaded[h % 2], 16)
                    if 0 <= m < NH:
                        key = ("E", m, u)
                        act.wait_ge(*is_full(key))
                        src = ps(key)
                        if u < 4:
                            if m >= 1:
                                act.wait_ge(*is_full(("pvg", m - 1)))
                            nc.scalar.activation(pg[:, u], src[0:HWIN, 0:2 * WIN], ACT.Exp).then_inc(emptied(key), 1)
                        else:
                            if m >= 1 and (m - 1) % 2:
                                act.wait_ge(*is_full(("pvw", (m - 1) // 2)))
                            elif m >= 1:
                                act.wait_ge(pvw_even, (m - 1) // 2 + 1)
                            dst, r0, r1 = (pwb, 112, 84) if u == 4 else (pwr, 128, 96)
                            nc.scalar.activation(dst[0:r0, 0:128], src[0:r0, 0:128], ACT.Exp)
                            nc.scalar.activation(dst[0:r1, 128:384], src[0:r1, 128:384], ACT.Exp).then_inc(emptied(key), 1)
                    if u == 0 and 0 <= m - 1 < NH:
                        key = ("pvg", m - 1)
                        act.wait_ge(*is_full(key))
                        nc.scalar.copy(ev[:, m - 1], ps(key)[:, 0:WIN]).then_inc(emptied(key), 1)
            for bp in range(3):
                outputs_read(act, nc.scalar.copy, 0, bp)
            act.wait_ge(late_in, 15 * 16)
            for bp in range(2):
                key = ("mT", bp, 0)
                act.wait_ge(*is_full(key))
                nc.scalar.activation(h2t[:, 0, 512 * bp:512 * bp + 512], ps(key)[0:CF, :], ACT.Identity,
                                     scale=ln2[:, 0, 0:1], bias=ln2[:, 0, 1:2]).then_inc(emptied(key), 1)
            for n in range(2):
                for m in range(6):
                    key = ("f1", n, m)
                    act.wait_ge(*is_full(key))
                    nc.scalar.activation(gl[:, m, 512 * n:512 * n + 512], ps(key)[:, :], ACT.Gelu,
                                         bias=f1b[:, m:m + 1]).then_inc(emptied(key), 1)
            for n in range(4):
                fa_read(act, nc.scalar.copy, n, 0)
            for n in range(4):
                key = ("fb", n)
                act.wait_ge(*is_full(key))
                nc.scalar.copy(fbp[:, 2 * n:2 * n + 2], pair(key)[:, :, 0:C]).then_inc(fb_kept, 1)
            for f in range(2):
                for x in range(2):
                    for p in range(2):
                        key = ("m1", f, x, p)
                        act.wait_ge(*is_full(key))
                        c0, c1 = ((0, 252), (252, 576))[p]
                        nc.scalar.activation(o1[:, x, f, c0:c1], ps(key)[0:CF, 0:c1 - c0], ACT.Relu,
                                             bias=b1c[:, x, f:f + 1]).then_inc(emptied(key), 1)
            for n in range(3):
                ia_read(act, nc.scalar.copy, n, 0)
            for n in (0, 2):
                key = ("ib", n)
                act.wait_ge(*is_full(key))
                nc.scalar.copy(ibq[:, 2 * n:2 * n + 2], pair(key)).then_inc(emptied(key), 1)

        @block.vector
        def _(dve):
            def norm_stats(ln, i, src):
                for t in range(4 * i, 4 * i + 4):
                    ins = nc.vector.bn_stats(stats[:, ln, t], src[:, t])
                ins.then_inc(stats_done, 1)
                dve.wait_ge(stats_done, 2 * ln + i + 1)
                for t in range(4 * i, 4 * i + 4):
                    ins = nc.vector.bn_aggr(mv[:, ln, t], stats[:, ln, t])
                ins.then_inc(mean_done, 1)
                dve.wait_ge(mean_done, 2 * ln + i + 1)
                nc.vector.tensor_scalar(veps[:, ln, 4 * i:4 * i + 4], mv[:, ln, 4 * i:4 * i + 4, 1], EPS, None,
                                        ALU.add).then_inc(veps_done, 1)

            for i in range(2):
                dve.wait_ge(x_in[i], 16)
                norm_stats(0, i, xt)
            for i in range(2):
                dve.wait_ge(rstd_done, i + 1)
                for t in range(4 * i, 4 * i + 4):
                    ins = nc.vector.tensor_scalar(xn[:, t], xt[:, t], mv[:, 0, t, 0:1], rstd[:, 0, t:t + 1],
                                                  ALU.subtract, ALU.mult)
                ins.then_inc(xn_done, 1)
            dve.wait_ge(rel_in, 48)
            for ax in range(2):
                key = ("relp", ax)
                dve.wait_ge(*is_full(key))
                src = ps(key)[0:CF, :]
                src = bass.AP(tensor=src.tensor, offset=src.offset + WS - 1,
                              ap=[list(src.ap[0]), [1, WS], [0, HH], [-1, WS]])
                nc.vector.tensor_tensor(relw[:, ax].rearrange("p r (j k) -> p r j k", j=HH), src,
                                        mask6[:, None, :, None].to_broadcast([CF, WS, HH, WS]),
                                        ALU.mult).then_inc(emptied(key), 1)
            dve.wait_ge(small_in, 48)
            for bp in range(2):
                normalised(dve, ("hT", bp, 1), 1, bp, lambda dst, src: nc.vector.tensor_scalar(
                    dst, src, ln1[:, 1, 0:1], ln1[:, 1, 1:2], ALU.mult, ALU.add))
            dve.wait_ge(wqkv_in, 16)
            dve.wait_ge(bqkv_in, 16)
            nc.vector.tensor_scalar(bk4[:], bqkv[:, 2:4], HD ** -0.5, None, ALU.mult).then_inc(k_scaled, 1)
            for f in range(2):
                nc.vector.tensor_scalar(wqkv[:, f, C:2 * C], wqkv[:, f, C:2 * C], HD ** -0.5, None,
                                        ALU.mult).then_inc(k_scaled, 1)
            dve.wait_ge(k_scaled, 3)
            for f in range(2):
                for g, (c0, c1) in enumerate(GROUPS):
                    key = ("q", f, g)
                    dve.wait_ge(q_high, 3 * f + g + 1)
                    nc.vector.scalar_tensor_tensor(q2[:, f, 1, c0:c1], ps(key)[0:CF, 0:c1 - c0], bqkv[:, f:f + 1],
                                                   q2[:, f, 0, c0:c1].bitcast(F32), ALU.add,
                                                   ALU.subtract).then_inc(emptied(key), 1)
                for g in range(3):
                    key = ("k", f, g)
                    dve.wait_ge(k_high, 3 * f + g + 1)
                    dst, src = k_places(key, f, g, 1)
                    high, _ = k_places(key, f, g, 0)
                    nc.vector.scalar_tensor_tensor(dst, src, bk4[:, f:f + 1], high.bitcast(F32), ALU.add,
                                                   ALU.subtract).then_inc(emptied(key), 1)
                for axis in range(2):
                    for p in range(2):
                        key = ("rel", f, axis, p)
                        dve.wait_ge(r_high, 4 * f + 2 * axis + p + 1)
                        part = ps(key)[0:84, :]
                        for (src, low), (_, high) in zip(rel_pieces(axis, part, p, relc[:, f, axis, 1]),
                                                         rel_pieces(axis, part, p, relc[:, f, axis, 0])):
                            ins = nc.vector.tensor_tensor(low, src, high.bitcast(F32), ALU.subtract)
                        ins.then_inc(emptied(key), 1)
            dve.wait_ge(bv_in, 16)
            nc.vector.tensor_copy(vaug[0:96, 10, :, 0:HD],
                                  bv[0:96].rearrange("p (h d) -> p h d", h=NH)).then_inc(v_padded, 1)
            for n in range(6):
                key = ("v", n)
                dve.wait_ge(*is_full(key))
                rows, tiles = (HWIN, 2) if n < 4 else ((112, 1), (128, 1))[n - 4]
                t = 2 * n if n < 4 else 4 + n
                nc.vector.tensor_tensor(
                    vaug[0:rows, t:t + tiles, :, 0:HD],
                    ps(key)[0:rows, 0:tiles * C].rearrange("p (t h d) -> p t h d", t=tiles, h=NH),
                    bv[0:rows, None].to_broadcast([rows, tiles, C]).rearrange("p t (h d) -> p t h d", h=NH),
                    ALU.add).then_inc(emptied(key), 1)
            dve.wait_ge(set_up, 5)
            for n in range(NH + 3):
                for u in range(6):
                    if n < NH:
                        key = ("S", n, u)
                        dve.wait_ge(*is_full(key))
                        if u == 0 and n >= 2:
                            dve.wait_ge(max_split, n - 1)
                        rows, cols, width, at = (HWIN, 2, WIN, 2 * u) if u < 4 else (
                            (128, 1, KR - KB, 8), (128, 1, KN - KR, 9))[u - 4]
                        nc.vector.tensor_reduce(negmax[0:rows, n % 2, at:at + cols],
                                                ps(key)[0:rows, 0:cols * width].rearrange("p (t k) -> p t k", t=cols),
                                                AX.X, ALU.max, negate=True).then_inc(emptied(key), 1)
                    if u == 1 and 4 <= n <= NH + 2 and n % 2 == 0:
                        i = (n - 4) // 2
                        key = ("pvw", i)
                        dve.wait_ge(*is_full(key))
                        nc.vector.tensor_copy(evw[:, i], ps(key)[:, 0:128]).then_inc(emptied(key), 1)
                if n < NH:
                    dve.wait_ge(*is_read(("S", n, 4)))
                    dve.wait_ge(*is_read(("S", n, 5)))
                    if n >= 2:
                        dve.wait_ge(*is_full(("mx", n - 2)))
                    whole, parts = negmax[:, n % 2], negmax2[:, n % 2]
                    nc.vector.tensor_copy(parts[:, 0:8].bitcast(F32R), whole[:, 0:8])
                    nc.vector.tensor_copy(parts[:, 16:18].bitcast(F32R), whole[:, 8:10]).then_inc(max_high, 1)
                    dve.wait_ge(max_high, n + 1)
                    nc.vector.tensor_tensor(parts[:, 8:16], whole[:, 0:8], parts[:, 0:8], ALU.subtract)
                    nc.vector.tensor_tensor(parts[:, 18:20], whole[:, 8:10], parts[:, 16:18],
                                            ALU.subtract).then_inc(max_split, 1)
            recips = 0
            for u in range(2):
                for n in range(3):
                    key = ("eT", u, n)
                    dve.wait_ge(*is_full(key))
                    src = ps(key)[0:HWIN, :].rearrange("p (h b d) -> p h b d", h=4, b=B)
                    rd = rden[:, u, 4 * n:4 * n + 4]
                    nc.vector.reciprocal(rd, src[:, :, :, HD]).then_inc(rden_done, 1)
                    recips += 1
                    dve.wait_ge(rden_done, recips)
                    nc.vector.tensor_tensor(
                        on[:, u].rearrange("p b (h d) -> p h b d", h=NH)[:, 4 * n:4 * n + 4], src[:, :, :, 0:HD],
                        rd[:, :, :, None].to_broadcast([HWIN, 4, B, HD]), ALU.mult).then_inc(emptied(key), 1)
            for n, hs in enumerate((8, 4)):
                key = ("wT", n)
                dve.wait_ge(*is_full(key))
                src = ps(key)[:, 0:64 * hs].rearrange("p (h g d) -> p h g d", h=hs, g=2)
                rd = rdenw[:, 8 * n:8 * n + hs]
                nc.vector.reciprocal(rd, src[:, :, :, HD]).then_inc(rden_done, 1)
                recips += 1
                dve.wait_ge(rden_done, recips)
                ins = nc.vector.tensor_tensor(
                    onw.rearrange("p g (h d) -> p h g d", h=NH)[:, 8 * n:8 * n + hs], src[:, :, :, 0:HD],
                    rd[:, :, :, None].to_broadcast([128, hs, 2, HD]), ALU.mult)
                ins.then_inc(emptied(key), 1)
            for bp in range(3):
                outputs_read(dve, nc.vector.tensor_copy, 1, bp)
            dve.wait_ge(xpb_done, NT)
            for n in range(4):
                key = ("pr", n)
                dve.wait_ge(*is_full(key))
                nc.vector.tensor_tensor(x1[:, 2 * n:2 * n + 2], ps(key)[:, 0:2 * C].rearrange("p (t c) -> p t c", t=2),
                                        xt[:, 2 * n:2 * n + 2], ALU.add).then_inc(emptied(key), 1)
                if n % 2:
                    dve.wait_ge(*is_read(("pr", n - 1)))
                    dve.wait_ge(*is_read(("pr", n)))
                    norm_stats(1, n // 2, x1)
            for i in range(2):
                dve.wait_ge(rstd_done, 3 + i)
                for t in range(4 * i, 4 * i + 4):
                    ins = nc.vector.tensor_scalar(x1n[:, t], x1[:, t], mv[:, 1, t, 0:1], rstd[:, 1, t:t + 1],
                                                  ALU.subtract, ALU.mult)
                ins.then_inc(x1n_done, 1)
            dve.wait_ge(late_in, 15 * 16)
            for bp in range(2):
                key = ("mT", bp, 1)
                dve.wait_ge(*is_full(key))
                nc.vector.tensor_scalar(h2t[:, 1, 512 * bp:512 * bp + 512], ps(key)[0:CF, :], ln2[:, 1, 0:1],
                                        ln2[:, 1, 1:2], ALU.mult, ALU.add).then_inc(emptied(key), 1)
            for i in range(2):
                nc.vector.tensor_tensor(wsum[:, i, 0], w12[:, i, 0], w12[:, i, 1], ALU.add).then_inc(wsum_done, 1)
                nc.vector.tensor_tensor(wsum[:, i, 1], w12[:, i, 0], w12[:, i, 1], ALU.subtract).then_inc(wsum_done, 1)
            dve.wait_ge(wsum_done, 4)
            for i in range(2):
                for x in range(2):
                    nc.vector.tensor_tensor(
                        wbd[:, i, x].rearrange("p f (n o) -> p f n o", n=NB // 2),
                        wsum[:, i, x, :, None].to_broadcast([CF, 2, NB // 2, BS]),
                        half4[:, None, :, None].to_broadcast([CF, 2, NB // 2, BS]), ALU.mult).then_inc(wbd_done, 1)
            dve.wait_ge(wbd_done, 4)
            nc.vector.tensor_tensor(wps[:], wbd[:, 1, 0], wbd[:, 1, 1], ALU.add).then_inc(wps_done, 1)
            nc.vector.tensor_tensor(bsum, b2r[:, 0], b2r[:, 1], ALU.add).then_inc(bsum_done, 1)
            dve.wait_ge(*is_full("w2T"))
            nc.vector.tensor_copy(w2t.rearrange("p x f c -> p (x f c)"), ps("w2T")[0:CF, 0:4 * CF]).then_inc(emptied("w2T"), 1)
            dve.wait_ge(*is_full("w2p"))
            dve.wait_ge(wps_done, 1)
            nc.vector.tensor_tensor(wab[:, 0], ps("w2p")[0:CF, 0:2 * CF].rearrange("p (f c) -> p f c", f=2),
                                    wbd[:, 1, 0], ALU.add)
            nc.vector.tensor_tensor(wab[:, 1], ps("w2p")[0:CF, 2 * CF:4 * CF].rearrange("p (f c) -> p f c", f=2),
                                    wps[:], ALU.add).then_inc(emptied("w2p"), 1)
            dve.wait_ge(*is_full("b2w"))
            dve.wait_ge(bsum_done, 1)
            nc.vector.tensor_tensor(bs, ps("b2w")[:, 0:C], bsum, ALU.add).then_inc(emptied("b2w"), 1)
            dve.wait_ge(x1b_done, NT)
            for n in range(4):
                key = ("f2", n)
                dve.wait_ge(*is_full(key))
                nc.vector.tensor_tensor(y[:, 2 * n:2 * n + 2], ps(key)[:, 0:2 * C].rearrange("p (t c) -> p t c", t=2),
                                        x1b[:, 2 * n:2 * n + 2], ALU.add).then_inc(emptied(key), 1)
            for n in range(4):
                fa_read(dve, nc.vector.tensor_copy, n, 1)
            for n in range(4):
                key = ("fb", n)
                dve.wait_ge(fb_kept, n + 1)
                nc.vector.tensor_copy(fbf[:, 2 * n:2 * n + 2], pair(key)[:, :, C:0:-1]).then_inc(emptied(key), 1)
            for f in range(2):
                for p, (c0, c1) in enumerate(((0, 512), (512, 576))):
                    key = ("fc", f, p)
                    dve.wait_ge(*is_full(key))
                    nc.vector.tensor_copy(dk[:, f, c0:c1], ps(key)[0:CF, 0:c1 - c0]).then_inc(emptied(key), 1)
            for n in range(3):
                key = ("m2", n)
                dve.wait_ge(*is_full(key))
                rows, tiles = (126, 2) if n < 2 else (72, 1)
                t = slice(2 * n, 2 * n + tiles)
                nc.vector.tensor_tensor(sm[0:rows, t], ps(key)[0:rows, 0:tiles * C].rearrange("p (t c) -> p t c", t=tiles),
                                        bs[0:rows, None].to_broadcast([rows, tiles, C]), ALU.add).then_inc(emptied(key), 1)
                dve.wait_ge(*is_read(key))
                nc.vector.tensor_scalar(sc[0:rows, t], sm[0:rows, t], -SHRINK, SHRINK, ALU.max,
                                        ALU.min).then_inc(clipped, 1)
                dve.wait_ge(clipped, n + 1)
                nc.vector.tensor_tensor(ss[0:rows, t], sm[0:rows, t], sc[0:rows, t], ALU.subtract).then_inc(shrunk, 1)
            for n in range(3):
                ia_read(dve, nc.vector.tensor_copy, n, 1)
            for n in (1, 3):
                key = ("ib", n)
                dve.wait_ge(*is_full(key))
                nc.vector.tensor_copy(ibq[:, 2 * n:2 * n + 2], pair(key)).then_inc(emptied(key), 1)
            dve.wait_ge(y2_in, 9 * 16)
            for n in range(4):
                key = ("ic", n)
                dve.wait_ge(*is_full(key))
                nc.vector.scalar_tensor_tensor(res[:, 2 * n:2 * n + 2],
                                               ps(key)[:, 0:2 * C].rearrange("p (t c) -> p t c", t=2),
                                               1.0 / (B * H * W * C), y2[:, 2 * n:2 * n + 2], ALU.mult,
                                               ALU.add).then_inc(emptied(key), 1)

        @block.tensor
        def _(pe):
            mm = nc.tensor.matmul
            pe.wait_ge(rel_in, 48)
            pe.wait_ge(small_in, 48)
            for ax in range(2):
                key = ("relp", ax)
                mm(ps(key)[0:CF, 0:2 * WS - 1], relpos[:, ax].rearrange("p j d -> p (j d)"),
                   ident[0:2 * WS - 1, 0:2 * WS - 1], start=True, stop=True).then_inc(filled(key), 1)
            for bp in range(2):
                pe.wait_ge(xn_done, bp + 1)
                for f in range(2):
                    key = ("hT", bp, f)
                    for t in range(4):
                        ins = nc.tensor.transpose(ps(key)[0:CF, 128 * t:128 * t + 128],
                                                  xn[:, 4 * bp + t, CF * f:CF * f + CF], ident[:])
                    ins.then_inc(filled(key), 1)
            pe.wait_ge(wqkv_in, 16)
            pe.wait_ge(k_scaled, 3)
            pe.wait_ge(set_up, 2)
            for bp in range(2):
                for f in range(2):
                    pe.wait_ge(*is_read(("hT", bp, f)))
            for f in range(2):
                for x, name in enumerate("qk"):
                    for g, (c0, c1) in enumerate(GROUPS):
                        key = (name, f, g)
                        pe.wait_ge(*is_free(key))
                        for c in range(2):
                            ins = mm(ps(key)[0:CF, 0:c1 - c0], wqkv[:, c, C * x + CF * f:C * x + CF * f + CF],
                                     h1t[:, c, c0:c1], start=c == 0, stop=c == 1)
                        ins.then_inc(filled(key), 1)
                pe.wait_ge(q_high, 3 * (f + 1))
                qb = qf[:, f].rearrange("p (b h w) -> p b h w", b=B, h=H)
                for axis in range(2):
                    pe.wait_ge(*is_read(("relp", axis)))
                    for p in range(2):
                        key = ("rel", f, axis, p)
                        pe.wait_ge(*is_free(key))
                        for i in range(8):
                            r = 8 * p + i
                            rhs = qb[:, :, r, :] if axis == 0 else qb[:, :, :, r]
                            ins = mm(ps(key)[0:84, 64 * i:64 * i + 64], relw[:, axis, r % WS], rhs,
                                     start=True, stop=True)
                        ins.then_inc(filled(key), 1)
            for n in range(6):
                key = ("v", n)
                pe.wait_ge(*is_free(key))
                spans = [(HWIN * (2 * n + t), HWIN) for t in range(2)] if n < 4 else [((QB, 112), (QR, 128))[n - 4]]
                for t, (c0, rows) in enumerate(spans):
                    for c in range(2):
                        ins = mm(ps(key)[0:rows, C * t:C * t + C], h1t[:, c, c0:c0 + rows], wqkv[:, c, 2 * C:3 * C],
                                 start=c == 0, stop=c == 1)
                ins.then_inc(filled(key), 1)

            def maxima(h):
                o = h % NOP
                for u in range(6):
                    key = ("S", h, u)
                    if u == 0:
                        for loaded in (q_loaded, k_loaded, r_loaded):
                            pe.wait_ge(loaded[o], 32 * (h // NOP + 1))
                    pe.wait_ge(*is_free(key))
                    if u < 4:
                        for t in range(2):
                            c0 = WIN * u + HWIN * t
                            ins = mm(ps(key)[0:HWIN, WIN * t:WIN * t + WIN], qop[0:126, o, c0:c0 + HWIN],
                                     kop[0:126, o, WIN * u:WIN * u + WIN], start=True, stop=True)
                    else:
                        q0, k0, k1 = ((QB, KB, KR), (QR, KR, KN))[u - 4]
                        ins = mm(ps(key)[:, 0:k1 - k0], qop[0:126, o, q0:q0 + 128], kop[0:126, o, k0:k1],
                                 start=True, stop=True)
                    ins.then_inc(filled(key), 1)
                    yield

            def shifted(h):
                o = h % NOP
                for u in range(6):
                    key = ("E", h, u)
                    if u == 0:
                        pe.wait_ge(max_loaded[h % 2], 32 * (h // 2 + 1))
                    pe.wait_ge(*is_free(key))
                    if u < 4:
                        chunks = [(WIN * u + HWIN * c, HWIN, WIN * c) for c in range(2)]
                        rhs = qop[:, o, WIN * u:WIN * u + WIN]
                    elif u == 4:
                        chunks = [(KB, 112, 0), (KPB, 84, 128), (KPB + 84, 84, 256)]
                        rhs = qop[:, o, QB:QB + 128]
                    else:
                        chunks = [(KR, 128, 0), (KPR, 96, 128), (KPR + 96, 96, 256)]
                        rhs = qop[:, o, QR:QR + 128]
                    n = rhs.shape[1]
                    for c0, rows, at in chunks:
                        ins = mm(ps(key)[0:rows, at:at + n], kop[:, o, c0:c0 + rows], rhs, start=True, stop=True)
                    ins.then_inc(filled(key), 1)
                    yield

            def values_g(h, c):
                key = ("pvg", h)
                if c == 0:
                    pe.wait_ge(*is_free(key))
                    pe.wait_ge(*is_read(("E", h, 2)))
                    pe.wait_ge(*is_read(("E", h, 3)))
                for b in range(B):
                    ins = mm(ps(key)[32 * b:32 * b + 32, 0:WIN], vaug[0:HWIN, 2 * b + c, h],
                             pg[:, b, WIN * c:WIN * c + WIN], start=c == 0, stop=c == 1)
                if c == 1:
                    ins.then_inc(filled(key), 1)

            def values_w(h):
                key = ("pvw", h // 2)
                if h % 2 == 0:
                    pe.wait_ge(*is_free(key))
                pe.wait_ge(*is_read(("E", h, 4)))
                pe.wait_ge(*is_read(("E", h, 5)))
                for c in range(3):
                    for g, (src, own, pad) in enumerate(((pwb, 112, 84), (pwr, 128, 96))):
                        rows, tile = (own, 8 + g) if c == 0 else (pad, 10)
                        q0 = 32 * (2 * (h % 2) + g)
                        ins = mm(ps(key)[q0:q0 + 32, 0:128], vaug[0:rows, tile, h], src[0:rows, 128 * c:128 * c + 128],
                                 start=c == 0, stop=c == 2)
                ins.then_inc(filled(key) if h % 2 else pvw_even, 1)

            def max_rows(h):
                key = ("mx", h)
                pe.wait_ge(*is_free(key))
                pe.wait_ge(max_split, h + 1)
                nc.tensor.transpose(ps(key)[0:16, 0:HWIN], negmax2[0:HWIN, h % 2, 0:16], ident[0:HWIN, 0:HWIN])
                nc.tensor.transpose(ps(key)[0:4, 128:256], negmax2[:, h % 2, 16:20], ident[:]).then_inc(filled(key), 1)

            pe.wait_ge(*is_read(("v", 5)))
            pe.wait_ge(v_padded, 1)
            pe.wait_ge(set_up, 6)
            pe.wait_ge(rows_set, 2)
            pe.wait_ge(rows_copied, 16 * 2 * (NOP - 1))
            for n in range(NH + 3):
                m = n - 2
                first = maxima(n) if n < NH else None
                second = shifted(m) if 0 <= m < NH else None
                for u in range(6):
                    if first:
                        next(first)
                    if u == 1 and 1 <= n <= NH:
                        max_rows(n - 1)
                    if second:
                        next(second)
                    if u == 0 and 0 <= m - 1 < NH:
                        values_w(m - 1)
                    if u >= 4 and second:
                        values_g(m, u - 4)

            for u in range(2):
                for n in range(3):
                    key = ("eT", u, n)
                    pe.wait_ge(*is_free(key))
                    pe.wait_ge(*is_read(("pvg", 4 * n + 3)))
                    for i in range(4):
                        ins = nc.tensor.transpose(ps(key)[0:HWIN, 128 * i:128 * i + 128],
                                                  ev[:, 4 * n + i, HWIN * u:HWIN * u + HWIN], ident[:])
                    ins.then_inc(filled(key), 1)
            for n, hp in enumerate((range(0, 4), range(4, 6))):
                key = ("wT", n)
                pe.wait_ge(*is_free(key))
                pe.wait_ge(*is_read(("pvw", hp[-1])))
                for i, p in enumerate(hp):
                    ins = nc.tensor.transpose(ps(key)[:, 128 * i:128 * i + 128], evw[:, p], ident[:])
                ins.then_inc(filled(key), 1)
            for bp in range(3):
                for f in range(2):
                    key = ("oT", f, bp)
                    pe.wait_ge(*is_free(key))
                    for k in [("eT", u, n) for u in range(2) for n in range(3)] if bp < 2 else [("wT", 0), ("wT", 1)]:
                        pe.wait_ge(*is_read(k))
                    for i in range(4 if bp < 2 else 2):
                        if bp < 2:
                            b, u = 2 * bp + i // 2, i % 2
                            ins = nc.tensor.transpose(ps(key)[0:CF, HWIN * i:HWIN * i + HWIN],
                                                      on[:, u, b, CF * f:CF * f + CF], ident[0:HWIN, 0:HWIN])
                        else:
                            ins = nc.tensor.transpose(ps(key)[0:CF, 128 * i:128 * i + 128],
                                                      onw[:, i, CF * f:CF * f + CF], ident[:])
                    ins.then_inc(filled(key), 1)
            pe.wait_ge(late_in, 15 * 16)
            pe.wait_ge(weights_in, 48)
            for bp in range(3):
                for f in range(2):
                    pe.wait_ge(*is_read(("oT", f, bp)))
            for n in range(4):
                key = ("pr", n)
                pe.wait_ge(*is_free(key))
                for t in range(2):
                    for c in range(2):
                        ins = mm(ps(key)[:, C * t:C * t + C], ot[:, c, 128 * (2 * n + t):128 * (2 * n + t) + 128],
                                 wproj[:, c], start=c == 0, stop=c == 1)
                ins.then_inc(filled(key), 1)
            for bp in range(2):
                pe.wait_ge(x1n_done, bp + 1)
                for f in range(2):
                    key = ("mT", bp, f)
                    pe.wait_ge(*is_free(key))
                    for t in range(4):
                        ins = nc.tensor.transpose(ps(key)[0:CF, 128 * t:128 * t + 128],
                                                  x1n[:, 4 * bp + t, CF * f:CF * f + CF], ident[:])
                    ins.then_inc(filled(key), 1)
            pe.wait_ge(wbd_done, 4)
            pe.wait_ge(*is_free("w2T"))
            for i in range(4):
                ins = nc.tensor.transpose(ps("w2T")[0:CF, CF * i:CF * i + CF], wbd[:, 1, i // 2, i % 2],
                                          ident[0:CF, 0:CF])
            ins.then_inc(filled("w2T"), 1)
            pe.wait_ge(*is_free("w2p"))
            pe.wait_ge(*is_read("w2T"))
            for i in range(4):
                ins = mm(ps("w2p")[0:CF, CF * i:CF * i + CF], w2t[:, i // 2, i % 2], wbd[:, 1, 1, i % 2],
                         start=True, stop=True)
            ins.then_inc(filled("w2p"), 1)
            pe.wait_ge(*is_free("b2w"))
            for f in range(2):
                ins = mm(ps("b2w")[:, CF * f:CF * f + CF], b20c[:, f:f + 1].to_broadcast([CF, 128]), wbd[:, 1, 1, f],
                         start=True, stop=True)
            ins.then_inc(filled("b2w"), 1)
            for n in range(2):
                for f in range(2):
                    pe.wait_ge(*is_read(("mT", n, f)))
                for m in range(6):
                    key = ("f1", n, m)
                    pe.wait_ge(*is_free(key))
                    for c in range(2):
                        ins = mm(ps(key)[:, :], wf1[:, c, 128 * m:128 * m + 128], h2t[:, c, 512 * n:512 * n + 512],
                                 start=c == 0, stop=c == 1)
                    ins.then_inc(filled(key), 1)
            for n in range(4):
                key = ("f2", n)
                pe.wait_ge(*is_free(key))
                for m in range(6):
                    pe.wait_ge(*is_read(("f1", n // 2, m)))
                for t in range(2):
                    for m in range(6):
                        ins = mm(ps(key)[:, C * t:C * t + C], gl[:, m, 128 * (2 * n + t):128 * (2 * n + t) + 128],
                                 wf2[:, m], start=m == 0, stop=m == 5)
                ins.then_inc(filled(key), 1)
            pe.wait_ge(tables_in, 6 * 16)
            for n in range(4):
                pe.wait_ge(*is_read(("f2", n)))
                for f in range(2):
                    key = ("fa", n, f)
                    pe.wait_ge(*is_free(key))
                    for t in range(2):
                        ins = mm(ps(key)[0:CF, 200 * t:200 * t + 200], y[:, 2 * n + t, CF * f:CF * f + CF], fw,
                                 start=True, stop=True)
                    ins.then_inc(filled(key), 1)
            for n in range(4):
                for f in range(2):
                    pe.wait_ge(*is_read(("fa", n, f)))
            for n in range(4):
                key = ("fb", n)
                pe.wait_ge(*is_free(key))
                for t in range(2):
                    for f in range(2):
                        j = 2 * n + t
                        ins = mm(ps(key)[:, CAS * t:CAS * t + CAS], ya[:, f, 128 * j:128 * j + 128], cas[:, f],
                                 start=f == 0, stop=f == 1)
                ins.then_inc(filled(key), 1)
            for f in range(2):
                for p, js in enumerate((range(0, 7), range(7, 8))):
                    key = ("fc", f, p)
                    pe.wait_ge(*is_free(key))
                    for j in js:
                        pe.wait_ge(*is_read(("fb", j // 2)))
                        n, c0 = (128, 0) if j == 0 else (64, (64 * (j + 1)) % 512)
                        at = 0 if j == 0 else 256
                        mm(ps(key)[0:CF, c0:c0 + n], fbp[:, j, CF * f:CF * f + CF], fg[:, at:at + n],
                           start=True, stop=False)
                        ins = mm(ps(key)[0:CF, c0:c0 + n], fbf[:, j, CF * f:CF * f + CF], fg[:, at + n:at + 2 * n],
                                 start=False, stop=True)
                    ins.then_inc(filled(key), 1)
            for f in range(2):
                for p in range(2):
                    pe.wait_ge(*is_read(("fc", f, p)))
                for x in range(2):
                    for p in range(2):
                        key = ("m1", f, x, p)
                        pe.wait_ge(*is_free(key))
                        k, nk = (t[:, f].rearrange("p (v g) -> p v g", v=NW) for t in (dk, an))

                        def tiles(t):
                            return t[:, :, 28 * p:28 * p + 28].rearrange("p v (t g) -> p t v g", t=2)

                        for i, (w, v) in enumerate(((0, (k, nk)[x]), (1, (nk, k)[x]))):
                            ins = mm(ps(key)[0:CF, 0:252], wbd[:, 0, w, f], tiles(v), start=i == 0, stop=i == 1)
                        if p == 1:
                            for i, (w, v) in enumerate(((0, (k, nk)[x]), (1, (nk, k)[x]))):
                                ins = mm(ps(key)[0:CF, 252:324], wbd[:, 0, w, f], v[:, :, 56:64],
                                         start=i == 0, stop=i == 1)
                        ins.then_inc(filled(key), 1)
            for f in range(2):
                for x in range(2):
                    for p in range(2):
                        pe.wait_ge(*is_read(("m1", f, x, p)))
            pe.wait_ge(*is_read("w2p"))
            for n in range(3):
                key = ("m2", n)
                pe.wait_ge(*is_free(key))
                for t in range(2 if n < 2 else 1):
                    g0, g1 = 14 * (2 * n + t), min(14 * (2 * n + t) + 14, 64)
                    rows = NW * (g1 - g0)
                    for f in range(2):
                        for x in range(2):
                            lhs = o1[:, x, f, NW * g0:NW * g1]
                            ins = mm(ps(key)[0:rows, C * t + CF * f:C * t + CF * f + CF], lhs, wab[:, x, f],
                                     start=x == 0, stop=x == 1)
                ins.then_inc(filled(key), 1)
            for n in range(3):
                pe.wait_ge(shrunk, n + 1)
                for f in range(2):
                    key = ("ia", f, n)
                    pe.wait_ge(*is_free(key))
                    for t in range(2 if n < 2 else 1):
                        rows, tab = (126, iw14) if n < 2 else (72, iw8)
                        w = tab.shape[1]
                        ins = mm(ps(key)[0:CF, w * t:w * t + w], ss[0:rows, 2 * n + t, CF * f:CF * f + CF], tab,
                                 start=True, stop=True)
                    ins.then_inc(filled(key), 1)
            for n in range(3):
                for f in range(2):
                    pe.wait_ge(*is_read(("ia", f, n)))
            for n in range(4):
                key = ("ib", n)
                pe.wait_ge(*is_free(key))
                for t in range(2):
                    for f in range(2):
                        j = 2 * n + t
                        ins = mm(ps(key)[:, CAS * t:CAS * t + CAS], iv[:, f, 128 * j:128 * j + 128], cas[:, f],
                                 start=f == 0, stop=f == 1)
                ins.then_inc(filled(key), 1)
            for n in range(4):
                key = ("ic", n)
                pe.wait_ge(*is_free(key))
                pe.wait_ge(*is_read(("ib", n)))
                for t in range(2):
                    j = 2 * n + t
                    at = 0 if j == 0 else 256
                    mm(ps(key)[:, C * t:C * t + C], ig[:, at:at + 128], ibq[:, j, 0:C], start=True, stop=False)
                    ins = mm(ps(key)[:, C * t:C * t + C], ig[:, at + 128:at + 256], ibq[:, j, C:0:-1],
                             start=False, stop=True)
                ins.then_inc(filled(key), 1)


_INS = {"x": "x", "L0_conv_ln1_g": "ln1_g", "L0_conv_ln1_b": "ln1_b", "L0_conv_qkv_w": "qkv_w",
        "L0_conv_qkv_b": "qkv_b", "L0_conv_proj_w": "proj_w", "L0_conv_proj_b": "proj_b",
        "L0_conv_rel_pos_h": "rel_pos_h", "L0_conv_rel_pos_w": "rel_pos_w", "L0_conv_ln2_g": "ln2_g",
        "L0_conv_ln2_b": "ln2_b", "L0_conv_fc1_w": "fc1_w", "L0_conv_fc1_b": "fc1_b", "L0_conv_fc2_w": "fc2_w",
        "L0_conv_fc2_b": "fc2_b", "L1_conv_w1": "w1", "L1_conv_b1": "b1", "L1_conv_w2": "w2", "L1_conv_b2": "b2"}


def kernel(**inputs):
    import concourse.bacc as bacc
    from concourse.bass_utils import run_bass_kernel_spmd

    nc = bacc.Bacc("TRN2", target_bir_lowering=False, num_devices=1)
    arrays, aps = {}, {}
    given = {short: np.ascontiguousarray(inputs[name]) for name, short in _INS.items()}
    for name, v in {**given, **tables()}.items():
        arrays[f"in_{name}"] = v
        aps[name] = nc.dram_tensor(f"in_{name}", v.shape, mybir.dt.from_np(v.dtype), kind="ExternalInput").ap()
    aps["scratch"] = nc.dram_tensor("scratch", (B, H, W, C), F32, kind="Internal").ap()
    aps["out"] = nc.dram_tensor("out_dram", (B, H, W, C), F32, kind="ExternalOutput").ap()
    build(nc, aps)
    r = run_bass_kernel_spmd(nc, [arrays], core_ids=[0])
    return r.results[0]["out_dram"]
```

```python
from contextlib import ExitStack

import concourse.bass as bass
from concourse import mybir
import numpy as np

F32 = mybir.dt.float32
F32R = mybir.dt.float32r
ALU = mybir.AluOpType
ACT = mybir.ActivationFunctionType
AX = mybir.AxisListType

B, H, W, C = 4, 16, 16, 192
NH, HD, WS = 12, 16, 14
MLP = 768
EPS = 1e-6
CF = C // 2
NT = B * H * W // 128
HH = NH // 2
WIN = WS * WS
HWIN = WIN // 2
GC = B * WIN
QB, QR, QN = GC, GC + 128, GC + 256
PADB = (WS - 2) * WS
PADR = WS * (WS - 2) + (WS - 2) * 2
KB, KPB = GC, GC + 112
KR = KPB + PADB
KPR = KR + 128
KN = KPR + PADR
BIG = 1e30
NB = 8
BS = C // NB
SHRINK = 0.01
NW = 9
CAS = C + 2


def tables():
    t = {}
    t["ident"] = np.eye(128)
    t["mask6"] = np.repeat(np.eye(HH), HD, axis=0)
    t["half4"] = 0.5 * np.repeat(np.eye(NB // 2), BS, axis=0)
    q = np.zeros((128, QN))
    k = np.zeros((128, KN))

    def key(col, kh, kw):
        for part in range(2):
            k[64 + 2 * kh + part, col] = 1
            k[96 + 2 * kw + part, col] = 1

    k[126:128] = 1
    for b in range(B):
        others = [92 + i for i in range(B) if i != b]
        for h in range(H):
            for w in range(W):
                if h < WS and w < WS:
                    key(b * WIN + h * WS + w, h, w)
                elif w < WS:
                    col = b * 28 + (h - WS) * WS + w
                    key(KB + col, h - WS, w)
                    k[others, KB + col] = -BIG
                    q[92 + b, QB + col] = 1
                else:
                    col = b * 32 + h * 2 + w - WS
                    corner = h >= WS
                    key(KR + col, h % WS, w - WS)
                    k[others, KR + col] = -BIG
                    k[124 if corner else 125, KR + col] = -BIG
                    q[92 + b, QR + col] = 1
                    q[125 if corner else 124, QR + col] = 1
    n = KPB
    for kh in range(2, WS):
        for kw in range(WS):
            key(n, kh, kw)
            n += 1
    n = KPR
    for kh in range(WS):
        for kw in range(2, WS):
            key(n, kh, kw)
            n += 1
    for kh in range(2, WS):
        for kw in range(2):
            key(n, kh, kw)
            k[124, n] = -BIG
            n += 1
    t["qrows"], t["krows"] = q, k
    w = np.arange(W)
    tw = np.zeros((W, 8, 2))
    tw[:, 0, 0] = 1
    tw[:, 0, 1] = np.cos(np.pi * w)
    for j in range(1, 8):
        tw[:, j, 0] = np.cos(2 * np.pi * j * w / W)
        tw[:, j, 1] = np.sin(2 * np.pi * j * w / W)
    fw = np.zeros((8, W, 8, 2, 8))
    for h in range(8):
        fw[h, :, :, :, h] = tw
    kept = [0, 8] + list(range(1, 8))
    flip = np.zeros((8, W, NW, 8))
    for h in range(8):
        for v, f in enumerate(kept):
            flip[h, (-f) % W, v, 7 - h] = 1
    t["fw"] = np.concatenate([fw.reshape(128, 128), flip.reshape(128, NW * 8)], 1)
    c, f = np.meshgrid(np.arange(C), np.arange(CAS) % C, indexing="ij")
    a = 2 * np.pi * ((c * f) % C) / C
    t["cas"] = (np.cos(a) - np.sin(a)).reshape(2, CF, CAS).transpose(1, 0, 2)
    b, h = np.meshgrid(np.arange(B), np.arange(H), indexing="ij")
    b, h = b.ravel(), h.ravel()
    u = (h + 9) % H
    g = 2 * np.pi * ((b[:, None] * b[None] * 4 + h[:, None] * u[None]) % 16) / 16
    cg, sg = np.cos(g), np.sin(g)
    z = np.zeros((64, 64))
    t["fg"] = np.concatenate([np.block([[cg, z], [z, cg]]), np.block([[-sg, z], [z, -sg]]),
                              np.concatenate([cg, -sg]), np.concatenate([-sg, -cg])], 1)
    cg, sg = cg.T, sg.T
    t["ig"] = np.concatenate([np.block([[cg, z], [z, cg]]), np.block([[-sg, z], [z, -sg]]),
                              np.block([[cg, cg], [-sg, sg]]), np.block([[-sg, -sg], [-cg, cg]])], 1)
    for name, m in (("iw14", 14), ("iw8", 8)):
        iw = np.zeros((NW, m, 8, 2, m))
        for v, f in enumerate(kept):
            for x in range(m):
                iw[v, x, :, :, x] = tw[f]
        t[name] = iw.reshape(NW * m, 16 * m)
    return {n: np.ascontiguousarray(v, np.float32) for n, v in t.items()}


def bank_order():
    count, place = [0] * 8, {}

    def add(key, bank):
        place[key] = (bank, count[bank])
        count[bank] += 1

    turn = [0]

    def rotate(keys):
        for key in keys:
            add(key, turn[0] % 8)
            turn[0] += 1

    rotate([("relp", a) for a in range(2)])
    rotate([("hT", bp, f) for bp in range(2) for f in range(2)])
    for f in range(2):
        rotate([("q", f, g) for g in range(3)])
        rotate([("k", f, g) for g in range(3)])
        if f == 0:
            rotate([("rel", f, a, p) for a in range(2) for p in range(2)])
    for n in range(6):
        add(("v", n), 4 + n % 3)
    for n in range(4):
        add(("rel", 1, n // 2, n % 2), 4 + n % 3)
    for h in range(NH):
        for u in range(6):
            add(("S", h, u), u % 2)
            add(("E", h, u), 2 + u % 2)
        add(("pvg", h), 4 + h % 2)
        if h % 2 == 0:
            add(("pvw", h // 2), 6)
        add(("mx", h), 7)
    for n in range(2):
        for u in range(2):
            add(("eT", u, n), u)
    add(("wT", 0), 0)
    turn[0] = 1
    rotate([("wT", 1), ("eT", 0, 2), ("eT", 1, 2)])
    rotate([("oT", f, bp) for bp in (2, 0, 1) for f in range(2)])
    rotate([("pr", n) for n in range(4)])
    rotate(["w2T", "b2w", "w2p"])
    rotate([("mT", 0, f) for f in range(2)])
    rotate([("f1", 0, m) for m in range(4)])
    rotate([("mT", 1, f) for f in range(2)])
    rotate([("f1", 0, m) for m in range(4, 6)] + [("f1", 1, m) for m in range(6)])
    rotate([("f2", n) for n in range(4)])
    rotate([("fa", n, f) for n in range(4) for f in range(2)])
    rotate([("fb", n) for n in range(4)])
    rotate([("fc", f, p) for f in range(2) for p in range(2)])
    rotate([("m1", f, x, p) for f in range(2) for x in range(2) for p in range(2)])
    rotate([("m2", n) for n in range(3)])
    rotate([("ia", f, n) for n in range(3) for f in range(2)])
    rotate([("ib", n) for n in range(4)])
    rotate([("ic", n) for n in range(4)])
    return place


def build(nc, a):
    place = bank_order()
    ctx = ExitStack()
    with ctx:
        def sb(name, shape, dt=F32):
            return ctx.enter_context(nc.sbuf_tensor(name, shape, dt))

        def sem(name):
            return ctx.enter_context(nc.semaphore(name))

        bank = [ctx.enter_context(nc.psum_tensor(f"bank{i}", [128, 512], F32)) for i in range(8)]
        bank_full = [sem(f"bank_full{i}") for i in range(8)]
        bank_free = [sem(f"bank_free{i}") for i in range(8)]

        def ps(key):
            return bank[place[key][0]]

        def filled(key):
            return bank_full[place[key][0]]

        def emptied(key):
            return bank_free[place[key][0]]

        def is_full(key):
            return bank_full[place[key][0]], place[key][1] + 1

        def is_read(key):
            return bank_free[place[key][0]], place[key][1] + 1

        def is_free(key):
            return bank_free[place[key][0]], place[key][1]

        ident = sb("ident", [128, 128])
        mask6 = sb("mask6", [CF, HH])
        xt = sb("xt", [128, NT, C])
        wqkv = sb("wqkv", [CF, 2, 3 * C])
        ln1 = sb("ln1", [CF, 2, 2])
        ln2 = sb("ln2", [CF, 2, 2])
        bqkv = sb("bqkv", [CF, 6])
        bk4 = sb("bk4", [CF, 2])
        bv = sb("bv", [128, C])
        pb = sb("pb", [128, C])
        f2b = sb("f2b", [128, C])
        f1b = sb("f1b", [128, 6])
        relpos = sb("relpos", [2 * WS - 1, 2, HH, HD])
        stats = sb("stats", [128, 2, NT, 6])
        mv = sb("mv", [128, 2, NT, 2])
        veps = sb("veps", [128, 2, NT])
        rstd = sb("rstd", [128, 2, NT])
        mhalf = sb("mhalf", [128, NT])
        wproj = sb("wproj", [CF, 2, C])
        wf1 = sb("wf1", [CF, 2, MLP])
        wf2 = sb("wf2", [128, 6, C])
        half4 = sb("half4", [CF, NB // 2])
        w12 = sb("w12", [CF, 2, 2, 2, BS])
        b1c = sb("b1c", [CF, 2, 2])
        b20c = sb("b20c", [CF, 2])
        b2r = sb("b2r", [128, 2, C])
        NOP = 4
        V_STEPS, R_STEPS = range(0, 4), range(4, 8)
        AHEAD = 2
        negmax = sb("negmax", [128, 2, 10])
        negmax2 = sb("negmax2", [128, 2, 20])
        maxg = sb("maxg", [16, 2, HWIN], F32R)
        maxw = sb("maxw", [4, 2, 128], F32R)

        def raw(t):
            return t.bitcast(F32)

        ARENA = 34200
        arena = sb("arena", [128, ARENA])
        with ExitStack() as scores:
            qop = scores.enter_context(nc.sbuf_tensor("qop", [128, NOP, QN], F32R))
            kop = scores.enter_context(nc.sbuf_tensor("kop", [128, NOP, KN], F32R))
        later = sb("later", [128, NOP * (QN + KN)])

        def layout(*items, at=0):
            views = []
            for rows, dims, dt in items:
                n = int(np.prod(dims))
                v = arena[0:rows, at:at + n]
                if dt is not F32:
                    v = v.bitcast(dt)
                names = "abcdefg"[:len(dims)]
                if len(dims) > 1:
                    v = v.rearrange(f"p ({' '.join(names)}) -> p {' '.join(names)}",
                                    **{names[i]: dims[i] for i in range(len(dims))})
                views.append(v)
                at += n
            assert at <= ARENA, at
            return views

        (relc, q2, k2, relw, qf, h1t, vaug, ev, evw) = layout(
            (84, (2, 2, 2, QN), F32R),
            (CF, (2, 2, QN), F32R),
            (CF, (2, 2, KN), F32R),
            (CF, (2, WS, 84), F32),
            (CF, (2, 1024), F32),
            (CF, (2, QN), F32),
            (128, (11, NH, 32), F32),
            (128, (NH, WIN), F32),
            (128, (NH // 2, 128), F32))
        relw_at = 2 * 2 * 2 * QN + 2 * 2 * QN + 2 * 2 * KN
        vaug_at = relw_at + 2 * WS * 84 + 2 * 1024 + 2 * QN
        pg, pwb, pwr = layout(
            (HWIN, (B, 2 * WIN), F32),
            (112, (2, 3 * 128), F32),
            (128, (2, 3 * 128), F32), at=relw_at)
        xn_at = vaug_at + 11 * NH * 32
        xn = arena[:, xn_at:xn_at + NT * C].rearrange("p (t c) -> p t c", t=NT)
        rows_at = xn_at + NT * C
        rows_k = arena[64:128, rows_at:rows_at + KN]
        rows_q = arena[64:128, rows_at + KN:rows_at + KN + QN]

        (on, onw, rden, rdenw, ot, x1, x1b, x1n, h2t, gl, y) = layout(
            (HWIN, (2, B, C), F32),
            (128, (2, C), F32),
            (HWIN, (2, NH, B), F32),
            (128, (NH, 2), F32),
            (CF, (2, 1024), F32),
            (128, (NT, C), F32),
            (128, (NT, C), F32),
            (128, (NT, C), F32),
            (CF, (2, 1024), F32),
            (128, (6, 1024), F32),
            (128, (NT, C), F32))
        fw, cas, fg, ig, iw14, iw8 = layout(
            (128, (200,), F32), (CF, (2, CAS), F32), (128, (384,), F32), (128, (512,), F32),
            (NW * 14, (224,), F32), (NW * 8, (128,), F32), at=vaug_at - (200 + 2 * CAS + 384 + 512 + 224 + 128))
        wsum, wbd, w2t, wps, wab, bsum, bs = layout(
            (CF, (2, 2, 2, BS), F32),
            (CF, (2, 2, 2, CF), F32),
            (CF, (2, 2, CF), F32),
            (CF, (2, CF), F32),
            (CF, (2, 2, CF), F32),
            (128, (C,), F32),
            (128, (C,), F32), at=vaug_at + 11 * NH * 32 + NH * WIN + NH // 2 * 128)
        x1_at = 2 * B * C + 2 * C + 2 * NH * B + NH // 2 * 4 + 2 * 1024
        gl_at = x1_at + 3 * NT * C + 2 * 1024

        def over(at, rows, a, b):
            return later[0:rows, at:at + a * b].rearrange("p (a b) -> p a b", a=a)

        ya = over(0, CF, 2, 1024)
        an = over(2048, CF, 2, NW * 64)
        fbp = over(3200, 128, 8, C)
        fbf = over(3200 + 8 * C, 128, 8, C)
        dk = over(3200 + 16 * C, CF, 2, NW * 64)
        o1, = layout((CF, (2, 2, NW * 64), F32), at=vaug_at)
        sm, sc, ss = (arena[0:126, gl_at + i * 5 * C:gl_at + (i + 1) * 5 * C].rearrange("p (t c) -> p t c", t=5)
                      for i in range(3))
        iv = arena[0:CF, gl_at + 15 * C:gl_at + 15 * C + 2048].rearrange("p (f n) -> p f n", f=2)
        ibq = arena[:, x1_at:x1_at + 8 * CAS].rearrange("p (j c) -> p j c", j=8)
        y2 = xt
        res = x1n

        x_in = [sem(f"x_in{i}") for i in range(2)]
        small_in = sem("small_in")
        bqkv_in = sem("bqkv_in")
        weights_in = sem("weights_in")
        rel_in = sem("rel_in")
        wqkv_in = sem("wqkv_in")
        bv_in = sem("bv_in")
        rows_in = sem("rows_in")
        late_in = sem("late_in")
        tables_in = sem("tables_in")
        rows_set = sem("rows_set")
        rows_copied = sem("rows_copied")
        set_up = sem("set_up")
        stats_done = sem("stats_done")
        mean_done = sem("mean_done")
        veps_done = sem("veps_done")
        rstd_done = sem("rstd_done")
        xn_done = sem("xn_done")
        k_scaled = sem("k_scaled")
        q_high = sem("q_high")
        k_high = sem("k_high")
        r_high = sem("r_high")
        k_padded = sem("k_padded")
        v_padded = sem("v_padded")
        q_loaded = [sem(f"q_loaded{i}") for i in range(NOP)]
        k_loaded = [sem(f"k_loaded{i}") for i in range(NOP)]
        r_loaded = [sem(f"r_loaded{i}") for i in range(NOP)]
        max_found = sem("max_found")
        max_high = sem("max_high")
        max_split = sem("max_split")
        max_loaded = [sem(f"max_loaded{i}") for i in range(2)]
        xpb_done = sem("xpb_done")
        rden_done = sem("rden_done")
        x1n_done = sem("x1n_done")
        x1b_done = sem("x1b_done")
        y_stored = sem("y_stored")
        y2_in = sem("y2_in")
        wsum_done = sem("wsum_done")
        wbd_done = sem("wbd_done")
        wps_done = sem("wps_done")
        bsum_done = sem("bsum_done")
        wab_half = sem("wab_half")
        fb_kept = sem("fb_kept")
        ib_kept = sem("ib_kept")
        clipped = sem("clipped")
        shrunk = sem("shrunk")
        out_stored = sem("out_stored")

        xd = a["x"].rearrange("b (t h) w c -> (h w) (b t) c", t=2)
        scratch = a["scratch"]
        sd = scratch.rearrange("b (t h) w c -> (h w) (b t) c", t=2)

        GROUPS = [(0, 2 * WIN), (2 * WIN, 4 * WIN), (GC, QN)]

        def win(t, piece, b0, nb):
            if piece == "G":
                return t[:, b0 * WIN:(b0 + nb) * WIN].rearrange("p (b h w) -> p b h w", b=nb, h=WS)
            if piece == "B":
                return t[:, QB + b0 * 28:QB + (b0 + nb) * 28].rearrange("p (b h w) -> p b h w", b=nb, h=2)
            return t[:, QR + b0 * 32:QR + (b0 + nb) * 32].rearrange("p (b h w) -> p b h w", b=nb, h=H)

        def nat(t, piece, nb):
            v = t.rearrange("p (b h w) -> p b h w", b=nb, h=H)
            return {"G": v[:, :, 0:WS, 0:WS], "B": v[:, :, WS:H, 0:WS], "R": v[:, :, :, WS:W]}[piece]

        def rel_pieces(axis, part, p, t):
            lo, n = 8 * p, min(8, WS - 8 * p)
            g = t[:, 0:GC].rearrange("p (b h w) -> p b h w", b=B, h=WS)
            bt = t[:, QB:QB + 112].rearrange("p (b h w) -> p b h w", b=B, h=2)
            r = t[:, QR:QN].rearrange("p (b h w) -> p b h w", b=B, h=H)
            s = part.rearrange("p (l b m) -> p l b m", l=8, b=B)
            if axis == 0:
                out = [(s[:, 0:n, :, 0:WS], g[:, :, lo:lo + n].rearrange("p b h w -> p h b w")),
                       (s[:, :, :, WS:W], r[:, :, lo:lo + 8].rearrange("p b h w -> p h b w"))]
                if p == 1:
                    out.append((s[:, 6:8, :, 0:WS], bt.rearrange("p b h w -> p h b w")))
            else:
                out = [(s[:, 0:n, :, 0:WS], g[:, :, :, lo:lo + n].rearrange("p b h w -> p w b h")),
                       (s[:, 0:n, :, WS:H], bt[:, :, :, lo:lo + n].rearrange("p b h w -> p w b h"))]
                if p == 1:
                    out.append((s[:, 6:8], r.rearrange("p b h w -> p w b h")))
            return out

        block = ctx.enter_context(nc.Block())

        @block.sync
        def _(sp):
            for i in range(2):
                sp.dma_start(xt[:, 4 * i:4 * i + 4], xd[:, 4 * i:4 * i + 4]).then_inc(x_in[i], 16)
            sp.dma_start(wqkv[:], a["qkv_w"].rearrange("(f p) n -> p f n", f=2)).then_inc(wqkv_in, 16)
            sp.dma_start(rows_k, a["krows"][64:128, :]).then_inc(rows_in, 16)
            sp.dma_start(rows_q, a["qrows"][64:128, :]).then_inc(rows_in, 16)
            sp.dma_start(wproj[:], a["proj_w"].rearrange("(f p) n -> p f n", f=2)).then_inc(weights_in, 16)
            sp.dma_start(wf1[:], a["fc1_w"].rearrange("(f p) n -> p f n", f=2)).then_inc(weights_in, 16)
            sp.dma_start(wf2[:], a["fc2_w"].rearrange("(m p) n -> p m n", m=6)).then_inc(weights_in, 16)
            sp.wait_ge(rows_set, 2)
            for i in range(1, NOP):
                sp.dma_start(raw(kop[64:128, i]), raw(kop[64:128, 0])).then_inc(rows_copied, 16)
                sp.dma_start(raw(qop[64:128, i]), raw(qop[64:128, 0])).then_inc(rows_copied, 16)
            def load_maxima(h):
                sp.wait_ge(*is_read(("mx", h)))
                sp.dma_start(raw(qop[126:128, h % NOP, 0:GC]), raw(maxg[:, h % 2])).then_inc(max_loaded[h % 2], 16)
                sp.dma_start(raw(qop[126:128, h % NOP, QB:QN]), raw(maxw[:, h % 2])).then_inc(max_loaded[h % 2], 16)

            for h in range(NH):
                f, j, o = h // HH, h % HH, h % NOP
                if h >= NOP:
                    sp.wait_ge(*is_full(("E", h - NOP, 4)))
                    sp.wait_ge(*is_full(("E", h - NOP, 5)))
                p0, p1 = HD * j, HD * (j + 1)
                for g in range(3):
                    sp.wait_ge(*is_read(("q", f, g)))
                for part in range(2):
                    src = q2[p0:p1, f, part, None, :].to_broadcast([HD, 2, QN])
                    sp.dma_start(raw(qop[32 * part:32 * part + 32, o]), raw(src)).then_inc(q_loaded[o], 16)
                for g in range(3):
                    sp.wait_ge(*is_read(("k", f, g)))
                sp.wait_ge(k_padded, 2 * (f + 1))
                for copy in range(2):
                    sp.dma_start(raw(kop[32 * copy:32 * copy + 32, o]), raw(k2[p0:p1, f])).then_inc(k_loaded[o], 16)
                if h >= AHEAD:
                    load_maxima(h - AHEAD)
                if 3 <= h < 9:
                    sp.wait_ge(*is_full(("v", 5)))
                    dst, name = ((fw, "fw"), (cas, "cas"), (fg, "fg"), (ig, "ig"), (iw14, "iw14"), (iw8, "iw8"))[h - 3]
                    sp.dma_start(dst, a[name]).then_inc(tables_in, 16)
            for h in range(NH - AHEAD, NH):
                load_maxima(h)
            for n in range(4):
                sp.wait_ge(*is_read(("f2", n)))
                sp.dma_start(sd[:, 2 * n:2 * n + 2], y[:, 2 * n:2 * n + 2]).then_inc(y_stored, 16)
            sp.wait_ge(y_stored, 64)
            sw = scratch.rearrange("b h w c -> (b h) w c")
            sp.dma_start(y2[0:64, :, :], sw[:, 0:8, :]).then_inc(y2_in, 16)
            sp.dma_start(y2[64:128, 0, :], sw[:, 8, :]).then_inc(y2_in, 16)
            for j in range(1, 8):
                sp.dma_start(y2[64:128, j, :], sw[:, W - j, :]).then_inc(y2_in, 16)
            od = a["out"].rearrange("b h w c -> (b h) w c")
            for n in range(4):
                sp.wait_ge(*is_read(("ic", n)))
                sp.dma_start(od[:, 2 * n:2 * n + 2, :], res[0:64, 2 * n:2 * n + 2, :]).then_inc(out_stored, 16)
                for j in (2 * n, 2 * n + 1):
                    sp.dma_start(od[:, W - j if j else 8, :], res[64:128, j, :]).then_inc(out_stored, 16)
            sp.wait_ge(out_stored, 16 * 12)

        @block.gpsimd
        def _(pool):
            pool.dma_start(bqkv[:], a["qkv_b"].rearrange("(f p) -> p f", p=CF), allow_slow_non_contiguous=True).then_inc(bqkv_in, 16)
            pool.dma_start(bv[:], a["qkv_b"][2 * C:3 * C].partition_broadcast(128)).then_inc(bv_in, 16)
            nc.gpsimd.memset(mhalf[:], -0.5).then_inc(set_up, 1)
            nc.gpsimd.memset(h1t[:, :, QB + 112:QR], 0.0).then_inc(set_up, 1)
            for f in range(2):
                nc.gpsimd.memset(raw(relc[:, f, :, :, QB + 112:QR]), 0.0).then_inc(set_up, 1)
            nc.gpsimd.memset(negmax[:], 0.0).then_inc(set_up, 1)
            pool.wait_ge(set_up, 5)
            for i in range(2):
                pool.wait_ge(veps_done, i + 1)
                nc.gpsimd.tensor_tensor(rstd[:, 0, 4 * i:4 * i + 4], veps[:, 0, 4 * i:4 * i + 4],
                                        mhalf[:, 0:4], ALU.pow).then_inc(rstd_done, 1)
            nc.gpsimd.memset(vaug[:, :, :, HD:2 * HD], 1.0).then_inc(set_up, 1)

            def halves(row):
                return row.rearrange("n o -> (n o)").rearrange("(f p) -> p f", p=CF)

            for dst, src in (
                    (pb[:], a["proj_b"].partition_broadcast(128)),
                    (f2b[:], a["fc2_b"].partition_broadcast(128)),
                    (f1b[:], a["fc1_b"].rearrange("(m p) -> p m", p=128)),
                    (ln2[:, :, 0], a["ln2_g"].rearrange("(f p) -> p f", p=CF)),
                    (ln2[:, :, 1], a["ln2_b"].rearrange("(f p) -> p f", p=CF)),
                    (half4[:], a["half4"]),
                    (b20c[:], halves(a["b2"][0])),
                    (b2r[:, 0], a["b2"][0].rearrange("n o -> (n o)").partition_broadcast(128)),
                    (b2r[:, 1], a["b2"][1].rearrange("n o -> (n o)").partition_broadcast(128)),
                    (b1c[:, 0], halves(a["b1"][0])),
                    (b1c[:, 1], halves(a["b1"][1])),
                    (w12[:, 0, 0], a["w1"][0].rearrange("(f n) i o -> (n i) f o", f=2)),
                    (w12[:, 0, 1], a["w1"][1].rearrange("(f n) i o -> (n i) f o", f=2)),
                    (w12[:, 1, 0], a["w2"][0].rearrange("(f n) i o -> (n i) f o", f=2)),
                    (w12[:, 1, 1], a["w2"][1].rearrange("(f n) i o -> (n i) f o", f=2))):
                pool.dma_start(dst, src, allow_slow_non_contiguous=True).then_inc(late_in, 16)
            for f in range(2):
                pool.wait_ge(*is_read(("k", f, 2)))
                for at, n in ((KPB + 16, PADB - 16), (KPR, PADR)):
                    nc.gpsimd.tensor_copy(k2[:, f, :, at:at + n],
                                          k2[:, f, :, KPB:KPB + 1].to_broadcast([CF, 2, n])).then_inc(k_padded, 1)
                for j in range(HH):
                    h = f * HH + j
                    o = h % NOP
                    if h == 0:
                        pool.wait_ge(rows_copied, 16 * 2 * (NOP - 1))
                    if h >= NOP:
                        pool.wait_ge(*is_full(("E", h - NOP, 4)))
                        pool.wait_ge(*is_full(("E", h - NOP, 5)))
                    for axis in range(2):
                        for p in range(2):
                            pool.wait_ge(*is_read(("rel", f, axis, p)))
                        pool.dma_start(raw(qop[64 + 32 * axis:92 + 32 * axis, o]),
                                       raw(relc[WS * j:WS * (j + 1), f, axis])).then_inc(r_loaded[o], 16)
            pool.wait_ge(late_in, 15 * 16)
            for t in range(NT):
                nc.gpsimd.tensor_tensor(xt[:, t], xt[:, t], pb[:], ALU.add).then_inc(xpb_done, 1)
            for i in range(2):
                nc.gpsimd.tensor_tensor(wsum[:, i, 0], w12[:, i, 0], w12[:, i, 1], ALU.add).then_inc(wsum_done, 1)
                nc.gpsimd.tensor_tensor(wsum[:, i, 1], w12[:, i, 0], w12[:, i, 1], ALU.subtract).then_inc(wsum_done, 1)
            pool.wait_ge(wsum_done, 4)
            for i in range(2):
                for x in range(2):
                    nc.gpsimd.tensor_tensor(
                        wbd[:, i, x].rearrange("p f (n o) -> p f n o", n=NB // 2),
                        wsum[:, i, x, :, None].to_broadcast([CF, 2, NB // 2, BS]),
                        half4[:, None, :, None].to_broadcast([CF, 2, NB // 2, BS]), ALU.mult).then_inc(wbd_done, 1)
            pool.wait_ge(wbd_done, 4)
            nc.gpsimd.tensor_tensor(wps[:], wbd[:, 1, 0], wbd[:, 1, 1], ALU.add).then_inc(wps_done, 1)
            nc.gpsimd.tensor_tensor(bsum, b2r[:, 0], b2r[:, 1], ALU.add).then_inc(bsum_done, 1)
            for i in range(2):
                pool.wait_ge(veps_done, 3 + i)
                nc.gpsimd.tensor_tensor(rstd[:, 1, 4 * i:4 * i + 4], veps[:, 1, 4 * i:4 * i + 4],
                                        mhalf[:, 0:4], ALU.pow).then_inc(rstd_done, 1)
            for n in range(4):
                pool.wait_ge(*is_read(("pr", n)))
                for t in (2 * n, 2 * n + 1):
                    nc.gpsimd.tensor_tensor(x1b[:, t], x1[:, t], f2b[:], ALU.add).then_inc(x1b_done, 1)

        def normalised(eng, key, f, bp, into):
            eng.wait_ge(*is_full(key))
            for piece in "GBR":
                ins = into(win(h1t[:, f], piece, 2 * bp, 2), nat(ps(key)[0:CF, :], piece, 2))
            ins.then_inc(emptied(key), 1)

        def outputs_read(eng, copy, f, bp):
            key = ("oT", f, bp)
            eng.wait_ge(*is_full(key))
            if bp < 2:
                ins = copy(nat(ot[:, f, 512 * bp:512 * bp + 512], "G", 2),
                           ps(key)[0:CF, 0:2 * WIN].rearrange("p (b h w) -> p b h w", b=2, h=WS))
            else:
                copy(nat(ot[:, f], "B", B), ps(key)[0:CF, 0:112].rearrange("p (b h w) -> p b h w", b=B, h=2))
                ins = copy(nat(ot[:, f], "R", B),
                           ps(key)[0:CF, 128:256].rearrange("p (b h w) -> p b h w", b=B, h=H))
            ins.then_inc(emptied(key), 1)

        def fa_read(eng, copy, n, f):
            key = ("fa", n, f)
            eng.wait_ge(*is_full(key))
            src = ps(key)[0:CF, 0:400].rearrange("p (t m) -> p t m", t=2)
            dst = ya[:, f].rearrange("p (m g) -> p m g", m=16)[:, :, 16 * n:16 * n + 16]
            copy(dst.rearrange("p m (t h) -> p t m h", t=2),
                 src[:, :, 0:128].rearrange("p t (m h) -> p t m h", m=16))
            dst = an[:, f].rearrange("p (v g) -> p v g", v=NW)[:, :, 16 * n:16 * n + 16]
            copy(dst.rearrange("p v (t h) -> p t v h", t=2),
                 src[:, :, 128:200].rearrange("p t (v h) -> p t v h", v=NW)).then_inc(emptied(key), 1)

        def ia_read(eng, copy, n, f):
            key = ("ia", f, n)
            eng.wait_ge(*is_full(key))
            dst = iv[:, f].rearrange("p (m g) -> p m g", m=16)
            if n < 2:
                copy(dst[:, :, 28 * n:28 * n + 28].rearrange("p m (t g) -> p t m g", t=2),
                     ps(key)[0:CF, 0:448].rearrange("p (t m g) -> p t m g", t=2, m=16)).then_inc(emptied(key), 1)
            else:
                copy(dst[:, :, 56:64],
                     ps(key)[0:CF, 0:128].rearrange("p (m g) -> p m g", m=16)).then_inc(emptied(key), 1)

        def pair(key):
            return ps(key)[:, 0:2 * CAS].rearrange("p (j c) -> p j c", j=2)

        def k_places(key, f, g, part):
            c0, c1 = GROUPS[g]
            src = ps(key)[0:CF, 0:c1 - c0]
            if g < 2:
                return k2[:, f, part, c0:c1], src
            dst = k2[:, f, part, KB:KB + 2 * (KR - KB)].rearrange("p (g c) -> p g c", g=2)[:, :, 0:128]
            return dst, src.rearrange("p (g c) -> p g c", g=2)

        @block.scalar
        def _(act):
            act.dma_start(ident[:], a["ident"]).then_inc(small_in, 16)
            act.dma_start(ln1[:, :, 0], a["ln1_g"].rearrange("(f p) -> p f", p=CF),
                          allow_slow_non_contiguous=True).then_inc(small_in, 16)
            act.dma_start(ln1[:, :, 1], a["ln1_b"].rearrange("(f p) -> p f", p=CF),
                          allow_slow_non_contiguous=True).then_inc(small_in, 16)
            act.dma_start(relpos[:, 0], a["rel_pos_h"][:, None].to_broadcast([2 * WS - 1, HH, HD])).then_inc(rel_in, 16)
            act.dma_start(relpos[:, 1], a["rel_pos_w"][:, None].to_broadcast([2 * WS - 1, HH, HD])).then_inc(rel_in, 16)
            act.dma_start(mask6[:], a["mask6"]).then_inc(rel_in, 16)
            act.wait_ge(rows_in, 32)
            nc.scalar.copy(kop[64:128, 0], rows_k).then_inc(rows_set, 1)
            nc.scalar.copy(qop[64:128, 0], rows_q).then_inc(rows_set, 1)
            act.wait_ge(small_in, 48)
            for bp in range(2):
                normalised(act, ("hT", bp, 0), 0, bp, lambda dst, src: nc.scalar.activation(
                    dst, src, ACT.Identity, scale=ln1[:, 0, 0:1], bias=ln1[:, 0, 1:2]))
            act.wait_ge(k_scaled, 3)

            def rel_high(f, axis, p):
                key = ("rel", f, axis, p)
                act.wait_ge(*is_full(key))
                for src, dst in rel_pieces(axis, ps(key)[0:84, :], p, relc[:, f, axis, 0]):
                    ins = nc.scalar.copy(dst, src)
                ins.then_inc(r_high, 1)

            for f in range(2):
                bq = bqkv[:, f:f + 1]
                for g, (c0, c1) in enumerate(GROUPS):
                    key = ("q", f, g)
                    act.wait_ge(*is_full(key))
                    src = ps(key)[0:CF, 0:c1 - c0]
                    if g < 2:
                        nc.scalar.activation(nat(qf[:, f, 512 * g:512 * g + 512], "G", 2),
                                             src.rearrange("p (b h w) -> p b h w", b=2, h=WS),
                                             ACT.Identity, bias=bq)
                    else:
                        nc.scalar.activation(nat(qf[:, f], "B", B),
                                             src[:, 0:112].rearrange("p (b h w) -> p b h w", b=B, h=2),
                                             ACT.Identity, bias=bq)
                        nc.scalar.activation(nat(qf[:, f], "R", B),
                                             src[:, 128:256].rearrange("p (b h w) -> p b h w", b=B, h=H),
                                             ACT.Identity, bias=bq)
                    nc.scalar.activation(q2[:, f, 0, c0:c1], src, ACT.Identity, bias=bq).then_inc(q_high, 1)
                for g in range(3):
                    key = ("k", f, g)
                    act.wait_ge(*is_full(key))
                    dst, src = k_places(key, f, g, 0)
                    nc.scalar.activation(dst, src, ACT.Identity, bias=bk4[:, f:f + 1]).then_inc(k_high, 1)
                if f == 0:
                    for n in range(4):
                        rel_high(0, n // 2, n % 2)
            for n in range(NH + 3):
                m = n - 2
                for u in range(6):
                    if 6 * n + u in R_STEPS:
                        rel_high(1, *divmod(6 * n + u - 4, 2))
                    if u == 1 and 1 <= n <= NH:
                        h = n - 1
                        key = ("mx", h)
                        act.wait_ge(*is_full(key))
                        if h >= 2:
                            act.wait_ge(max_loaded[h % 2], 32 * (h // 2))
                        nc.scalar.copy(maxg[:, h % 2], ps(key)[0:16, 0:HWIN])
                        nc.scalar.copy(maxw[:, h % 2], ps(key)[0:4, 128:256]).then_inc(emptied(key), 1)
                    if 0 <= m < NH:
                        key = ("E", m, u)
                        act.wait_ge(*is_full(key))
                        src = ps(key)
                        if u < 4:
                            if m >= 1:
                                act.wait_ge(*is_full(("pvg", m - 1)))
                            nc.scalar.activation(pg[:, u], src[0:HWIN, 0:2 * WIN], ACT.Exp).then_inc(emptied(key), 1)
                        else:
                            if m >= 2:
                                act.wait_ge(*is_full(("pvw", m // 2 - 1)))
                            dst, r0, r1 = (pwb, 112, 84) if u == 4 else (pwr, 128, 96)
                            nc.scalar.activation(dst[0:r0, m % 2, 0:128], src[0:r0, 0:128], ACT.Exp)
                            nc.scalar.activation(dst[0:r1, m % 2, 128:384], src[0:r1, 128:384],
                                                 ACT.Exp).then_inc(emptied(key), 1)
                    if u == 1 and 0 <= m - 1 < NH:
                        key = ("pvg", m - 1)
                        act.wait_ge(*is_full(key))
                        nc.scalar.copy(ev[:, m - 1], ps(key)[:, 0:WIN]).then_inc(emptied(key), 1)
            for bp in (2, 0, 1):
                outputs_read(act, nc.scalar.copy, 0, bp)
            act.wait_ge(*is_full("w2T"))
            nc.scalar.copy(w2t.rearrange("p x f c -> p (x f c)"), ps("w2T")[0:CF, 0:4 * CF]).then_inc(emptied("w2T"), 1)
            act.wait_ge(late_in, 15 * 16)

            def shifted_0(bp):
                key = ("mT", bp, 0)
                act.wait_ge(*is_full(key))
                nc.scalar.activation(h2t[:, 0, 512 * bp:512 * bp + 512], ps(key)[0:CF, :], ACT.Identity,
                                     scale=ln2[:, 0, 0:1], bias=ln2[:, 0, 1:2]).then_inc(emptied(key), 1)

            shifted_0(0)
            for n in range(2):
                for m in range(6):
                    if (n, m) == (0, 4):
                        shifted_0(1)
                    key = ("f1", n, m)
                    act.wait_ge(*is_full(key))
                    nc.scalar.activation(gl[:, m, 512 * n:512 * n + 512], ps(key)[:, :], ACT.Gelu,
                                         bias=f1b[:, m:m + 1]).then_inc(emptied(key), 1)
            for n in range(4):
                fa_read(act, nc.scalar.copy, n, 0)
            for n in range(4):
                key = ("fb", n)
                act.wait_ge(*is_full(key))
                nc.scalar.copy(fbp[:, 2 * n:2 * n + 2], pair(key)[:, :, 0:C]).then_inc(fb_kept, 1)
            for f in range(2):
                for x in range(2):
                    for p in range(2):
                        key = ("m1", f, x, p)
                        act.wait_ge(*is_full(key))
                        c0, c1 = ((0, 252), (252, 576))[p]
                        nc.scalar.activation(o1[:, x, f, c0:c1], ps(key)[0:CF, 0:c1 - c0], ACT.Relu,
                                             bias=b1c[:, x, f:f + 1]).then_inc(emptied(key), 1)
            for n in range(3):
                ia_read(act, nc.scalar.copy, n, 0)
            for n in (0, 2):
                key = ("ib", n)
                act.wait_ge(*is_full(key))
                nc.scalar.copy(ibq[:, 2 * n:2 * n + 2], pair(key)).then_inc(emptied(key), 1)

        @block.vector
        def _(dve):
            def norm_stats(ln, i, src):
                for t in range(4 * i, 4 * i + 4):
                    ins = nc.vector.bn_stats(stats[:, ln, t], src[:, t])
                ins.then_inc(stats_done, 1)
                dve.wait_ge(stats_done, 2 * ln + i + 1)
                for t in range(4 * i, 4 * i + 4):
                    ins = nc.vector.bn_aggr(mv[:, ln, t], stats[:, ln, t])
                ins.then_inc(mean_done, 1)
                dve.wait_ge(mean_done, 2 * ln + i + 1)
                nc.vector.tensor_scalar(veps[:, ln, 4 * i:4 * i + 4], mv[:, ln, 4 * i:4 * i + 4, 1], EPS, None,
                                        ALU.add).then_inc(veps_done, 1)

            for i in range(2):
                dve.wait_ge(x_in[i], 16)
                norm_stats(0, i, xt)
            for i in range(2):
                dve.wait_ge(rstd_done, i + 1)
                for t in range(4 * i, 4 * i + 4):
                    ins = nc.vector.tensor_scalar(xn[:, t], xt[:, t], mv[:, 0, t, 0:1], rstd[:, 0, t:t + 1],
                                                  ALU.subtract, ALU.mult)
                ins.then_inc(xn_done, 1)
            dve.wait_ge(rel_in, 48)
            for ax in range(2):
                key = ("relp", ax)
                dve.wait_ge(*is_full(key))
                src = ps(key)[0:CF, :]
                src = bass.AP(tensor=src.tensor, offset=src.offset + WS - 1,
                              ap=[list(src.ap[0]), [1, WS], [0, HH], [-1, WS]])
                nc.vector.tensor_tensor(relw[:, ax].rearrange("p r (j k) -> p r j k", j=HH), src,
                                        mask6[:, None, :, None].to_broadcast([CF, WS, HH, WS]),
                                        ALU.mult).then_inc(emptied(key), 1)
            dve.wait_ge(small_in, 48)
            for bp in range(2):
                normalised(dve, ("hT", bp, 1), 1, bp, lambda dst, src: nc.vector.tensor_scalar(
                    dst, src, ln1[:, 1, 0:1], ln1[:, 1, 1:2], ALU.mult, ALU.add))
            dve.wait_ge(wqkv_in, 16)
            dve.wait_ge(bqkv_in, 16)
            nc.vector.tensor_scalar(bk4[:], bqkv[:, 2:4], HD ** -0.5, None, ALU.mult).then_inc(k_scaled, 1)
            for f in range(2):
                nc.vector.tensor_scalar(wqkv[:, f, C:2 * C], wqkv[:, f, C:2 * C], HD ** -0.5, None,
                                        ALU.mult).then_inc(k_scaled, 1)
            dve.wait_ge(k_scaled, 3)

            def rel_low(f, axis, p):
                key = ("rel", f, axis, p)
                dve.wait_ge(r_high, 4 * f + 2 * axis + p + 1)
                part = ps(key)[0:84, :]
                for (src, low), (_, high) in zip(rel_pieces(axis, part, p, relc[:, f, axis, 1]),
                                                 rel_pieces(axis, part, p, relc[:, f, axis, 0])):
                    ins = nc.vector.tensor_tensor(low, src, high.bitcast(F32), ALU.subtract)
                ins.then_inc(emptied(key), 1)

            for f in range(2):
                for g, (c0, c1) in enumerate(GROUPS):
                    key = ("q", f, g)
                    dve.wait_ge(q_high, 3 * f + g + 1)
                    nc.vector.scalar_tensor_tensor(q2[:, f, 1, c0:c1], ps(key)[0:CF, 0:c1 - c0], bqkv[:, f:f + 1],
                                                   q2[:, f, 0, c0:c1].bitcast(F32), ALU.add,
                                                   ALU.subtract).then_inc(emptied(key), 1)
                for g in range(3):
                    key = ("k", f, g)
                    dve.wait_ge(k_high, 3 * f + g + 1)
                    dst, src = k_places(key, f, g, 1)
                    high, _ = k_places(key, f, g, 0)
                    nc.vector.scalar_tensor_tensor(dst, src, bk4[:, f:f + 1], high.bitcast(F32), ALU.add,
                                                   ALU.subtract).then_inc(emptied(key), 1)
                if f == 0:
                    for n in range(4):
                        rel_low(0, n // 2, n % 2)
            dve.wait_ge(bv_in, 16)
            nc.vector.tensor_copy(vaug[0:96, 10, :, 0:HD],
                                  bv[0:96].rearrange("p (h d) -> p h d", h=NH)).then_inc(v_padded, 1)

            def values(n):
                key = ("v", n)
                dve.wait_ge(*is_full(key))
                rows, tiles = (HWIN, 2) if n < 4 else ((112, 1), (128, 1))[n - 4]
                t = 2 * n if n < 4 else 4 + n
                nc.vector.tensor_tensor(
                    vaug[0:rows, t:t + tiles, :, 0:HD],
                    ps(key)[0:rows, 0:tiles * C].rearrange("p (t h d) -> p t h d", t=tiles, h=NH),
                    bv[0:rows, None].to_broadcast([rows, tiles, C]).rearrange("p t (h d) -> p t h d", h=NH),
                    ALU.add).then_inc(emptied(key), 1)

            recips = [0]

            def over_sums(key, src, rd, dst):
                dve.wait_ge(*is_full(key))
                nc.vector.reciprocal(rd, src[:, :, :, HD]).then_inc(rden_done, 1)
                recips[0] += 1
                dve.wait_ge(rden_done, recips[0])
                nc.vector.tensor_tensor(dst, src[:, :, :, 0:HD], rd[:, :, :, None].to_broadcast(list(dst.shape)),
                                        ALU.mult).then_inc(emptied(key), 1)

            def tokens_g(u, n):
                key = ("eT", u, n)
                over_sums(key, ps(key)[0:HWIN, :].rearrange("p (h b d) -> p h b d", h=4, b=B),
                          rden[:, u, 4 * n:4 * n + 4],
                          on[:, u].rearrange("p b (h d) -> p h b d", h=NH)[:, 4 * n:4 * n + 4])

            def tokens_w(n):
                key, hs = ("wT", n), (8, 4)[n]
                over_sums(key, ps(key)[:, 0:64 * hs].rearrange("p (h g d) -> p h g d", h=hs, g=2),
                          rdenw[:, 8 * n:8 * n + hs],
                          onw.rearrange("p g (h d) -> p h g d", h=NH)[:, 8 * n:8 * n + hs])

            dve.wait_ge(set_up, 5)
            values(0)
            values(1)
            for n in range(NH + 3):
                for u in range(6):
                    if n < NH:
                        key = ("S", n, u)
                        dve.wait_ge(*is_full(key))
                        if u == 0 and n >= 2:
                            dve.wait_ge(max_split, n - 1)
                        rows, cols, width, at = (HWIN, 2, WIN, 2 * u) if u < 4 else (
                            (128, 1, KR - KB, 8), (128, 1, KN - KR, 9))[u - 4]
                        nc.vector.tensor_reduce(negmax[0:rows, n % 2, at:at + cols],
                                                ps(key)[0:rows, 0:cols * width].rearrange("p (t k) -> p t k", t=cols),
                                                AX.X, ALU.max, negate=True).then_inc(emptied(key), 1)
                    if 6 * n + u in V_STEPS:
                        values(6 * n + u + 2)
                    if 6 * n + u in R_STEPS:
                        rel_low(1, *divmod(6 * n + u - 4, 2))
                    if u == 1 and 4 <= n <= NH + 2 and n % 2 == 0:
                        i = (n - 4) // 2
                        key = ("pvw", i)
                        dve.wait_ge(*is_full(key))
                        nc.vector.tensor_copy(evw[:, i], ps(key)[:, 0:128]).then_inc(emptied(key), 1)
                    if n in (NH, NH + 1) and u in (2, 4):
                        tokens_g(u // 2 - 1, n - NH)
                    if n == NH + 1 and u == 5:
                        tokens_w(0)
                if n < NH:
                    dve.wait_ge(*is_read(("S", n, 4)))
                    dve.wait_ge(*is_read(("S", n, 5)))
                    if n >= 2:
                        dve.wait_ge(*is_full(("mx", n - 2)))
                    whole, parts = negmax[:, n % 2], negmax2[:, n % 2]
                    nc.vector.tensor_copy(parts[:, 0:8].bitcast(F32R), whole[:, 0:8])
                    nc.vector.tensor_copy(parts[:, 16:18].bitcast(F32R), whole[:, 8:10]).then_inc(max_high, 1)
                    dve.wait_ge(max_high, n + 1)
                    nc.vector.tensor_tensor(parts[:, 8:16], whole[:, 0:8], parts[:, 0:8], ALU.subtract)
                    nc.vector.tensor_tensor(parts[:, 18:20], whole[:, 8:10], parts[:, 16:18],
                                            ALU.subtract).then_inc(max_split, 1)
            tokens_w(1)
            for u in range(2):
                tokens_g(u, 2)
            for bp in (2, 0, 1):
                outputs_read(dve, nc.vector.tensor_copy, 1, bp)
            dve.wait_ge(xpb_done, NT)

            def residual(n):
                key = ("pr", n)
                dve.wait_ge(*is_full(key))
                nc.vector.tensor_tensor(x1[:, 2 * n:2 * n + 2], ps(key)[:, 0:2 * C].rearrange("p (t c) -> p t c", t=2),
                                        xt[:, 2 * n:2 * n + 2], ALU.add).then_inc(emptied(key), 1)

            def x1_normalised(i):
                dve.wait_ge(rstd_done, 3 + i)
                for t in range(4 * i, 4 * i + 4):
                    ins = nc.vector.tensor_scalar(x1n[:, t], x1[:, t], mv[:, 1, t, 0:1], rstd[:, 1, t:t + 1],
                                                  ALU.subtract, ALU.mult)
                ins.then_inc(x1n_done, 1)

            def shifted_1(bp):
                key = ("mT", bp, 1)
                dve.wait_ge(*is_full(key))
                nc.vector.tensor_scalar(h2t[:, 1, 512 * bp:512 * bp + 512], ps(key)[0:CF, :], ln2[:, 1, 0:1],
                                        ln2[:, 1, 1:2], ALU.mult, ALU.add).then_inc(emptied(key), 1)

            residual(0)
            residual(1)
            dve.wait_ge(*is_read(("pr", 0)))
            dve.wait_ge(*is_read(("pr", 1)))
            norm_stats(1, 0, x1)
            residual(2)
            x1_normalised(0)
            residual(3)
            dve.wait_ge(late_in, 15 * 16)
            shifted_1(0)
            dve.wait_ge(*is_read(("pr", 2)))
            dve.wait_ge(*is_read(("pr", 3)))
            norm_stats(1, 1, x1)
            x1_normalised(1)
            dve.wait_ge(*is_full("w2p"))
            dve.wait_ge(wps_done, 1)
            nc.vector.tensor_tensor(wab[:, 0], ps("w2p")[0:CF, 0:2 * CF].rearrange("p (f c) -> p f c", f=2),
                                    wbd[:, 1, 0], ALU.add)
            nc.vector.tensor_tensor(wab[:, 1], ps("w2p")[0:CF, 2 * CF:4 * CF].rearrange("p (f c) -> p f c", f=2),
                                    wps[:], ALU.add).then_inc(emptied("w2p"), 1)
            dve.wait_ge(*is_full("b2w"))
            dve.wait_ge(bsum_done, 1)
            nc.vector.tensor_tensor(bs, ps("b2w")[:, 0:C], bsum, ALU.add).then_inc(emptied("b2w"), 1)
            shifted_1(1)
            dve.wait_ge(x1b_done, NT)
            for n in range(4):
                key = ("f2", n)
                dve.wait_ge(*is_full(key))
                nc.vector.tensor_tensor(y[:, 2 * n:2 * n + 2], ps(key)[:, 0:2 * C].rearrange("p (t c) -> p t c", t=2),
                                        x1b[:, 2 * n:2 * n + 2], ALU.add).then_inc(emptied(key), 1)
            for n in range(4):
                fa_read(dve, nc.vector.tensor_copy, n, 1)
            for n in range(4):
                key = ("fb", n)
                dve.wait_ge(fb_kept, n + 1)
                nc.vector.tensor_copy(fbf[:, 2 * n:2 * n + 2], pair(key)[:, :, C:0:-1]).then_inc(emptied(key), 1)
            for f in range(2):
                for p, (c0, c1) in enumerate(((0, 512), (512, 576))):
                    key = ("fc", f, p)
                    dve.wait_ge(*is_full(key))
                    nc.vector.tensor_copy(dk[:, f, c0:c1], ps(key)[0:CF, 0:c1 - c0]).then_inc(emptied(key), 1)
            for n in range(3):
                key = ("m2", n)
                dve.wait_ge(*is_full(key))
                rows, tiles = (126, 2) if n < 2 else (72, 1)
                t = slice(2 * n, 2 * n + tiles)
                nc.vector.tensor_tensor(sm[0:rows, t], ps(key)[0:rows, 0:tiles * C].rearrange("p (t c) -> p t c", t=tiles),
                                        bs[0:rows, None].to_broadcast([rows, tiles, C]), ALU.add).then_inc(emptied(key), 1)
                dve.wait_ge(*is_read(key))
                nc.vector.tensor_scalar(sc[0:rows, t], sm[0:rows, t], -SHRINK, SHRINK, ALU.max,
                                        ALU.min).then_inc(clipped, 1)
                dve.wait_ge(clipped, n + 1)
                nc.vector.tensor_tensor(ss[0:rows, t], sm[0:rows, t], sc[0:rows, t], ALU.subtract).then_inc(shrunk, 1)
            for n in range(3):
                ia_read(dve, nc.vector.tensor_copy, n, 1)
            for n in (1, 3):
                key = ("ib", n)
                dve.wait_ge(*is_full(key))
                nc.vector.tensor_copy(ibq[:, 2 * n:2 * n + 2], pair(key)).then_inc(emptied(key), 1)
            dve.wait_ge(y2_in, 9 * 16)
            for n in range(4):
                key = ("ic", n)
                dve.wait_ge(*is_full(key))
                nc.vector.scalar_tensor_tensor(res[:, 2 * n:2 * n + 2],
                                               ps(key)[:, 0:2 * C].rearrange("p (t c) -> p t c", t=2),
                                               1.0 / (B * H * W * C), y2[:, 2 * n:2 * n + 2], ALU.mult,
                                               ALU.add).then_inc(emptied(key), 1)

        @block.tensor
        def _(pe):
            mm = nc.tensor.matmul
            pe.wait_ge(rel_in, 48)
            pe.wait_ge(small_in, 48)
            for ax in range(2):
                key = ("relp", ax)
                mm(ps(key)[0:CF, 0:2 * WS - 1], relpos[:, ax].rearrange("p j d -> p (j d)"),
                   ident[0:2 * WS - 1, 0:2 * WS - 1], start=True, stop=True).then_inc(filled(key), 1)
            for bp in range(2):
                pe.wait_ge(xn_done, bp + 1)
                for f in range(2):
                    key = ("hT", bp, f)
                    for t in range(4):
                        ins = nc.tensor.transpose(ps(key)[0:CF, 128 * t:128 * t + 128],
                                                  xn[:, 4 * bp + t, CF * f:CF * f + CF], ident[:])
                    ins.then_inc(filled(key), 1)
            pe.wait_ge(wqkv_in, 16)
            pe.wait_ge(k_scaled, 3)
            pe.wait_ge(set_up, 2)
            for bp in range(2):
                for f in range(2):
                    pe.wait_ge(*is_read(("hT", bp, f)))

            def rel(f, axis, p):
                pe.wait_ge(q_high, 3 * (f + 1))
                pe.wait_ge(*is_read(("relp", axis)))
                qb = qf[:, f].rearrange("p (b h w) -> p b h w", b=B, h=H)
                key = ("rel", f, axis, p)
                pe.wait_ge(*is_free(key))
                for i in range(8):
                    r = 8 * p + i
                    rhs = qb[:, :, r, :] if axis == 0 else qb[:, :, :, r]
                    ins = mm(ps(key)[0:84, 64 * i:64 * i + 64], relw[:, axis, r % WS], rhs, start=True, stop=True)
                ins.then_inc(filled(key), 1)

            def values(n):
                key = ("v", n)
                pe.wait_ge(*is_free(key))
                spans = [(HWIN * (2 * n + t), HWIN) for t in range(2)] if n < 4 else [((QB, 112), (QR, 128))[n - 4]]
                for t, (c0, rows) in enumerate(spans):
                    for c in range(2):
                        ins = mm(ps(key)[0:rows, C * t:C * t + C], h1t[:, c, c0:c0 + rows], wqkv[:, c, 2 * C:3 * C],
                                 start=c == 0, stop=c == 1)
                ins.then_inc(filled(key), 1)

            for f in range(2):
                for x, name in enumerate("qk"):
                    for g, (c0, c1) in enumerate(GROUPS):
                        key = (name, f, g)
                        pe.wait_ge(*is_free(key))
                        for c in range(2):
                            ins = mm(ps(key)[0:CF, 0:c1 - c0], wqkv[:, c, C * x + CF * f:C * x + CF * f + CF],
                                     h1t[:, c, c0:c1], start=c == 0, stop=c == 1)
                        ins.then_inc(filled(key), 1)
                if f == 0:
                    for n in range(4):
                        rel(0, n // 2, n % 2)

            def maxima(h):
                o = h % NOP
                for u in range(6):
                    key = ("S", h, u)
                    if u == 0:
                        for loaded in (q_loaded, k_loaded, r_loaded):
                            pe.wait_ge(loaded[o], 32 * (h // NOP + 1))
                    pe.wait_ge(*is_free(key))
                    if u < 4:
                        for t in range(2):
                            c0 = WIN * u + HWIN * t
                            ins = mm(ps(key)[0:HWIN, WIN * t:WIN * t + WIN], qop[0:126, o, c0:c0 + HWIN],
                                     kop[0:126, o, WIN * u:WIN * u + WIN], start=True, stop=True)
                    else:
                        q0, k0, k1 = ((QB, KB, KR), (QR, KR, KN))[u - 4]
                        ins = mm(ps(key)[:, 0:k1 - k0], qop[0:126, o, q0:q0 + 128], kop[0:126, o, k0:k1],
                                 start=True, stop=True)
                    ins.then_inc(filled(key), 1)
                    yield

            def shifted(h):
                o = h % NOP
                for u in range(6):
                    key = ("E", h, u)
                    if u == 0:
                        pe.wait_ge(max_loaded[h % 2], 32 * (h // 2 + 1))
                    pe.wait_ge(*is_free(key))
                    if u < 4:
                        chunks = [(WIN * u + HWIN * c, HWIN, WIN * c) for c in range(2)]
                        rhs = qop[:, o, WIN * u:WIN * u + WIN]
                    elif u == 4:
                        chunks = [(KB, 112, 0), (KPB, 84, 128), (KPB + 84, 84, 256)]
                        rhs = qop[:, o, QB:QB + 128]
                    else:
                        chunks = [(KR, 128, 0), (KPR, 96, 128), (KPR + 96, 96, 256)]
                        rhs = qop[:, o, QR:QR + 128]
                    n = rhs.shape[1]
                    for c0, rows, at in chunks:
                        ins = mm(ps(key)[0:rows, at:at + n], kop[:, o, c0:c0 + rows], rhs, start=True, stop=True)
                    ins.then_inc(filled(key), 1)
                    yield

            def values_g(h, c):
                key = ("pvg", h)
                if c == 0:
                    if h == 0:
                        pe.wait_ge(*is_read(("v", 5)))
                    pe.wait_ge(*is_free(key))
                    pe.wait_ge(*is_read(("E", h, 2)))
                    pe.wait_ge(*is_read(("E", h, 3)))
                for b in range(B):
                    ins = mm(ps(key)[32 * b:32 * b + 32, 0:WIN], vaug[0:HWIN, 2 * b + c, h],
                             pg[:, b, WIN * c:WIN * c + WIN], start=c == 0, stop=c == 1)
                if c == 1:
                    ins.then_inc(filled(key), 1)

            def values_w(i):
                key = ("pvw", i)
                pe.wait_ge(*is_free(key))
                pe.wait_ge(*is_read(("E", 2 * i + 1, 4)))
                pe.wait_ge(*is_read(("E", 2 * i + 1, 5)))
                for c in range(3):
                    for e in range(2):
                        for g, (src, own, pad) in enumerate(((pwb, 112, 84), (pwr, 128, 96))):
                            rows, tile = (own, 8 + g) if c == 0 else (pad, 10)
                            q0 = 32 * (2 * e + g)
                            ins = mm(ps(key)[q0:q0 + 32, 0:128], vaug[0:rows, tile, 2 * i + e],
                                     src[0:rows, e, 128 * c:128 * c + 128], start=c == 0, stop=c == 2)
                ins.then_inc(filled(key), 1)

            def max_rows(h):
                key = ("mx", h)
                pe.wait_ge(*is_free(key))
                pe.wait_ge(max_split, h + 1)
                nc.tensor.transpose(ps(key)[0:16, 0:HWIN], negmax2[0:HWIN, h % 2, 0:16], ident[0:HWIN, 0:HWIN])
                nc.tensor.transpose(ps(key)[0:4, 128:256], negmax2[:, h % 2, 16:20], ident[:]).then_inc(filled(key), 1)

            def tokens_g(u, n):
                key = ("eT", u, n)
                pe.wait_ge(*is_free(key))
                pe.wait_ge(*is_read(("pvg", 4 * n + 3)))
                for i in range(4):
                    ins = nc.tensor.transpose(ps(key)[0:HWIN, 128 * i:128 * i + 128],
                                              ev[:, 4 * n + i, HWIN * u:HWIN * u + HWIN], ident[:])
                ins.then_inc(filled(key), 1)

            def tokens_w(n):
                key, pairs = ("wT", n), (range(0, 4), range(4, 6))[n]
                pe.wait_ge(*is_free(key))
                pe.wait_ge(*is_read(("pvw", pairs[-1])))
                for i, p in enumerate(pairs):
                    ins = nc.tensor.transpose(ps(key)[:, 128 * i:128 * i + 128], evw[:, p], ident[:])
                ins.then_inc(filled(key), 1)

            pe.wait_ge(v_padded, 1)
            pe.wait_ge(set_up, 6)
            pe.wait_ge(rows_set, 2)
            pe.wait_ge(rows_copied, 16 * 2 * (NOP - 1))
            values(0)
            values(1)
            for n in range(NH + 3):
                m = n - 2
                first = maxima(n) if n < NH else None
                second = shifted(m) if 0 <= m < NH else None
                for u in range(6):
                    if first:
                        next(first)
                    if 6 * n + u in V_STEPS:
                        values(6 * n + u + 2)
                    if 6 * n + u in R_STEPS:
                        rel(1, *divmod(6 * n + u - 4, 2))
                    if u == 1 and 1 <= n <= NH:
                        max_rows(n - 1)
                    if second:
                        next(second)
                    if u == 0 and second and m >= 1:
                        values_g(m - 1, 1)
                    if u == 1 and m >= 2 and m % 2 == 0:
                        values_w(m // 2 - 1)
                    if u == 5 and second:
                        values_g(m, 0)
                    if n in (NH, NH + 1) and u in (2, 4):
                        tokens_g(u // 2 - 1, n - NH)
                    if n == NH + 1 and u == 5:
                        tokens_w(0)
                if m == NH - 1:
                    values_g(m, 1)
            tokens_w(1)
            for u in range(2):
                tokens_g(u, 2)

            for bp in (2, 0, 1):
                for f in range(2):
                    key = ("oT", f, bp)
                    pe.wait_ge(*is_free(key))
                    for k in (("eT", 0, 2), ("eT", 1, 2)) if bp < 2 else (("wT", 0), ("wT", 1)):
                        pe.wait_ge(*is_read(k))
                    for i in range(4 if bp < 2 else 2):
                        if bp < 2:
                            b, u = 2 * bp + i // 2, i % 2
                            ins = nc.tensor.transpose(ps(key)[0:CF, HWIN * i:HWIN * i + HWIN],
                                                      on[:, u, b, CF * f:CF * f + CF], ident[0:HWIN, 0:HWIN])
                        else:
                            ins = nc.tensor.transpose(ps(key)[0:CF, 128 * i:128 * i + 128],
                                                      onw[:, i, CF * f:CF * f + CF], ident[:])
                    ins.then_inc(filled(key), 1)
            pe.wait_ge(late_in, 15 * 16)
            pe.wait_ge(weights_in, 48)
            for n in range(4):
                key = ("pr", n)
                pe.wait_ge(*is_free(key))
                for f in range(2):
                    pe.wait_ge(*is_read(("oT", f, 2)))
                    pe.wait_ge(*is_read(("oT", f, n // 2)))
                for t in range(2):
                    for c in range(2):
                        ins = mm(ps(key)[:, C * t:C * t + C], ot[:, c, 128 * (2 * n + t):128 * (2 * n + t) + 128],
                                 wproj[:, c], start=c == 0, stop=c == 1)
                ins.then_inc(filled(key), 1)
            pe.wait_ge(wbd_done, 4)
            pe.wait_ge(*is_free("w2T"))
            for i in range(4):
                ins = nc.tensor.transpose(ps("w2T")[0:CF, CF * i:CF * i + CF], wbd[:, 1, i // 2, i % 2],
                                          ident[0:CF, 0:CF])
            ins.then_inc(filled("w2T"), 1)
            pe.wait_ge(*is_free("b2w"))
            for f in range(2):
                ins = mm(ps("b2w")[:, CF * f:CF * f + CF], b20c[:, f:f + 1].to_broadcast([CF, 128]), wbd[:, 1, 1, f],
                         start=True, stop=True)
            ins.then_inc(filled("b2w"), 1)
            pe.wait_ge(*is_free("w2p"))
            pe.wait_ge(*is_read("w2T"))
            for i in range(4):
                ins = mm(ps("w2p")[0:CF, CF * i:CF * i + CF], w2t[:, i // 2, i % 2], wbd[:, 1, 1, i % 2],
                         start=True, stop=True)
            ins.then_inc(filled("w2p"), 1)

            def normalised_t(bp):
                pe.wait_ge(x1n_done, bp + 1)
                for f in range(2):
                    key = ("mT", bp, f)
                    pe.wait_ge(*is_free(key))
                    for t in range(4):
                        ins = nc.tensor.transpose(ps(key)[0:CF, 128 * t:128 * t + 128],
                                                  x1n[:, 4 * bp + t, CF * f:CF * f + CF], ident[:])
                    ins.then_inc(filled(key), 1)

            def hidden(n, ms):
                for f in range(2):
                    pe.wait_ge(*is_read(("mT", n, f)))
                for m in ms:
                    key = ("f1", n, m)
                    pe.wait_ge(*is_free(key))
                    for c in range(2):
                        ins = mm(ps(key)[:, :], wf1[:, c, 128 * m:128 * m + 128], h2t[:, c, 512 * n:512 * n + 512],
                                 start=c == 0, stop=c == 1)
                    ins.then_inc(filled(key), 1)

            normalised_t(0)
            hidden(0, range(0, 4))
            normalised_t(1)
            hidden(0, range(4, 6))
            hidden(1, range(0, 6))
            for n in range(4):
                key = ("f2", n)
                pe.wait_ge(*is_free(key))
                for m in range(6):
                    pe.wait_ge(*is_read(("f1", n // 2, m)))
                for t in range(2):
                    for m in range(6):
                        ins = mm(ps(key)[:, C * t:C * t + C], gl[:, m, 128 * (2 * n + t):128 * (2 * n + t) + 128],
                                 wf2[:, m], start=m == 0, stop=m == 5)
                ins.then_inc(filled(key), 1)
            pe.wait_ge(tables_in, 6 * 16)
            for n in range(4):
                pe.wait_ge(*is_read(("f2", n)))
                for f in range(2):
                    key = ("fa", n, f)
                    pe.wait_ge(*is_free(key))
                    for t in range(2):
                        ins = mm(ps(key)[0:CF, 200 * t:200 * t + 200], y[:, 2 * n + t, CF * f:CF * f + CF], fw,
                                 start=True, stop=True)
                    ins.then_inc(filled(key), 1)
            for n in range(4):
                for f in range(2):
                    pe.wait_ge(*is_read(("fa", n, f)))
            for n in range(4):
                key = ("fb", n)
                pe.wait_ge(*is_free(key))
                for t in range(2):
                    for f in range(2):
                        j = 2 * n + t
                        ins = mm(ps(key)[:, CAS * t:CAS * t + CAS], ya[:, f, 128 * j:128 * j + 128], cas[:, f],
                                 start=f == 0, stop=f == 1)
                ins.then_inc(filled(key), 1)
            for f in range(2):
                for p, js in enumerate((range(0, 7), range(7, 8))):
                    key = ("fc", f, p)
                    pe.wait_ge(*is_free(key))
                    for j in js:
                        pe.wait_ge(*is_read(("fb", j // 2)))
                        n, c0 = (128, 0) if j == 0 else (64, (64 * (j + 1)) % 512)
                        at = 0 if j == 0 else 256
                        mm(ps(key)[0:CF, c0:c0 + n], fbp[:, j, CF * f:CF * f + CF], fg[:, at:at + n],
                           start=True, stop=False)
                        ins = mm(ps(key)[0:CF, c0:c0 + n], fbf[:, j, CF * f:CF * f + CF], fg[:, at + n:at + 2 * n],
                                 start=False, stop=True)
                    ins.then_inc(filled(key), 1)
            for f in range(2):
                for p in range(2):
                    pe.wait_ge(*is_read(("fc", f, p)))
                for x in range(2):
                    for p in range(2):
                        key = ("m1", f, x, p)
                        pe.wait_ge(*is_free(key))
                        k, nk = (t[:, f].rearrange("p (v g) -> p v g", v=NW) for t in (dk, an))

                        def tiles(t):
                            return t[:, :, 28 * p:28 * p + 28].rearrange("p v (t g) -> p t v g", t=2)

                        for i, (w, v) in enumerate(((0, (k, nk)[x]), (1, (nk, k)[x]))):
                            ins = mm(ps(key)[0:CF, 0:252], wbd[:, 0, w, f], tiles(v), start=i == 0, stop=i == 1)
                        if p == 1:
                            for i, (w, v) in enumerate(((0, (k, nk)[x]), (1, (nk, k)[x]))):
                                ins = mm(ps(key)[0:CF, 252:324], wbd[:, 0, w, f], v[:, :, 56:64],
                                         start=i == 0, stop=i == 1)
                        ins.then_inc(filled(key), 1)
            for f in range(2):
                for x in range(2):
                    for p in range(2):
                        pe.wait_ge(*is_read(("m1", f, x, p)))
            pe.wait_ge(*is_read("w2p"))
            for n in range(3):
                key = ("m2", n)
                pe.wait_ge(*is_free(key))
                for t in range(2 if n < 2 else 1):
                    g0, g1 = 14 * (2 * n + t), min(14 * (2 * n + t) + 14, 64)
                    rows = NW * (g1 - g0)
                    for f in range(2):
                        for x in range(2):
                            lhs = o1[:, x, f, NW * g0:NW * g1]
                            ins = mm(ps(key)[0:rows, C * t + CF * f:C * t + CF * f + CF], lhs, wab[:, x, f],
                                     start=x == 0, stop=x == 1)
                ins.then_inc(filled(key), 1)
            for n in range(3):
                pe.wait_ge(shrunk, n + 1)
                for f in range(2):
                    key = ("ia", f, n)
                    pe.wait_ge(*is_free(key))
                    for t in range(2 if n < 2 else 1):
                        rows, tab = (126, iw14) if n < 2 else (72, iw8)
                        w = tab.shape[1]
                        ins = mm(ps(key)[0:CF, w * t:w * t + w], ss[0:rows, 2 * n + t, CF * f:CF * f + CF], tab,
                                 start=True, stop=True)
                    ins.then_inc(filled(key), 1)
            for n in range(3):
                for f in range(2):
                    pe.wait_ge(*is_read(("ia", f, n)))
            for n in range(4):
                key = ("ib", n)
                pe.wait_ge(*is_free(key))
                for t in range(2):
                    for f in range(2):
                        j = 2 * n + t
                        ins = mm(ps(key)[:, CAS * t:CAS * t + CAS], iv[:, f, 128 * j:128 * j + 128], cas[:, f],
                                 start=f == 0, stop=f == 1)
                ins.then_inc(filled(key), 1)
            for n in range(4):
                key = ("ic", n)
                pe.wait_ge(*is_free(key))
                pe.wait_ge(*is_read(("ib", n)))
                for t in range(2):
                    j = 2 * n + t
                    at = 0 if j == 0 else 256
                    mm(ps(key)[:, C * t:C * t + C], ig[:, at:at + 128], ibq[:, j, 0:C], start=True, stop=False)
                    ins = mm(ps(key)[:, C * t:C * t + C], ig[:, at + 128:at + 256], ibq[:, j, C:0:-1],
                             start=False, stop=True)
                ins.then_inc(filled(key), 1)


_INS = {"x": "x", "L0_conv_ln1_g": "ln1_g", "L0_conv_ln1_b": "ln1_b", "L0_conv_qkv_w": "qkv_w",
        "L0_conv_qkv_b": "qkv_b", "L0_conv_proj_w": "proj_w", "L0_conv_proj_b": "proj_b",
        "L0_conv_rel_pos_h": "rel_pos_h", "L0_conv_rel_pos_w": "rel_pos_w", "L0_conv_ln2_g": "ln2_g",
        "L0_conv_ln2_b": "ln2_b", "L0_conv_fc1_w": "fc1_w", "L0_conv_fc1_b": "fc1_b", "L0_conv_fc2_w": "fc2_w",
        "L0_conv_fc2_b": "fc2_b", "L1_conv_w1": "w1", "L1_conv_b1": "b1", "L1_conv_w2": "w2", "L1_conv_b2": "b2"}


def kernel(**inputs):
    import concourse.bacc as bacc
    from concourse.bass_utils import run_bass_kernel_spmd

    nc = bacc.Bacc("TRN2", target_bir_lowering=False, num_devices=1)
    arrays, aps = {}, {}
    given = {short: np.ascontiguousarray(inputs[name]) for name, short in _INS.items()}
    for name, v in {**given, **tables()}.items():
        arrays[f"in_{name}"] = v
        aps[name] = nc.dram_tensor(f"in_{name}", v.shape, mybir.dt.from_np(v.dtype), kind="ExternalInput").ap()
    aps["scratch"] = nc.dram_tensor("scratch", (B, H, W, C), F32, kind="Internal").ap()
    aps["out"] = nc.dram_tensor("out_dram", (B, H, W, C), F32, kind="ExternalOutput").ap()
    build(nc, aps)
    r = run_bass_kernel_spmd(nc, [arrays], core_ids=[0])
    return r.results[0]["out_dram"]
```

```python
from contextlib import ExitStack

import concourse.bass as bass
from concourse import mybir
import numpy as np

F32 = mybir.dt.float32
F32R = mybir.dt.float32r
ALU = mybir.AluOpType
ACT = mybir.ActivationFunctionType
AX = mybir.AxisListType

B, H, W, C = 4, 16, 16, 192
NH, HD, WS = 12, 16, 14
MLP = 768
EPS = 1e-6
CF = C // 2
NT = B * H * W // 128
HH = NH // 2
WIN = WS * WS
HWIN = WIN // 2
GC = B * WIN
QB, QR, QN = GC, GC + 128, GC + 256
PADB = (WS - 2) * WS
PADR = WS * (WS - 2) + (WS - 2) * 2
KB, KPB = GC, GC + 112
KR = KPB + PADB
KPR = KR + 128
KN = KPR + PADR
BIG = 1e30
NB = 8
BS = C // NB
SHRINK = 0.01
NW = 9
CAS = C + 1


def tables():
    t = {}
    t["ident"] = np.eye(128)
    t["mask6"] = np.repeat(np.eye(HH), HD, axis=0)
    t["half4"] = 0.5 * np.repeat(np.eye(NB // 2), BS, axis=0)
    q = np.zeros((128, QN))
    k = np.zeros((128, KN))

    def key(col, kh, kw):
        for part in range(2):
            k[64 + 2 * kh + part, col] = 1
            k[96 + 2 * kw + part, col] = 1

    k[126:128] = 1
    for b in range(B):
        others = [92 + i for i in range(B) if i != b]
        for h in range(H):
            for w in range(W):
                if h < WS and w < WS:
                    key(b * WIN + h * WS + w, h, w)
                elif w < WS:
                    col = b * 28 + (h - WS) * WS + w
                    key(KB + col, h - WS, w)
                    k[others, KB + col] = -BIG
                    q[92 + b, QB + col] = 1
                else:
                    col = b * 32 + h * 2 + w - WS
                    corner = h >= WS
                    key(KR + col, h % WS, w - WS)
                    k[others, KR + col] = -BIG
                    k[124 if corner else 125, KR + col] = -BIG
                    q[92 + b, QR + col] = 1
                    q[125 if corner else 124, QR + col] = 1
    n = KPB
    for kh in range(2, WS):
        for kw in range(WS):
            key(n, kh, kw)
            n += 1
    n = KPR
    for kh in range(WS):
        for kw in range(2, WS):
            key(n, kh, kw)
            n += 1
    for kh in range(2, WS):
        for kw in range(2):
            key(n, kh, kw)
            k[124, n] = -BIG
            n += 1
    t["qrows"], t["krows"] = q, k
    w = np.arange(W)
    tw = np.zeros((W, 8, 2))
    tw[:, 0, 0] = 1
    tw[:, 0, 1] = np.cos(np.pi * w)
    for j in range(1, 8):
        tw[:, j, 0] = np.cos(2 * np.pi * j * w / W)
        tw[:, j, 1] = np.sin(2 * np.pi * j * w / W)
    fw = np.zeros((8, W, 8, 2, 8))
    for h in range(8):
        fw[h, :, :, :, h] = tw
    kept = [0, 8] + list(range(1, 8))
    flip = np.zeros((8, W, NW, 8))
    for h in range(8):
        for v, f in enumerate(kept):
            flip[h, (-f) % W, v, 7 - h] = 1
    t["fw"] = np.concatenate([fw.reshape(128, 128), flip.reshape(128, NW * 8)], 1)
    c, s, f = np.meshgrid(np.arange(CF), np.arange(2), np.arange(CF), indexing="ij")
    a = 2 * np.pi * ((c * (2 * f + s)) % C) / C
    t["cas"] = np.cos(a) - np.sin(a)
    b, h = np.meshgrid(np.arange(B), np.arange(H), indexing="ij")
    b, h = b.ravel(), h.ravel()
    u = (h + 9) % H
    g = 2 * np.pi * ((b[:, None] * b[None] * 4 + h[:, None] * u[None]) % 16) / 16
    cg, sg = np.cos(g), np.sin(g)
    z = np.zeros((64, 64))
    t["fg"] = np.concatenate([np.block([[cg, z], [z, cg]]), np.block([[-sg, z], [z, -sg]]),
                              np.concatenate([cg, -sg]), np.concatenate([-sg, -cg])], 1)
    cg, sg = cg.T, sg.T
    t["ig"] = np.concatenate([np.block([[cg, z], [z, cg]]), np.block([[-sg, z], [z, -sg]]),
                              np.block([[cg, cg], [-sg, sg]]), np.block([[-sg, -sg], [-cg, cg]])], 1)
    for name, m in (("iw14", 14), ("iw8", 8)):
        iw = np.zeros((NW, m, 8, 2, m))
        for v, f in enumerate(kept):
            for x in range(m):
                iw[v, x, :, :, x] = tw[f]
        t[name] = iw.reshape(NW * m, 16 * m)
    return {n: np.ascontiguousarray(v, np.float32) for n, v in t.items()}


def bank_order():
    count, place = [0] * 8, {}

    def add(key, bank):
        place[key] = (bank, count[bank])
        count[bank] += 1

    turn = [0]

    def rotate(keys):
        for key in keys:
            add(key, turn[0] % 8)
            turn[0] += 1

    rotate([("hT", bp, f) for bp in range(2) for f in range(2)])
    rotate([("relp", a) for a in range(2)])
    rotate([("q", 0, g) for g in range(3)])
    rotate([("k", 0, g) for g in range(3)])
    rotate([("rel", 0, a, p) for a in range(2) for p in range(2)])
    rotate([("v", n) for n in range(6)])
    beside = [("q", 1, g) for g in range(3)] + [("k", 1, g) for g in range(3)]
    beside += [("rel", 1, a, p) for a in range(2) for p in range(2)]
    for i, key in enumerate(beside):
        add(key, 2 + i % 4)
    for h in range(NH):
        for u in range(6):
            add(("S", h, u), (0, 1, 7)[(6 * h + u) % 3])
            add(("E", h, u), (2, 3, 5)[(6 * h + u) % 3])
        add(("pvg", h), 4)
    for n in range(1, NH + 3):
        if n <= NH:
            add(("mx", n - 1), 6)
        if n >= 4 and n % 2 == 0:
            add(("pvw", n // 2 - 2), 6)
    add("f1c", 7)
    for n in range(2):
        for u in range(2):
            add(("eT", u, n), u)
    add(("wT", 0), 0)
    turn[0] = 1
    rotate([("wT", 1), ("eT", 0, 2), ("eT", 1, 2)])
    rotate([("oT", f, bp) for bp in (2, 0, 1) for f in range(2)])
    rotate([("pr", n) for n in range(4)])
    rotate(["w2T", "b2w", "w2p"])
    rotate([("mT", 0, f) for f in range(2)])
    rotate([("f1", 0, m) for m in range(5)])
    rotate([("mT", 1, f) for f in range(2)])
    rotate([("f1", 0, 5)] + [("f1", 1, m) for m in range(6)])
    rotate([("f2", n) for n in range(4)])
    rotate([("fa", n, f) for n in range(4) for f in (1, 0)])
    rotate([("fb", n) for n in range(4)])
    rotate([("fc", f, p) for f in range(2) for p in range(2)])
    rotate([("m1", f, p) for p in range(3) for f in range(2)])
    rotate([("m2", n) for n in range(3)])
    rotate([("ia", f, n) for n in range(3) for f in (1, 0)])
    rotate([("ib", n) for n in range(4)])
    rotate([("ic", n) for n in range(4)])
    return place


def build(nc, a):
    place = bank_order()
    ctx = ExitStack()
    with ctx:
        def sb(name, shape, dt=F32):
            return ctx.enter_context(nc.sbuf_tensor(name, shape, dt))

        def sem(name):
            return ctx.enter_context(nc.semaphore(name))

        bank = [ctx.enter_context(nc.psum_tensor(f"bank{i}", [128, 512], F32)) for i in range(8)]
        bank_full = [sem(f"bank_full{i}") for i in range(8)]
        bank_free = [sem(f"bank_free{i}") for i in range(8)]

        def ps(key):
            return bank[place[key][0]]

        def filled(key):
            return bank_full[place[key][0]]

        def emptied(key):
            return bank_free[place[key][0]]

        def is_full(key):
            return bank_full[place[key][0]], place[key][1] + 1

        def is_read(key):
            return bank_free[place[key][0]], place[key][1] + 1

        def is_free(key):
            return bank_free[place[key][0]], place[key][1]

        ident = sb("ident", [128, 128])
        mask6 = sb("mask6", [CF, HH])
        xt = sb("xt", [128, NT, C])
        ln1 = sb("ln1", [CF, 2, 2])
        ln2 = sb("ln2", [CF, 2, 2])
        bqkv = sb("bqkv", [CF, 6])
        bk4 = sb("bk4", [CF, 2])
        bv = sb("bv", [128, C])
        pb = sb("pb", [128, C])
        f2b = sb("f2b", [128, C])
        f1b = sb("f1b", [128, 6])
        gelu_warm = sb("gelu_warm", [128, 1])
        f1s = sb("f1s", [128, 6])
        stats = sb("stats", [128, 2, NT, 6])
        mv = sb("mv", [128, 2, NT, 2])
        veps = sb("veps", [128, 2, NT])
        mhalf = sb("mhalf", [128, NT])
        rstd = sb("rstd", [128, 2, NT])
        wproj = sb("wproj", [CF, 2, C])
        with ExitStack() as early:
            wqkv = early.enter_context(nc.sbuf_tensor("wqkv", [CF, 2, 3 * C], F32))
            relpos = early.enter_context(nc.sbuf_tensor("relpos", [2 * WS - 1, 2, HH, HD], F32))
        wf1 = sb("wf1", [CF, 2, 2, MLP], F32R)
        wf2 = sb("wf2", [128, 6, C])
        half4 = sb("half4", [CF, NB // 2])
        w12 = sb("w12", [CF, 2, 2, 2, BS])
        b1c = sb("b1c", [CF, 2, 2])
        b20c = sb("b20c", [CF, 2])
        b2r = sb("b2r", [128, 2, C])
        NOP, NOK = 4, 5
        Q_STEPS = [(0, 0), (0, 1), (0, 2)]
        K_STEPS = [(0, 3), (0, 4), (0, 5)]
        R_STEPS = [(1, 2), (1, 3), (1, 4), (1, 5)]
        W_STEPS = [(NH + 2, 2), (NH + 2, 3), (NH + 2, 4), (NH + 2, 5)]
        B_STEPS = [(NH, 3), (NH + 1, 1), (NH + 1, 3), (NH + 2, 0), (NH + 2, 3)]
        AHEAD = 2
        negmax = sb("negmax", [128, 2, 10])
        negmax2 = sb("negmax2", [128, 2, 20])
        maxg = sb("maxg", [16, 2, HWIN], F32R)
        maxw = sb("maxw", [4, 2, 128], F32R)

        def raw(t):
            return t.bitcast(F32)

        ARENA = 33440
        arena = sb("arena", [128, ARENA])
        with ExitStack() as scores:
            qop = scores.enter_context(nc.sbuf_tensor("qop", [128, NOP, QN], F32R))
            kop = scores.enter_context(nc.sbuf_tensor("kop", [128, NOK, KN], F32R))
        with ExitStack() as mlp:
            h2t = mlp.enter_context(nc.sbuf_tensor("h2t", [CF, 2, 2, 1024], F32R))
        later = sb("later", [128, NOP * QN + NOK * KN])

        def layout(*items, at=0):
            views = []
            for rows, dims, dt in items:
                n = int(np.prod(dims))
                v = arena[0:rows, at:at + n]
                if dt is not F32:
                    v = v.bitcast(dt)
                names = "abcdefg"[:len(dims)]
                if len(dims) > 1:
                    v = v.rearrange(f"p ({' '.join(names)}) -> p {' '.join(names)}",
                                    **{names[i]: dims[i] for i in range(len(dims))})
                views.append(v)
                at += n
            assert at <= ARENA, at
            return views

        (relc, q2, k2, relw, qf, h1t, vaug, ev, evw) = layout(
            (84, (2, 2, 2, QN), F32R),
            (CF, (2, 2, QN), F32R),
            (CF, (2, 2, KN), F32R),
            (CF, (2, WS, 84), F32),
            (CF, (2, 1024), F32),
            (CF, (2, QN), F32),
            (128, (11, NH, 32), F32),
            (128, (NH, WIN), F32),
            (128, (NH // 2, 128), F32))
        relw_at = 2 * 2 * 2 * QN + 2 * 2 * QN + 2 * 2 * KN
        vaug_at = relw_at + 2 * WS * 84 + 2 * 1024 + 2 * QN
        ev_end = vaug_at + 11 * NH * 32 + NH * WIN + NH // 2 * 128
        pg, = layout((HWIN, (B, 2 * WIN), F32), at=ev_end)
        pwb, pwr = layout(
            (112, (2, 3 * 128), F32),
            (128, (2, 3 * 128), F32), at=vaug_at - 2 * QN)
        xn_at = vaug_at + 11 * NH * 32
        wf1_raw, = layout((CF, (2, MLP), F32))
        xn = arena[:, xn_at:xn_at + NT * C].rearrange("p (t c) -> p t c", t=NT)
        rows_at = xn_at + NT * C
        rows_k = arena[64:128, rows_at:rows_at + KN]
        rows_q = arena[64:128, rows_at + KN:rows_at + KN + QN]

        x1_at = 2 * MLP + 2 * 1024
        gl_at = x1_at + 3 * NT * C
        on, onw, rden, rdenw = layout(
            (HWIN, (2, B, C), F32),
            (128, (2, C), F32),
            (HWIN, (2, NH, B), F32),
            (128, (NH, 2), F32), at=gl_at + 6 * 1024)
        ot, x1, x1b, x1n, gl = layout(
            (CF, (2, 1024), F32),
            (128, (NT, C), F32),
            (128, (NT, C), F32),
            (128, (NT, C), F32),
            (128, (6, 1024), F32), at=2 * MLP)
        fw, cas, fg, ig, iw14, iw8 = layout(
            (128, (200,), F32), (CF, (2, CF), F32), (128, (384,), F32), (128, (512,), F32),
            (NW * 14, (224,), F32), (NW * 8, (128,), F32), at=relw_at)
        wsum, wbd, w2t, wps, wab, bsum, bs = layout(
            (CF, (2, 2, BS), F32),
            (CF, (2, 2, 2, CF), F32),
            (CF, (2, 2, CF), F32),
            (CF, (2, CF), F32),
            (CF, (2, 2, CF), F32),
            (128, (C,), F32),
            (128, (C,), F32), at=relw_at + 200 + 2 * CF + 384 + 512 + 224 + 128)

        def over(at, rows, a, b):
            return later[0:rows, at:at + a * b].rearrange("p (a b) -> p a b", a=a)

        ya = over(0, CF, 2, 1024)
        an = over(2048, CF, 2, NW * 64)
        fbp = over(3200, 128, 8, C)
        fbf = over(3200 + 8 * C, 128, 8, C)
        dks = over(3200 + 16 * C, CF, 2, NW * 64)
        dkd = over(3200 + 16 * C + 2 * NW * 64, CF, 2, NW * 64)
        od = over(3200 + 16 * C + 4 * NW * 64, CF, 2, NW * 64)
        o1, y = layout((CF, (2, 2, NW * 64), F32),
                       (128, (NT, C), F32), at=vaug_at)
        sm, sc, ss = (arena[0:126, gl_at + i * 5 * C:gl_at + (i + 1) * 5 * C].rearrange("p (t c) -> p t c", t=5)
                      for i in range(3))
        iv = arena[0:CF, gl_at + 15 * C:gl_at + 15 * C + 2048].rearrange("p (f n) -> p f n", f=2)
        half1 = arena[0:CF, gl_at + 15 * C + 2048:gl_at + 15 * C + 2048 + 1024]
        ibq = arena[:, x1_at:x1_at + 8 * CAS].rearrange("p (j c) -> p j c", j=8)
        y2 = xt
        res = x1n

        x_in = [sem(f"x_in{i}") for i in range(4)]
        small_in = sem("small_in")
        bqkv_in = sem("bqkv_in")
        weights_in = sem("weights_in")
        rel_in = sem("rel_in")
        wqkv_in = sem("wqkv_in")
        bv_in = sem("bv_in")
        rows_in = sem("rows_in")
        late_in = sem("late_in")
        wf1_in = sem("wf1_in")
        wf1_high = sem("wf1_high")
        wf1_scaled = sem("wf1_scaled")
        wf1_split = sem("wf1_split")
        h2_high = sem("h2_high")
        tables_in = sem("tables_in")
        rows_set = sem("rows_set")
        rows_copied = sem("rows_copied")
        set_up = sem("set_up")
        ones_set = sem("ones_set")
        stats_done = sem("stats_done")
        mean_done = sem("mean_done")
        veps_done = sem("veps_done")
        rstd_done = sem("rstd_done")
        xn_done = sem("xn_done")
        k_scaled = sem("k_scaled")
        q_high = sem("q_high")
        k_high = sem("k_high")
        r_high = sem("r_high")
        k_padded = sem("k_padded")
        v_padded = sem("v_padded")
        q_loaded = [sem(f"q_loaded{i}") for i in range(NOP)]
        k_loaded = [sem(f"k_loaded{i}") for i in range(NOK)]
        r_loaded = [sem(f"r_loaded{i}") for i in range(NOP)]
        max_found = sem("max_found")
        max_high = sem("max_high")
        max_split = sem("max_split")
        maxg_loaded = [sem(f"maxg_loaded{i}") for i in range(2)]
        maxw_loaded = [sem(f"maxw_loaded{i}") for i in range(2)]
        xpb_done = sem("xpb_done")
        rden_done = sem("rden_done")
        x1n_done = sem("x1n_done")
        x1b_done = sem("x1b_done")
        y_stored = sem("y_stored")
        y2_in = sem("y2_in")
        wsum_done = sem("wsum_done")
        wbd_done = sem("wbd_done")
        wps_done = sem("wps_done")
        bsum_done = sem("bsum_done")
        wab_half = sem("wab_half")
        summed = sem("summed")
        subtracted = sem("subtracted")
        fb_kept = sem("fb_kept")
        ib_kept = sem("ib_kept")
        od_kept = sem("od_kept")
        o1_done = sem("o1_done")
        clipped = sem("clipped")
        shrunk = sem("shrunk")
        out_stored = sem("out_stored")

        xd = a["x"].rearrange("b (t h) w c -> (h w) (b t) c", t=2)
        scratch = a["scratch"]
        sd = scratch.rearrange("b (t h) w c -> (h w) (b t) c", t=2)

        GROUPS = [(0, 2 * WIN), (2 * WIN, 4 * WIN), (GC, QN)]

        def win(t, piece, b0, nb):
            if piece == "G":
                return t[:, b0 * WIN:(b0 + nb) * WIN].rearrange("p (b h w) -> p b h w", b=nb, h=WS)
            if piece == "B":
                return t[:, QB + b0 * 28:QB + (b0 + nb) * 28].rearrange("p (b h w) -> p b h w", b=nb, h=2)
            return t[:, QR + b0 * 32:QR + (b0 + nb) * 32].rearrange("p (b h w) -> p b h w", b=nb, h=H)

        def nat(t, piece, nb):
            v = t.rearrange("p (b h w) -> p b h w", b=nb, h=H)
            return {"G": v[:, :, 0:WS, 0:WS], "B": v[:, :, WS:H, 0:WS], "R": v[:, :, :, WS:W]}[piece]

        def rel_pieces(axis, part, p, t):
            lo, n = 8 * p, min(8, WS - 8 * p)
            g = t[:, 0:GC].rearrange("p (b h w) -> p b h w", b=B, h=WS)
            bt = t[:, QB:QB + 112].rearrange("p (b h w) -> p b h w", b=B, h=2)
            r = t[:, QR:QN].rearrange("p (b h w) -> p b h w", b=B, h=H)
            s = part.rearrange("p (l b m) -> p l b m", l=8, b=B)
            if axis == 0:
                out = [(s[:, 0:n, :, 0:WS], g[:, :, lo:lo + n].rearrange("p b h w -> p h b w")),
                       (s[:, :, :, WS:W], r[:, :, lo:lo + 8].rearrange("p b h w -> p h b w"))]
                if p == 1:
                    out.append((s[:, 6:8, :, 0:WS], bt.rearrange("p b h w -> p h b w")))
            else:
                out = [(s[:, 0:n, :, 0:WS], g[:, :, :, lo:lo + n].rearrange("p b h w -> p w b h")),
                       (s[:, 0:n, :, WS:H], bt[:, :, :, lo:lo + n].rearrange("p b h w -> p w b h"))]
                if p == 1:
                    out.append((s[:, 6:8], r.rearrange("p b h w -> p w b h")))
            return out

        block = ctx.enter_context(nc.Block())

        @block.sync
        def _(sp):
            for i in range(4):
                sp.dma_start(xt[:, 2 * i:2 * i + 2], xd[:, 2 * i:2 * i + 2]).then_inc(x_in[i], 16)
            sp.dma_start(wqkv[:], a["qkv_w"].rearrange("(f p) n -> p f n", f=2)).then_inc(wqkv_in, 16)
            sp.dma_start(rows_k, a["krows"][64:128, :]).then_inc(rows_in, 16)
            sp.dma_start(rows_q, a["qrows"][64:128, :]).then_inc(rows_in, 16)
            sp.dma_start(wproj[:], a["proj_w"].rearrange("(f p) n -> p f n", f=2)).then_inc(weights_in, 16)
            sp.dma_start(wf2[:], a["fc2_w"].rearrange("(m p) n -> p m n", m=6)).then_inc(weights_in, 16)
            sp.wait_ge(rows_set, 2)
            for i in range(1, NOK):
                if i < NOP:
                    sp.dma_start(raw(qop[64:128, i]), raw(qop[64:128, 0])).then_inc(rows_copied, 16)
                sp.dma_start(raw(kop[64:128, i]), raw(kop[64:128, 0])).then_inc(rows_copied, 16)

            def second_product_over(h):
                sp.wait_ge(*is_full(("E", h, 4)))
                sp.wait_ge(*is_full(("E", h, 5)))

            def load_q(h):
                f, j = h // HH, h % HH
                if h >= NOP:
                    second_product_over(h - NOP)
                for g in range(3):
                    sp.wait_ge(*is_read(("q", f, g)))
                for part in range(2):
                    src = q2[HD * j:HD * (j + 1), f, part, None, :].to_broadcast([HD, 2, QN])
                    sp.dma_start(raw(qop[32 * part:32 * part + 32, h % NOP]), raw(src)).then_inc(q_loaded[h % NOP], 16)

            def load_k(h):
                f, j = h // HH, h % HH
                if h >= NOK:
                    second_product_over(h - NOK)
                for g in range(3):
                    sp.wait_ge(*is_read(("k", f, g)))
                sp.wait_ge(k_padded, 2 * (f + 1))
                for copy in range(2):
                    sp.dma_start(raw(kop[32 * copy:32 * copy + 32, h % NOK]),
                                 raw(k2[HD * j:HD * (j + 1), f])).then_inc(k_loaded[h % NOK], 16)

            def load_maxima(h):
                sp.wait_ge(*is_read(("mx", h)))
                sp.dma_start(raw(qop[126:128, h % NOP, 0:GC]), raw(maxg[:, h % 2])).then_inc(maxg_loaded[h % 2], 16)
                sp.dma_start(raw(qop[126:128, h % NOP, QB:QN]), raw(maxw[:, h % 2])).then_inc(maxw_loaded[h % 2], 16)

            for h in range(NH):
                load_q(h)
                if h == 0:
                    load_k(0)
                if h >= AHEAD:
                    load_maxima(h - AHEAD)
                if h + 1 < NH:
                    load_k(h + 1)
            for h in range(NH - AHEAD, NH):
                load_maxima(h)
            for n in range(4):
                sp.wait_ge(*is_read(("f2", n)))
                sp.dma_start(sd[:, 2 * n:2 * n + 2], y[:, 2 * n:2 * n + 2]).then_inc(y_stored, 16)
            sp.wait_ge(y_stored, 64)
            sw = scratch.rearrange("b h w c -> (b h) w c")
            sp.dma_start(y2[0:64, :, :], sw[:, 0:8, :]).then_inc(y2_in, 16)
            sp.dma_start(y2[64:128, 0, :], sw[:, 8, :]).then_inc(y2_in, 16)
            sp.dma_start(y2[64:128, 1:8, :], sw[:, W - 1:W // 2:-1, :]).then_inc(y2_in, 16)
            od = a["out"].rearrange("b h w c -> (b h) w c")
            for n in range(4):
                sp.wait_ge(*is_read(("ic", n)))
                sp.dma_start(od[:, 2 * n:2 * n + 2, :], res[0:64, 2 * n:2 * n + 2, :]).then_inc(out_stored, 16)
                if n == 0:
                    sp.dma_start(od[:, 8, :], res[64:128, 0, :]).then_inc(out_stored, 16)
                    sp.dma_start(od[:, W - 1, :], res[64:128, 1, :]).then_inc(out_stored, 16)
                else:
                    sp.dma_start(od[:, W - 2 * n:W - 2 * n - 2:-1, :],
                                 res[64:128, 2 * n:2 * n + 2, :]).then_inc(out_stored, 16)
            sp.wait_ge(out_stored, 16 * 9)

        @block.gpsimd
        def _(pool):
            pool.dma_start(bqkv[:], a["qkv_b"].rearrange("(f p) -> p f", p=CF), allow_slow_non_contiguous=True).then_inc(bqkv_in, 16)
            pool.dma_start(bv[:], a["qkv_b"][2 * C:3 * C].partition_broadcast(128)).then_inc(bv_in, 16)
            nc.gpsimd.memset(mhalf[:], -0.5).then_inc(set_up, 1)
            nc.gpsimd.memset(h1t[:, :, QB + 112:QR], 0.0).then_inc(set_up, 1)
            for f in range(2):
                nc.gpsimd.memset(raw(relc[:, f, :, :, QB + 112:QR]), 0.0).then_inc(set_up, 1)
            nc.gpsimd.memset(negmax[:], 0.0).then_inc(set_up, 1)
            pool.wait_ge(set_up, 5)
            for i in range(2):
                pool.wait_ge(veps_done, i + 1)
                nc.gpsimd.tensor_tensor(rstd[:, 0, 4 * i:4 * i + 4], veps[:, 0, 4 * i:4 * i + 4],
                                        mhalf[:, 0:4], ALU.pow).then_inc(rstd_done, 1)

            def halves(row):
                return row.rearrange("n o -> (n o)").rearrange("(f p) -> p f", p=CF)

            later_inputs = (
                    (pb[:], a["proj_b"].partition_broadcast(128)),
                    (f2b[:], a["fc2_b"].partition_broadcast(128)),
                    (f1b[:], a["fc1_b"].rearrange("(m p) -> p m", p=128)),
                    (ln2[:, :, 0], a["ln2_g"].rearrange("(f p) -> p f", p=CF)),
                    (ln2[:, :, 1], a["ln2_b"].rearrange("(f p) -> p f", p=CF)),
                    (half4[:], a["half4"]),
                    (b20c[:], halves(a["b2"][0])),
                    (b2r[:, 0], a["b2"][0].rearrange("n o -> (n o)").partition_broadcast(128)),
                    (b2r[:, 1], a["b2"][1].rearrange("n o -> (n o)").partition_broadcast(128)),
                    (b1c[:, 0], halves(a["b1"][0])),
                    (b1c[:, 1], halves(a["b1"][1])),
                    (w12[:, 0, 0], a["w1"][0].rearrange("(f n) i o -> (n i) f o", f=2)),
                    (w12[:, 0, 1], a["w1"][1].rearrange("(f n) i o -> (n i) f o", f=2)),
                    (w12[:, 1, 0], a["w2"][0].rearrange("(f n) i o -> (n i) f o", f=2)),
                    (w12[:, 1, 1], a["w2"][1].rearrange("(f n) i o -> (n i) f o", f=2)))
            for dst, src in later_inputs[:12]:
                pool.dma_start(dst, src, allow_slow_non_contiguous=True).then_inc(late_in, 16)

            def pad_k(f):
                pool.wait_ge(*is_read(("k", f, 2)))
                for at, n in ((KPB + 16, PADB - 16), (KPR, PADR)):
                    nc.gpsimd.tensor_copy(k2[:, f, :, at:at + n],
                                          k2[:, f, :, KPB:KPB + 1].to_broadcast([CF, 2, n])).then_inc(k_padded, 1)

            pad_k(0)
            for f in range(2):
                for j in range(HH):
                    h = f * HH + j
                    o = h % NOP
                    if h == 0:
                        pool.wait_ge(rows_copied, 16 * (NOP + NOK - 2))
                    if h >= NOP:
                        pool.wait_ge(*is_full(("E", h - NOP, 4)))
                        pool.wait_ge(*is_full(("E", h - NOP, 5)))
                    for axis in range(2):
                        for p in range(2):
                            pool.wait_ge(*is_read(("rel", f, axis, p)))
                        pool.dma_start(raw(qop[64 + 32 * axis:92 + 32 * axis, o]),
                                       raw(relc[WS * j:WS * (j + 1), f, axis])).then_inc(r_loaded[o], 16)
                    if h == NOP - 1:
                        pad_k(1)
                    if NOP <= h < NOP + 3:
                        dst, src = later_inputs[12 + h - NOP]
                        pool.dma_start(dst, src, allow_slow_non_contiguous=True).then_inc(late_in, 16)
            for i in range(NOP):
                pool.wait_ge(r_loaded[i], 32 * len(range(i, HH, NOP)))
            pool.wait_ge(*is_full(("E", 9, 0)))
            for c in range(2):
                pool.dma_start(wf1_raw[:, c], a["fc1_w"][CF * c:CF * c + CF, :]).then_inc(wf1_in, 16)
            for dst, name in ((fw, "fw"), (cas, "cas"), (fg, "fg"), (ig, "ig"), (iw14, "iw14"), (iw8, "iw8")):
                pool.dma_start(dst, a[name]).then_inc(tables_in, 16)
            pool.wait_ge(late_in, 15 * 16)
            for t in range(NT):
                nc.gpsimd.tensor_tensor(xt[:, t], xt[:, t], pb[:], ALU.add).then_inc(xpb_done, 1)
            nc.gpsimd.tensor_tensor(wsum[:, 0], w12[:, 1, 0], w12[:, 1, 1], ALU.add).then_inc(wsum_done, 1)
            nc.gpsimd.tensor_tensor(wsum[:, 1], w12[:, 1, 0], w12[:, 1, 1], ALU.subtract).then_inc(wsum_done, 1)
            pool.wait_ge(wsum_done, 2)
            for i in range(2):
                for x in range(2):
                    nc.gpsimd.tensor_tensor(
                        wbd[:, i, x].rearrange("p f (n o) -> p f n o", n=NB // 2),
                        (w12[:, 0, x] if i == 0 else wsum[:, x])[:, :, None].to_broadcast([CF, 2, NB // 2, BS]),
                        half4[:, None, :, None].to_broadcast([CF, 2, NB // 2, BS]), ALU.mult).then_inc(wbd_done, 1)
            pool.wait_ge(wbd_done, 4)
            nc.gpsimd.tensor_tensor(wps[:], wbd[:, 1, 0], wbd[:, 1, 1], ALU.add).then_inc(wps_done, 1)
            pool.wait_ge(*is_full("f1c"))
            for c in range(2):
                pool.wait_ge(wf1_high, 2 * (c + 1))
                nc.gpsimd.tensor_tensor(wf1_raw[:, c], wf1_raw[:, c], ln2[:, c, 0:1].to_broadcast([CF, MLP]),
                                        ALU.mult).then_inc(wf1_scaled, 1)
            for c in range(2):
                pool.wait_ge(wf1_scaled, c + 1)
                nc.gpsimd.tensor_tensor(wf1[:, 1, c], wf1_raw[:, c], wf1[:, 0, c].bitcast(F32),
                                        ALU.subtract).then_inc(wf1_split, 1)
            nc.gpsimd.tensor_tensor(bsum, b2r[:, 0], b2r[:, 1], ALU.add).then_inc(bsum_done, 1)
            for i in range(2):
                pool.wait_ge(veps_done, 3 + i)
                nc.gpsimd.tensor_tensor(rstd[:, 1, 4 * i:4 * i + 4], veps[:, 1, 4 * i:4 * i + 4],
                                        mhalf[:, 0:4], ALU.pow).then_inc(rstd_done, 1)
            for n in range(4):
                pool.wait_ge(*is_read(("pr", n)))
                for t in (2 * n, 2 * n + 1):
                    nc.gpsimd.tensor_tensor(x1b[:, t], x1[:, t], f2b[:], ALU.add).then_inc(x1b_done, 1)

        def normalised(eng, key, f, bp, into):
            eng.wait_ge(*is_full(key))
            for piece in "GBR":
                ins = into(win(h1t[:, f], piece, 2 * bp, 2), nat(ps(key)[0:CF, :], piece, 2))
            ins.then_inc(emptied(key), 1)

        def outputs_read(eng, copy, f, bp):
            key = ("oT", f, bp)
            eng.wait_ge(*is_full(key))
            if bp < 2:
                ins = copy(nat(ot[:, f, 512 * bp:512 * bp + 512], "G", 2),
                           ps(key)[0:CF, 0:2 * WIN].rearrange("p (b h w) -> p b h w", b=2, h=WS))
            else:
                copy(nat(ot[:, f], "B", B), ps(key)[0:CF, 0:112].rearrange("p (b h w) -> p b h w", b=B, h=2))
                ins = copy(nat(ot[:, f], "R", B),
                           ps(key)[0:CF, 128:256].rearrange("p (b h w) -> p b h w", b=B, h=H))
            ins.then_inc(emptied(key), 1)

        def fa_places(n):
            return (lambda bank: bank[0:CF, 0:400].rearrange("p (t m) -> p t m", t=2)[:, :, 0:128]
                    .rearrange("p t (m h) -> p t m h", m=16),
                    lambda row: row.rearrange("p (m g) -> p m g", m=16)[:, :, 16 * n:16 * n + 16]
                    .rearrange("p m (t h) -> p t m h", t=2))

        def flipped(copy, n, f):
            src = ps(("fa", n, f))[0:CF, 0:400].rearrange("p (t m) -> p t m", t=2)
            dst = an[:, f].rearrange("p (v g) -> p v g", v=NW)[:, :, 16 * n:16 * n + 16]
            return copy(dst.rearrange("p v (t h) -> p t v h", t=2),
                        src[:, :, 128:200].rearrange("p t (v h) -> p t v h", v=NW))

        def ia_places(n):
            if n < 2:
                return (lambda bank: bank[0:CF, 0:448].rearrange("p (t m g) -> p t m g", t=2, m=16),
                        lambda row: row.rearrange("p (m g) -> p m g", m=16)[:, :, 28 * n:28 * n + 28]
                        .rearrange("p m (t g) -> p t m g", t=2))
            return (lambda bank: bank[0:CF, 0:128].rearrange("p (m g) -> p m g", m=16),
                    lambda row: row.rearrange("p (m g) -> p m g", m=16)[:, :, 56:64])

        def by_parity(key):
            return ps(key)[:, 0:2 * C].rearrange("p (j s k) -> p j s k", j=2, s=2)

        def interleaved(t):
            return t[:, :, 0:C].rearrange("p j (k s) -> p j s k", s=2)

        def ib_read(eng, copy, n):
            key = ("ib", n)
            eng.wait_ge(*is_full(key))
            dst = ibq[:, 2 * n:2 * n + 2]
            copy(interleaved(dst), by_parity(key))
            copy(dst[:, :, C:C + 1], by_parity(key)[:, :, 0, 0:1]).then_inc(emptied(key), 1)

        def k_places(key, f, g, part):
            c0, c1 = GROUPS[g]
            src = ps(key)[0:CF, 0:c1 - c0]
            if g < 2:
                return k2[:, f, part, c0:c1], src
            dst = k2[:, f, part, KB:KB + 2 * (KR - KB)].rearrange("p (g c) -> p g c", g=2)[:, :, 0:128]
            return dst, src.rearrange("p (g c) -> p g c", g=2)

        @block.scalar
        def _(act):
            act.dma_start(ident[:], a["ident"]).then_inc(small_in, 16)
            act.dma_start(ln1[:, :, 0], a["ln1_g"].rearrange("(f p) -> p f", p=CF),
                          allow_slow_non_contiguous=True).then_inc(small_in, 16)
            act.dma_start(ln1[:, :, 1], a["ln1_b"].rearrange("(f p) -> p f", p=CF),
                          allow_slow_non_contiguous=True).then_inc(small_in, 16)
            act.dma_start(relpos[:, 0], a["rel_pos_h"][:, None].to_broadcast([2 * WS - 1, HH, HD])).then_inc(rel_in, 16)
            act.dma_start(relpos[:, 1], a["rel_pos_w"][:, None].to_broadcast([2 * WS - 1, HH, HD])).then_inc(rel_in, 16)
            act.dma_start(mask6[:], a["mask6"]).then_inc(rel_in, 16)
            act.wait_ge(small_in, 48)
            for bp in range(2):
                normalised(act, ("hT", bp, 0), 0, bp, lambda dst, src: nc.scalar.activation(
                    dst, src, ACT.Identity, scale=ln1[:, 0, 0:1], bias=ln1[:, 0, 1:2]))
            act.wait_ge(rows_in, 32)
            nc.scalar.copy(kop[64:128, 0], rows_k).then_inc(rows_set, 1)
            nc.scalar.copy(qop[64:128, 0], rows_q).then_inc(rows_set, 1)
            act.wait_ge(k_scaled, 3)

            def rel_high(f, axis, p):
                key = ("rel", f, axis, p)
                act.wait_ge(*is_full(key))
                for src, dst in rel_pieces(axis, ps(key)[0:84, :], p, relc[:, f, axis, 0]):
                    ins = nc.scalar.copy(dst, src)
                ins.then_inc(r_high, 1)


            def q_high_part(f, g):
                key, (c0, c1), bq = ("q", f, g), GROUPS[g], bqkv[:, f:f + 1]
                act.wait_ge(*is_full(key))
                src = ps(key)[0:CF, 0:c1 - c0]
                if g < 2:
                    nc.scalar.activation(nat(qf[:, f, 512 * g:512 * g + 512], "G", 2),
                                         src.rearrange("p (b h w) -> p b h w", b=2, h=WS), ACT.Identity, bias=bq)
                else:
                    nc.scalar.activation(nat(qf[:, f], "B", B),
                                         src[:, 0:112].rearrange("p (b h w) -> p b h w", b=B, h=2),
                                         ACT.Identity, bias=bq)
                    nc.scalar.activation(nat(qf[:, f], "R", B),
                                         src[:, 128:256].rearrange("p (b h w) -> p b h w", b=B, h=H),
                                         ACT.Identity, bias=bq)
                nc.scalar.activation(q2[:, f, 0, c0:c1], src, ACT.Identity, bias=bq).then_inc(q_high, 1)

            def k_high_part(f, g):
                key = ("k", f, g)
                act.wait_ge(*is_full(key))
                dst, src = k_places(key, f, g, 0)
                nc.scalar.activation(dst, src, ACT.Identity, bias=bk4[:, f:f + 1]).then_inc(k_high, 1)

            for g in range(3):
                q_high_part(0, g)
            for g in range(3):
                k_high_part(0, g)
            for n in range(4):
                rel_high(0, *divmod(n, 2))
            for n in range(NH + 3):
                m = n - 2
                for u in range(6):
                    if (n, u) in Q_STEPS:
                        q_high_part(1, Q_STEPS.index((n, u)))
                    if (n, u) in K_STEPS:
                        k_high_part(1, K_STEPS.index((n, u)))
                    if (n, u) in R_STEPS:
                        rel_high(1, *divmod(R_STEPS.index((n, u)), 2))
                    if (n, u) in W_STEPS:
                        c, x = divmod(W_STEPS.index((n, u)), 2)
                        act.wait_ge(wf1_in, 16 * (c + 1))
                        act.wait_ge(late_in, 15 * 16)
                        cols = slice(MLP // 2 * x, MLP // 2 * (x + 1))
                        nc.scalar.activation(wf1[:, 0, c, cols], wf1_raw[:, c, cols], ACT.Identity,
                                             scale=ln2[:, c, 0:1]).then_inc(wf1_high, 1)
                    if 0 <= m < NH:
                        key = ("E", m, u)
                        act.wait_ge(*is_full(key))
                        src = ps(key)
                        if u < 4:
                            if m >= 1:
                                act.wait_ge(*is_full(("pvg", m - 1)))
                            nc.scalar.activation(pg[:, u], src[0:HWIN, 0:2 * WIN], ACT.Exp).then_inc(emptied(key), 1)
                        else:
                            if m >= 2:
                                act.wait_ge(*is_full(("pvw", m // 2 - 1)))
                            dst, r0, r1 = (pwb, 112, 84) if u == 4 else (pwr, 128, 96)
                            nc.scalar.activation(dst[0:r0, m % 2, 0:128], src[0:r0, 0:128], ACT.Exp)
                            nc.scalar.activation(dst[0:r1, m % 2, 128:384], src[0:r1, 128:384],
                                                 ACT.Exp).then_inc(emptied(key), 1)
                    if u == 0 and 1 <= n <= NH:
                        h = n - 1
                        key = ("mx", h)
                        act.wait_ge(*is_full(key))
                        if h >= 2:
                            act.wait_ge(maxg_loaded[h % 2], 16 * (h // 2))
                            act.wait_ge(maxw_loaded[h % 2], 16 * (h // 2))
                        nc.scalar.copy(maxg[:, h % 2], ps(key)[0:16, 0:HWIN])
                        nc.scalar.copy(maxw[:, h % 2], ps(key)[0:4, 128:256]).then_inc(emptied(key), 1)
                    if u == 1 and 0 <= m - 1 < NH:
                        key = ("pvg", m - 1)
                        act.wait_ge(*is_full(key))
                        nc.scalar.copy(ev[:, m - 1], ps(key)[:, 0:WIN]).then_inc(emptied(key), 1)
            nc.scalar.activation(gelu_warm[:], negmax[:, 0, 0:1], ACT.Gelu)
            for bp in (2, 0, 1):
                outputs_read(act, nc.scalar.copy, 0, bp)
            act.wait_ge(*is_full("w2T"))
            nc.scalar.copy(w2t.rearrange("p x f c -> p (x f c)"), ps("w2T")[0:CF, 0:4 * CF]).then_inc(emptied("w2T"), 1)
            act.wait_ge(late_in, 15 * 16)

            def h2_high_part(bp):
                for f in range(2):
                    key = ("mT", bp, f)
                    act.wait_ge(*is_full(key))
                    nc.scalar.copy(h2t[:, 0, f, 512 * bp:512 * bp + 512], ps(key)[0:CF, :]).then_inc(h2_high, 1)

            h2_high_part(0)
            act.wait_ge(*is_read("f1c"))
            for n in range(2):
                for m in range(6):
                    if (n, m) == (0, 5):
                        h2_high_part(1)
                    key = ("f1", n, m)
                    act.wait_ge(*is_full(key))
                    nc.scalar.activation(gl[:, m, 512 * n:512 * n + 512], ps(key)[:, :], ACT.Gelu,
                                         bias=f1s[:, m:m + 1]).then_inc(emptied(key), 1)
            for n in range(4):
                key = ("fa", n, 1)
                act.wait_ge(*is_full(key))
                src, dst = fa_places(n)
                nc.scalar.copy(dst(half1), src(ps(key)))
                flipped(nc.scalar.copy, n, 1).then_inc(emptied(key), 1)
            for n in range(4):
                key = ("fb", n)
                act.wait_ge(*is_full(key))
                nc.scalar.copy(interleaved(fbp[:, 2 * n:2 * n + 2]), by_parity(key)).then_inc(fb_kept, 1)
            def difference_kept(f, p):
                key, (c0, c1) = ("m1", f, p), ((0, 252), (252, 504), (504, 576))[p]
                act.wait_ge(*is_full(key))
                nc.scalar.copy(od[:, f, c0:c1], ps(key)[0:CF, 256:256 + c1 - c0]).then_inc(od_kept, 1)

            def mixed(f, p):
                c0, c1 = ((0, 252), (252, 504), (504, 576))[p]
                act.wait_ge(*is_read(("m1", f, p)))
                nc.scalar.activation(o1[:, :, f, c0:c1], o1[:, :, f, c0:c1], ACT.Relu).then_inc(o1_done, 1)

            parts = [(f, p) for p in range(3) for f in range(2)]
            difference_kept(*parts[0])
            for part, following in zip(parts, parts[1:] + [None]):
                if following:
                    difference_kept(*following)
                mixed(*part)
            for n in range(3):
                key = ("ia", 1, n)
                act.wait_ge(*is_full(key))
                src, dst = ia_places(n)
                nc.scalar.copy(dst(half1), src(ps(key))).then_inc(emptied(key), 1)
            for n in (0, 2):
                ib_read(act, nc.scalar.copy, n)

        @block.vector
        def _(dve):
            def pair_stats(ln, i, src):
                for t in (2 * i, 2 * i + 1):
                    ins = nc.vector.bn_stats(stats[:, ln, t], src[:, t])
                ins.then_inc(stats_done, 1)

            def mean_and_variance(ln, i):
                dve.wait_ge(stats_done, 4 * ln + 2 * i + 2)
                for t in range(4 * i, 4 * i + 4):
                    ins = nc.vector.bn_aggr(mv[:, ln, t], stats[:, ln, t])
                ins.then_inc(mean_done, 1)
                dve.wait_ge(mean_done, 2 * ln + i + 1)
                nc.vector.tensor_scalar(veps[:, ln, 4 * i:4 * i + 4], mv[:, ln, 4 * i:4 * i + 4, 1], EPS, None,
                                        ALU.add).then_inc(veps_done, 1)

            nc.vector.memset(vaug[:, :, :, HD:2 * HD], 1.0).then_inc(ones_set, 1)
            for i in range(4):
                dve.wait_ge(x_in[i], 16)
                pair_stats(0, i, xt)
                if i % 2:
                    mean_and_variance(0, i // 2)
            for i in range(2):
                dve.wait_ge(rstd_done, i + 1)
                for t in range(4 * i, 4 * i + 4):
                    ins = nc.vector.tensor_scalar(xn[:, t], xt[:, t], mv[:, 0, t, 0:1], rstd[:, 0, t:t + 1],
                                                  ALU.subtract, ALU.mult)
                ins.then_inc(xn_done, 1)
            dve.wait_ge(wqkv_in, 16)
            dve.wait_ge(bqkv_in, 16)
            nc.vector.tensor_scalar(bk4[:], bqkv[:, 2:4], HD ** -0.5, None, ALU.mult).then_inc(k_scaled, 1)
            for f in range(2):
                nc.vector.tensor_scalar(wqkv[:, f, C:2 * C], wqkv[:, f, C:2 * C], HD ** -0.5, None,
                                        ALU.mult).then_inc(k_scaled, 1)
            dve.wait_ge(small_in, 48)
            for bp in range(2):
                normalised(dve, ("hT", bp, 1), 1, bp, lambda dst, src: nc.vector.tensor_scalar(
                    dst, src, ln1[:, 1, 0:1], ln1[:, 1, 1:2], ALU.mult, ALU.add))
            dve.wait_ge(rel_in, 48)
            for ax in range(2):
                key = ("relp", ax)
                dve.wait_ge(*is_full(key))
                src = ps(key)[0:CF, :]
                src = bass.AP(tensor=src.tensor, offset=src.offset + WS - 1,
                              ap=[list(src.ap[0]), [1, WS], [0, HH], [-1, WS]])
                nc.vector.tensor_tensor(relw[:, ax].rearrange("p r (j k) -> p r j k", j=HH), src,
                                        mask6[:, None, :, None].to_broadcast([CF, WS, HH, WS]),
                                        ALU.mult).then_inc(emptied(key), 1)
            dve.wait_ge(k_scaled, 3)

            def rel_low(f, axis, p):
                key = ("rel", f, axis, p)
                dve.wait_ge(r_high, 4 * f + 2 * axis + p + 1)
                part = ps(key)[0:84, :]
                for (src, low), (_, high) in zip(rel_pieces(axis, part, p, relc[:, f, axis, 1]),
                                                 rel_pieces(axis, part, p, relc[:, f, axis, 0])):
                    ins = nc.vector.tensor_tensor(low, src, high.bitcast(F32), ALU.subtract)
                ins.then_inc(emptied(key), 1)


            def q_low(f, g):
                key, (c0, c1) = ("q", f, g), GROUPS[g]
                dve.wait_ge(q_high, 3 * f + g + 1)
                nc.vector.scalar_tensor_tensor(q2[:, f, 1, c0:c1], ps(key)[0:CF, 0:c1 - c0], bqkv[:, f:f + 1],
                                               q2[:, f, 0, c0:c1].bitcast(F32), ALU.add,
                                               ALU.subtract).then_inc(emptied(key), 1)

            def k_low(f, g):
                key = ("k", f, g)
                dve.wait_ge(k_high, 3 * f + g + 1)
                dst, src = k_places(key, f, g, 1)
                high, _ = k_places(key, f, g, 0)
                nc.vector.scalar_tensor_tensor(dst, src, bk4[:, f:f + 1], high.bitcast(F32), ALU.add,
                                               ALU.subtract).then_inc(emptied(key), 1)

            for g in range(3):
                q_low(0, g)
            for g in range(3):
                k_low(0, g)
            for n in range(4):
                rel_low(0, *divmod(n, 2))
            dve.wait_ge(bv_in, 16)
            nc.vector.tensor_copy(vaug[0:96, 10, :, 0:HD],
                                  bv[0:96].rearrange("p (h d) -> p h d", h=NH)).then_inc(v_padded, 1)

            def values(n):
                key = ("v", n)
                dve.wait_ge(*is_full(key))
                rows, tiles = (HWIN, 2) if n < 4 else ((112, 1), (128, 1))[n - 4]
                t = 2 * n if n < 4 else 4 + n
                nc.vector.tensor_tensor(
                    vaug[0:rows, t:t + tiles, :, 0:HD],
                    ps(key)[0:rows, 0:tiles * C].rearrange("p (t h d) -> p t h d", t=tiles, h=NH),
                    bv[0:rows, None].to_broadcast([rows, tiles, C]).rearrange("p t (h d) -> p t h d", h=NH),
                    ALU.add).then_inc(emptied(key), 1)

            recips = [0]

            def over_sums(key, src, rd, dst):
                dve.wait_ge(*is_full(key))
                nc.vector.reciprocal(rd, src[:, :, :, HD]).then_inc(rden_done, 1)
                recips[0] += 1
                dve.wait_ge(rden_done, recips[0])
                nc.vector.tensor_tensor(dst, src[:, :, :, 0:HD], rd[:, :, :, None].to_broadcast(list(dst.shape)),
                                        ALU.mult).then_inc(emptied(key), 1)

            def tokens_g(u, n):
                key = ("eT", u, n)
                over_sums(key, ps(key)[0:HWIN, :].rearrange("p (h b d) -> p h b d", h=4, b=B),
                          rden[:, u, 4 * n:4 * n + 4],
                          on[:, u].rearrange("p b (h d) -> p h b d", h=NH)[:, 4 * n:4 * n + 4])

            def tokens_w(n):
                key, hs = ("wT", n), (8, 4)[n]
                over_sums(key, ps(key)[:, 0:64 * hs].rearrange("p (h g d) -> p h g d", h=hs, g=2),
                          rdenw[:, 8 * n:8 * n + hs],
                          onw.rearrange("p g (h d) -> p h g d", h=NH)[:, 8 * n:8 * n + hs])

            def second_half(n, u):
                if (n, u) in Q_STEPS:
                    q_low(1, Q_STEPS.index((n, u)))
                if (n, u) in K_STEPS:
                    k_low(1, K_STEPS.index((n, u)))
                if (n, u) in R_STEPS:
                    rel_low(1, *divmod(R_STEPS.index((n, u)), 2))

            dve.wait_ge(set_up, 5)
            for n in range(6):
                values(n)
            for n in range(NH + 3):
                for u in range(6):
                    if n < NH:
                        key = ("S", n, u)
                        dve.wait_ge(*is_full(key))
                        if u == 0 and n >= 2:
                            dve.wait_ge(max_split, n - 1)
                        rows, cols, width, at = (HWIN, 2, WIN, 2 * u) if u < 4 else (
                            (128, 1, KR - KB, 8), (128, 1, KN - KR, 9))[u - 4]
                        nc.vector.tensor_reduce(negmax[0:rows, n % 2, at:at + cols],
                                                ps(key)[0:rows, 0:cols * width].rearrange("p (t k) -> p t k", t=cols),
                                                AX.X, ALU.max, negate=True).then_inc(emptied(key), 1)
                    if u > 0:
                        second_half(n, u - 1)
                    if u == 3 and 4 <= n <= NH + 2 and n % 2 == 0:
                        i = (n - 4) // 2
                        key = ("pvw", i)
                        dve.wait_ge(*is_full(key))
                        nc.vector.tensor_copy(evw[:, i], ps(key)[:, 0:128]).then_inc(emptied(key), 1)
                    if n in (NH, NH + 1) and u in (2, 4):
                        tokens_g(u // 2 - 1, n - NH)
                    if n == NH + 1 and u == 5:
                        tokens_w(0)
                if n < NH:
                    dve.wait_ge(*is_read(("S", n, 4)))
                    dve.wait_ge(*is_read(("S", n, 5)))
                    if n >= 2:
                        dve.wait_ge(*is_full(("mx", n - 2)))
                    whole, parts = negmax[:, n % 2], negmax2[:, n % 2]
                    nc.vector.tensor_copy(parts[:, 0:8].bitcast(F32R), whole[:, 0:8])
                    nc.vector.tensor_copy(parts[:, 16:18].bitcast(F32R), whole[:, 8:10]).then_inc(max_high, 1)
                    dve.wait_ge(max_high, n + 1)
                    nc.vector.tensor_tensor(parts[:, 8:16], whole[:, 0:8], parts[:, 0:8], ALU.subtract)
                    nc.vector.tensor_tensor(parts[:, 18:20], whole[:, 8:10], parts[:, 16:18],
                                            ALU.subtract).then_inc(max_split, 1)
                second_half(n, 5)
            dve.wait_ge(*is_full("f1c"))
            nc.vector.tensor_tensor(f1s[:], ps("f1c")[:, 0:6], f1b[:], ALU.add).then_inc(emptied("f1c"), 1)
            tokens_w(1)
            for u in range(2):
                tokens_g(u, 2)
            for bp in (2, 0, 1):
                outputs_read(dve, nc.vector.tensor_copy, 1, bp)
            dve.wait_ge(xpb_done, NT)

            def residual(n):
                key = ("pr", n)
                dve.wait_ge(*is_full(key))
                nc.vector.tensor_tensor(x1[:, 2 * n:2 * n + 2], ps(key)[:, 0:2 * C].rearrange("p (t c) -> p t c", t=2),
                                        xt[:, 2 * n:2 * n + 2], ALU.add).then_inc(emptied(key), 1)

            def x1_normalised(i):
                dve.wait_ge(rstd_done, 3 + i)
                for t in range(4 * i, 4 * i + 4):
                    ins = nc.vector.tensor_scalar(x1n[:, t], x1[:, t], mv[:, 1, t, 0:1], rstd[:, 1, t:t + 1],
                                                  ALU.subtract, ALU.mult)
                ins.then_inc(x1n_done, 1)

            def h2_low_part(bp):
                for f in range(2):
                    key = ("mT", bp, f)
                    dve.wait_ge(h2_high, 2 * bp + f + 1)
                    nc.vector.tensor_tensor(h2t[:, 1, f, 512 * bp:512 * bp + 512], ps(key)[0:CF, :],
                                            h2t[:, 0, f, 512 * bp:512 * bp + 512].bitcast(F32),
                                            ALU.subtract).then_inc(emptied(key), 1)

            for n in range(2):
                residual(n)
                dve.wait_ge(*is_read(("pr", n)))
                pair_stats(1, n, x1)
            mean_and_variance(1, 0)
            residual(2)
            x1_normalised(0)
            residual(3)
            dve.wait_ge(late_in, 15 * 16)
            h2_low_part(0)
            dve.wait_ge(*is_full("w2p"))
            dve.wait_ge(wps_done, 1)
            nc.vector.tensor_tensor(wab[:, 0], ps("w2p")[0:CF, 0:2 * CF].rearrange("p (f c) -> p f c", f=2),
                                    wbd[:, 1, 0], ALU.add)
            nc.vector.tensor_tensor(wab[:, 1], ps("w2p")[0:CF, 2 * CF:4 * CF].rearrange("p (f c) -> p f c", f=2),
                                    wps[:], ALU.add).then_inc(emptied("w2p"), 1)
            dve.wait_ge(*is_full("b2w"))
            dve.wait_ge(bsum_done, 1)
            nc.vector.tensor_tensor(bs, ps("b2w")[:, 0:C], bsum, ALU.add).then_inc(emptied("b2w"), 1)
            for n in range(2, 4):
                dve.wait_ge(*is_read(("pr", n)))
                pair_stats(1, n, x1)
            mean_and_variance(1, 1)
            x1_normalised(1)
            h2_low_part(1)
            dve.wait_ge(x1b_done, NT)
            for n in range(4):
                key = ("f2", n)
                dve.wait_ge(*is_full(key))
                nc.vector.tensor_tensor(y[:, 2 * n:2 * n + 2], ps(key)[:, 0:2 * C].rearrange("p (t c) -> p t c", t=2),
                                        x1b[:, 2 * n:2 * n + 2], ALU.add).then_inc(emptied(key), 1)
            def halves_summed(key, other, places, to):
                dve.wait_ge(*is_full(key))
                dve.wait_ge(*is_read(other))
                src, dst = places
                nc.vector.tensor_tensor(dst(to[:, 0]), src(ps(key)), dst(half1), ALU.add).then_inc(summed, 1)

            def halves_subtracted(key, places, to):
                src, dst = places
                return nc.vector.tensor_tensor(dst(to[:, 1]), src(ps(key)), dst(half1), ALU.subtract)

            for n in range(4):
                key = ("fa", n, 0)
                halves_summed(key, ("fa", n, 1), fa_places(n), ya)
                halves_subtracted(key, fa_places(n), ya).then_inc(subtracted, 1)
                flipped(nc.vector.tensor_copy, n, 0).then_inc(emptied(key), 1)
            for n in range(4):
                key = ("fb", n)
                dve.wait_ge(fb_kept, n + 1)
                src, dst = by_parity(key), interleaved(fbf[:, 2 * n:2 * n + 2])
                nc.vector.tensor_copy(dst[:, :, 0, 0:1], src[:, :, 0, 0:1])
                nc.vector.tensor_copy(dst[:, :, 0, 1:CF], src[:, :, 0, CF - 1:0:-1])
                nc.vector.tensor_copy(dst[:, :, 1], src[:, :, 1, ::-1]).then_inc(emptied(key), 1)
            for f in range(2):
                for p, (c0, c1) in enumerate(((0, 512), (512, 576))):
                    key = ("fc", f, p)
                    dve.wait_ge(*is_full(key))
                    nc.vector.tensor_tensor(dks[:, f, c0:c1], ps(key)[0:CF, 0:c1 - c0], an[:, f, c0:c1], ALU.add)
                    nc.vector.tensor_tensor(dkd[:, f, c0:c1], ps(key)[0:CF, 0:c1 - c0], an[:, f, c0:c1],
                                            ALU.subtract).then_inc(emptied(key), 1)
            for p in range(3):
                for f in range(2):
                    key, (c0, c1) = ("m1", f, p), ((0, 252), (252, 504), (504, 576))[p]
                    dve.wait_ge(od_kept, 2 * p + f + 1)
                    for x, op in enumerate((ALU.add, ALU.subtract)):
                        ins = nc.vector.scalar_tensor_tensor(o1[:, x, f, c0:c1], ps(key)[0:CF, 0:c1 - c0],
                                                             b1c[:, x, f:f + 1], od[:, f, c0:c1], ALU.add, op)
                    ins.then_inc(emptied(key), 1)
            for n in range(3):
                key = ("m2", n)
                dve.wait_ge(*is_full(key))
                rows, tiles = (126, 2) if n < 2 else (72, 1)
                t = slice(2 * n, 2 * n + tiles)
                nc.vector.tensor_tensor(sm[0:rows, t], ps(key)[0:rows, 0:tiles * C].rearrange("p (t c) -> p t c", t=tiles),
                                        bs[0:rows, None].to_broadcast([rows, tiles, C]), ALU.add).then_inc(emptied(key), 1)
                dve.wait_ge(*is_read(key))
                nc.vector.tensor_scalar(sc[0:rows, t], sm[0:rows, t], -SHRINK, SHRINK, ALU.max,
                                        ALU.min).then_inc(clipped, 1)
                dve.wait_ge(clipped, n + 1)
                nc.vector.tensor_tensor(ss[0:rows, t], sm[0:rows, t], sc[0:rows, t], ALU.subtract).then_inc(shrunk, 1)
            for n in range(3):
                halves_summed(("ia", 0, n), ("ia", 1, n), ia_places(n), iv)
                if n != 1:
                    for i in range(max(n - 1, 0), n + 1):
                        halves_subtracted(("ia", 0, i), ia_places(i), iv).then_inc(emptied(("ia", 0, i)), 1)
            for n in (1, 3):
                ib_read(dve, nc.vector.tensor_copy, n)
            dve.wait_ge(y2_in, 3 * 16)
            for n in range(4):
                key = ("ic", n)
                dve.wait_ge(*is_full(key))
                nc.vector.scalar_tensor_tensor(res[:, 2 * n:2 * n + 2],
                                               ps(key)[:, 0:2 * C].rearrange("p (t c) -> p t c", t=2),
                                               1.0 / (B * H * W * C), y2[:, 2 * n:2 * n + 2], ALU.mult,
                                               ALU.add).then_inc(emptied(key), 1)

        @block.tensor
        def _(pe):
            mm = nc.tensor.matmul
            pe.wait_ge(small_in, 48)
            for bp in range(2):
                pe.wait_ge(xn_done, bp + 1)
                for f in range(2):
                    key = ("hT", bp, f)
                    for t in range(4):
                        ins = nc.tensor.transpose(ps(key)[0:CF, 128 * t:128 * t + 128],
                                                  xn[:, 4 * bp + t, CF * f:CF * f + CF], ident[:])
                    ins.then_inc(filled(key), 1)
            pe.wait_ge(rel_in, 48)
            for ax in range(2):
                key = ("relp", ax)
                mm(ps(key)[0:CF, 0:2 * WS - 1], relpos[:, ax].rearrange("p j d -> p (j d)"),
                   ident[0:2 * WS - 1, 0:2 * WS - 1], start=True, stop=True).then_inc(filled(key), 1)
            pe.wait_ge(wqkv_in, 16)
            pe.wait_ge(set_up, 2)

            def rel(f, axis, p):
                pe.wait_ge(q_high, 3 * (f + 1))
                pe.wait_ge(*is_read(("relp", axis)))
                qb = qf[:, f].rearrange("p (b h w) -> p b h w", b=B, h=H)
                key = ("rel", f, axis, p)
                pe.wait_ge(*is_free(key))
                for i in range(8):
                    r = 8 * p + i
                    rhs = qb[:, :, r, :] if axis == 0 else qb[:, :, :, r]
                    ins = mm(ps(key)[0:84, 64 * i:64 * i + 64], relw[:, axis, r % WS], rhs, start=True, stop=True)
                ins.then_inc(filled(key), 1)

            def values(n):
                key = ("v", n)
                pe.wait_ge(*is_free(key))
                spans = [(HWIN * (2 * n + t), HWIN) for t in range(2)] if n < 4 else [((QB, 112), (QR, 128))[n - 4]]
                for t, (c0, rows) in enumerate(spans):
                    for c in range(2):
                        ins = mm(ps(key)[0:rows, C * t:C * t + C], h1t[:, c, c0:c0 + rows], wqkv[:, c, 2 * C:3 * C],
                                 start=c == 0, stop=c == 1)
                ins.then_inc(filled(key), 1)

            def product(name, f, g):
                key, (c0, c1), x = (name, f, g), GROUPS[g], "qk".index(name)
                pe.wait_ge(*is_free(key))
                if name == "k":
                    pe.wait_ge(k_scaled, 3)
                for c in range(2):
                    pe.wait_ge(*is_read(("hT", min(g, 1), c)))
                for c in range(2):
                    ins = mm(ps(key)[0:CF, 0:c1 - c0], wqkv[:, c, C * x + CF * f:C * x + CF * f + CF],
                             h1t[:, c, c0:c1], start=c == 0, stop=c == 1)
                ins.then_inc(filled(key), 1)

            for name in "qk":
                for g in range(3):
                    product(name, 0, g)
            for n in range(4):
                rel(0, *divmod(n, 2))
            for n in range(6):
                values(n)

            def bias_through_fc1(m):
                if m == 0:
                    pe.wait_ge(wf1_in, 32)
                    pe.wait_ge(late_in, 15 * 16)
                    pe.wait_ge(*is_free("f1c"))
                for c in range(2):
                    ins = mm(ps("f1c")[:, m:m + 1], wf1_raw[:, c, 128 * m:128 * m + 128], ln2[:, c, 1:2],
                             start=c == 0, stop=c == 1)
                if m == 5:
                    ins.then_inc(filled("f1c"), 1)

            def maxima(h):
                o = h % NOP
                for u in range(6):
                    key = ("S", h, u)
                    if u == 0:
                        pe.wait_ge(q_loaded[o], 32 * (h // NOP + 1))
                        pe.wait_ge(r_loaded[o], 32 * (h // NOP + 1))
                        pe.wait_ge(k_loaded[h % NOK], 32 * (h // NOK + 1))
                    pe.wait_ge(*is_free(key))
                    if u < 4:
                        for t in range(2):
                            c0 = WIN * u + HWIN * t
                            ins = mm(ps(key)[0:HWIN, WIN * t:WIN * t + WIN], qop[0:126, o, c0:c0 + HWIN],
                                     kop[0:126, h % NOK, WIN * u:WIN * u + WIN], start=True, stop=True)
                    else:
                        q0, k0, k1 = ((QB, KB, KR), (QR, KR, KN))[u - 4]
                        ins = mm(ps(key)[:, 0:k1 - k0], qop[0:126, o, q0:q0 + 128], kop[0:126, h % NOK, k0:k1],
                                 start=True, stop=True)
                    ins.then_inc(filled(key), 1)
                    yield

            def shifted(h):
                o = h % NOP
                for u in range(6):
                    key = ("E", h, u)
                    if u == 0:
                        pe.wait_ge(maxg_loaded[h % 2], 16 * (h // 2 + 1))
                    if u == 4:
                        pe.wait_ge(maxw_loaded[h % 2], 16 * (h // 2 + 1))
                    pe.wait_ge(*is_free(key))
                    if u < 4:
                        chunks = [(WIN * u + HWIN * c, HWIN, WIN * c) for c in range(2)]
                        rhs = qop[:, o, WIN * u:WIN * u + WIN]
                    elif u == 4:
                        chunks = [(KB, 112, 0), (KPB, 84, 128), (KPB + 84, 84, 256)]
                        rhs = qop[:, o, QB:QB + 128]
                    else:
                        chunks = [(KR, 128, 0), (KPR, 96, 128), (KPR + 96, 96, 256)]
                        rhs = qop[:, o, QR:QR + 128]
                    n = rhs.shape[1]
                    for c0, rows, at in chunks:
                        ins = mm(ps(key)[0:rows, at:at + n], kop[:, h % NOK, c0:c0 + rows], rhs, start=True, stop=True)
                    ins.then_inc(filled(key), 1)
                    yield

            def values_g(h, c):
                key = ("pvg", h)
                if c == 0:
                    if h == 0:
                        pe.wait_ge(*is_read(("v", 5)))
                        pe.wait_ge(ones_set, 1)
                    pe.wait_ge(*is_free(key))
                    pe.wait_ge(*is_read(("E", h, 2)))
                    pe.wait_ge(*is_read(("E", h, 3)))
                for b in range(B):
                    ins = mm(ps(key)[32 * b:32 * b + 32, 0:WIN], vaug[0:HWIN, 2 * b + c, h],
                             pg[:, b, WIN * c:WIN * c + WIN], start=c == 0, stop=c == 1)
                if c == 1:
                    ins.then_inc(filled(key), 1)

            def values_w(i):
                key = ("pvw", i)
                pe.wait_ge(*is_free(key))
                pe.wait_ge(*is_read(("E", 2 * i + 1, 4)))
                pe.wait_ge(*is_read(("E", 2 * i + 1, 5)))
                for c in range(3):
                    for e in range(2):
                        for g, (src, own, pad) in enumerate(((pwb, 112, 84), (pwr, 128, 96))):
                            rows, tile = (own, 8 + g) if c == 0 else (pad, 10)
                            q0 = 32 * (2 * e + g)
                            ins = mm(ps(key)[q0:q0 + 32, 0:128], vaug[0:rows, tile, 2 * i + e],
                                     src[0:rows, e, 128 * c:128 * c + 128], start=c == 0, stop=c == 2)
                ins.then_inc(filled(key), 1)

            def max_rows(h):
                key = ("mx", h)
                pe.wait_ge(*is_free(key))
                pe.wait_ge(max_split, h + 1)
                nc.tensor.transpose(ps(key)[0:16, 0:HWIN], negmax2[0:HWIN, h % 2, 0:16], ident[0:HWIN, 0:HWIN])
                nc.tensor.transpose(ps(key)[0:4, 128:256], negmax2[:, h % 2, 16:20], ident[:]).then_inc(filled(key), 1)

            def tokens_g(u, n):
                key = ("eT", u, n)
                pe.wait_ge(*is_free(key))
                pe.wait_ge(*is_read(("pvg", 4 * n + 3)))
                for i in range(4):
                    ins = nc.tensor.transpose(ps(key)[0:HWIN, 128 * i:128 * i + 128],
                                              ev[:, 4 * n + i, HWIN * u:HWIN * u + HWIN], ident[:])
                ins.then_inc(filled(key), 1)

            def tokens_w(n):
                key, pairs = ("wT", n), (range(0, 4), range(4, 6))[n]
                pe.wait_ge(*is_free(key))
                pe.wait_ge(*is_read(("pvw", pairs[-1])))
                for i, p in enumerate(pairs):
                    ins = nc.tensor.transpose(ps(key)[:, 128 * i:128 * i + 128], evw[:, p], ident[:])
                ins.then_inc(filled(key), 1)

            pe.wait_ge(v_padded, 1)
            pe.wait_ge(rows_set, 2)
            pe.wait_ge(rows_copied, 16 * (NOP + NOK - 2))
            for n in range(NH + 3):
                m = n - 2
                first = maxima(n) if n < NH else None
                second = shifted(m) if 0 <= m < NH else None
                for u in range(6):
                    if first:
                        next(first)
                    if (n, u) in Q_STEPS:
                        product("q", 1, Q_STEPS.index((n, u)))
                    if (n, u) in K_STEPS:
                        product("k", 1, K_STEPS.index((n, u)))
                    if (n, u) in R_STEPS:
                        rel(1, *divmod(R_STEPS.index((n, u)), 2))
                    if (n, u) in B_STEPS:
                        bias_through_fc1(B_STEPS.index((n, u)))
                    if second:
                        next(second)
                    if u == 0 and second and m >= 1:
                        values_g(m - 1, 1)
                    if u == 0 and 1 <= n <= NH:
                        max_rows(n - 1)
                    if u == 3 and m >= 2 and m % 2 == 0:
                        values_w(m // 2 - 1)
                    if u == 5 and second:
                        values_g(m, 0)
                    if n in (NH, NH + 1) and u in (2, 4):
                        tokens_g(u // 2 - 1, n - NH)
                    if n == NH + 1 and u == 5:
                        tokens_w(0)
                if m == NH - 1:
                    values_g(m, 1)
            bias_through_fc1(5)
            tokens_w(1)
            for u in range(2):
                tokens_g(u, 2)

            for bp in (2, 0, 1):
                for f in range(2):
                    key = ("oT", f, bp)
                    pe.wait_ge(*is_free(key))
                    for k in (("eT", 0, 2), ("eT", 1, 2)) if bp < 2 else (("wT", 0), ("wT", 1)):
                        pe.wait_ge(*is_read(k))
                    for i in range(4 if bp < 2 else 2):
                        if bp < 2:
                            b, u = 2 * bp + i // 2, i % 2
                            ins = nc.tensor.transpose(ps(key)[0:CF, HWIN * i:HWIN * i + HWIN],
                                                      on[:, u, b, CF * f:CF * f + CF], ident[0:HWIN, 0:HWIN])
                        else:
                            ins = nc.tensor.transpose(ps(key)[0:CF, 128 * i:128 * i + 128],
                                                      onw[:, i, CF * f:CF * f + CF], ident[:])
                    ins.then_inc(filled(key), 1)
            pe.wait_ge(late_in, 15 * 16)
            pe.wait_ge(weights_in, 32)
            for n in range(4):
                key = ("pr", n)
                pe.wait_ge(*is_free(key))
                for f in range(2):
                    pe.wait_ge(*is_read(("oT", f, 2)))
                    pe.wait_ge(*is_read(("oT", f, n // 2)))
                for t in range(2):
                    for c in range(2):
                        ins = mm(ps(key)[:, C * t:C * t + C], ot[:, c, 128 * (2 * n + t):128 * (2 * n + t) + 128],
                                 wproj[:, c], start=c == 0, stop=c == 1)
                ins.then_inc(filled(key), 1)
            pe.wait_ge(wbd_done, 4)
            pe.wait_ge(*is_free("w2T"))
            for i in range(4):
                ins = nc.tensor.transpose(ps("w2T")[0:CF, CF * i:CF * i + CF], wbd[:, 1, i // 2, i % 2],
                                          ident[0:CF, 0:CF])
            ins.then_inc(filled("w2T"), 1)
            pe.wait_ge(*is_free("b2w"))
            for f in range(2):
                ins = mm(ps("b2w")[:, CF * f:CF * f + CF], b20c[:, f:f + 1].to_broadcast([CF, 128]), wbd[:, 1, 1, f],
                         start=True, stop=True)
            ins.then_inc(filled("b2w"), 1)
            pe.wait_ge(*is_free("w2p"))
            pe.wait_ge(*is_read("w2T"))
            for i in range(4):
                ins = mm(ps("w2p")[0:CF, CF * i:CF * i + CF], w2t[:, i // 2, i % 2], wbd[:, 1, 1, i % 2],
                         start=True, stop=True)
            ins.then_inc(filled("w2p"), 1)

            def normalised_t(bp):
                pe.wait_ge(x1n_done, bp + 1)
                for f in range(2):
                    key = ("mT", bp, f)
                    pe.wait_ge(*is_free(key))
                    for t in range(4):
                        ins = nc.tensor.transpose(ps(key)[0:CF, 128 * t:128 * t + 128],
                                                  x1n[:, 4 * bp + t, CF * f:CF * f + CF], ident[:])
                    ins.then_inc(filled(key), 1)

            def hidden(n, ms):
                for m in ms:
                    key = ("f1", n, m)
                    pe.wait_ge(*is_free(key))
                    for i, (x, w, c) in enumerate(((0, 0, 0), (0, 1, 0), (0, 0, 1), (0, 1, 1), (1, 0, 0), (1, 0, 1))):
                        if x == 0:
                            pe.wait_ge(h2_high, 2 * n + c + 1)
                        else:
                            pe.wait_ge(*is_read(("mT", n, c)))
                        ins = mm(ps(key)[:, :], wf1[:, w, c, 128 * m:128 * m + 128],
                                 h2t[:, x, c, 512 * n:512 * n + 512], start=i == 0, stop=i == 5)
                    ins.then_inc(filled(key), 1)

            pe.wait_ge(wf1_split, 2)
            normalised_t(0)
            hidden(0, range(0, 5))
            normalised_t(1)
            hidden(0, range(5, 6))
            hidden(1, range(0, 6))
            for n in range(4):
                key = ("f2", n)
                pe.wait_ge(*is_free(key))
                for m in range(6):
                    pe.wait_ge(*is_read(("f1", n // 2, m)))
                for t in range(2):
                    for m in range(6):
                        ins = mm(ps(key)[:, C * t:C * t + C], gl[:, m, 128 * (2 * n + t):128 * (2 * n + t) + 128],
                                 wf2[:, m], start=m == 0, stop=m == 5)
                ins.then_inc(filled(key), 1)
            pe.wait_ge(tables_in, 6 * 16)
            for n in range(4):
                pe.wait_ge(*is_read(("f2", n)))
                for f in (1, 0):
                    key = ("fa", n, f)
                    pe.wait_ge(*is_free(key))
                    for t in range(2):
                        ins = mm(ps(key)[0:CF, 200 * t:200 * t + 200], y[:, 2 * n + t, CF * f:CF * f + CF], fw,
                                 start=True, stop=True)
                    ins.then_inc(filled(key), 1)
            def over_channels(key, n, s, src):
                if s == 0:
                    pe.wait_ge(*is_free(key))
                for t in range(2):
                    j, at = 2 * n + t, C * t + CF * s
                    ins = mm(ps(key)[:, at:at + CF], src[:, s, 128 * j:128 * j + 128], cas[:, s],
                             start=True, stop=True)
                if s == 1:
                    ins.then_inc(filled(key), 1)

            in_turn = [(0, 0), (1, 0), (0, 1), (1, 1), (2, 0), (2, 1), (3, 0), (3, 1)]
            pe.wait_ge(summed, 4)
            for n, s in in_turn:
                if (n, s) == (0, 1):
                    pe.wait_ge(subtracted, 4)
                over_channels(("fb", n), n, s, ya)
            for f in range(2):
                for p, js in enumerate((range(0, 7), range(7, 8))):
                    key = ("fc", f, p)
                    pe.wait_ge(*is_free(key))
                    for j in js:
                        pe.wait_ge(*is_read(("fb", j // 2)))
                        n, c0 = (128, 0) if j == 0 else (64, (64 * (j + 1)) % 512)
                        at = 0 if j == 0 else 256
                        mm(ps(key)[0:CF, c0:c0 + n], fbp[:, j, CF * f:CF * f + CF], fg[:, at:at + n],
                           start=True, stop=False)
                        ins = mm(ps(key)[0:CF, c0:c0 + n], fbf[:, j, CF * f:CF * f + CF], fg[:, at + n:at + 2 * n],
                                 start=False, stop=True)
                    ins.then_inc(filled(key), 1)
            for p in range(3):
                for f in range(2):
                    for i in range(2):
                        pe.wait_ge(*is_read(("fc", f, i)))
                    key = ("m1", f, p)
                    pe.wait_ge(*is_free(key))
                    for x, t in enumerate((dks, dkd)):
                        v = t[:, f].rearrange("p (v g) -> p v g", v=NW)
                        if p < 2:
                            v, n = v[:, :, 28 * p:28 * p + 28].rearrange("p v (t g) -> p t v g", t=2), 252
                        else:
                            v, n = v[:, :, 56:64], 72
                        ins = mm(ps(key)[0:CF, 256 * x:256 * x + n], wbd[:, 0, x, f], v, start=True, stop=True)
                    ins.then_inc(filled(key), 1)
            pe.wait_ge(*is_read("w2p"))
            for n in range(3):
                key = ("m2", n)
                pe.wait_ge(*is_free(key))
                pe.wait_ge(o1_done, 2 * (n + 1))
                for t in range(2 if n < 2 else 1):
                    g0, g1 = 14 * (2 * n + t), min(14 * (2 * n + t) + 14, 64)
                    rows = NW * (g1 - g0)
                    for f in range(2):
                        for x in range(2):
                            lhs = o1[:, x, f, NW * g0:NW * g1]
                            ins = mm(ps(key)[0:rows, C * t + CF * f:C * t + CF * f + CF], lhs, wab[:, x, f],
                                     start=x == 0, stop=x == 1)
                ins.then_inc(filled(key), 1)
            for n in range(3):
                pe.wait_ge(shrunk, n + 1)
                for f in (1, 0):
                    key = ("ia", f, n)
                    pe.wait_ge(*is_free(key))
                    for t in range(2 if n < 2 else 1):
                        rows, tab = (126, iw14) if n < 2 else (72, iw8)
                        w = tab.shape[1]
                        ins = mm(ps(key)[0:CF, w * t:w * t + w], ss[0:rows, 2 * n + t, CF * f:CF * f + CF], tab,
                                 start=True, stop=True)
                    ins.then_inc(filled(key), 1)
            pe.wait_ge(summed, 7)
            for n, s in in_turn:
                if (n, s) == (0, 1):
                    for i in range(3):
                        pe.wait_ge(*is_read(("ia", 0, i)))
                over_channels(("ib", n), n, s, iv)
            for n in range(4):
                key = ("ic", n)
                pe.wait_ge(*is_free(key))
                pe.wait_ge(*is_read(("ib", n)))
                for t in range(2):
                    j = 2 * n + t
                    at = 0 if j == 0 else 256
                    mm(ps(key)[:, C * t:C * t + C], ig[:, at:at + 128], ibq[:, j, 0:C], start=True, stop=False)
                    ins = mm(ps(key)[:, C * t:C * t + C], ig[:, at + 128:at + 256], ibq[:, j, C:0:-1],
                             start=False, stop=True)
                ins.then_inc(filled(key), 1)


_INS = {"x": "x", "L0_conv_ln1_g": "ln1_g", "L0_conv_ln1_b": "ln1_b", "L0_conv_qkv_w": "qkv_w",
        "L0_conv_qkv_b": "qkv_b", "L0_conv_proj_w": "proj_w", "L0_conv_proj_b": "proj_b",
        "L0_conv_rel_pos_h": "rel_pos_h", "L0_conv_rel_pos_w": "rel_pos_w", "L0_conv_ln2_g": "ln2_g",
        "L0_conv_ln2_b": "ln2_b", "L0_conv_fc1_w": "fc1_w", "L0_conv_fc1_b": "fc1_b", "L0_conv_fc2_w": "fc2_w",
        "L0_conv_fc2_b": "fc2_b", "L1_conv_w1": "w1", "L1_conv_b1": "b1", "L1_conv_w2": "w2", "L1_conv_b2": "b2"}


def kernel(**inputs):
    import concourse.bacc as bacc
    from concourse.bass_utils import run_bass_kernel_spmd

    nc = bacc.Bacc("TRN2", target_bir_lowering=False, num_devices=1)
    arrays, aps = {}, {}
    given = {short: np.ascontiguousarray(inputs[name]) for name, short in _INS.items()}
    for name, v in {**given, **tables()}.items():
        arrays[f"in_{name}"] = v
        aps[name] = nc.dram_tensor(f"in_{name}", v.shape, mybir.dt.from_np(v.dtype), kind="ExternalInput").ap()
    aps["scratch"] = nc.dram_tensor("scratch", (B, H, W, C), F32, kind="Internal").ap()
    aps["out"] = nc.dram_tensor("out_dram", (B, H, W, C), F32, kind="ExternalOutput").ap()
    build(nc, aps)
    r = run_bass_kernel_spmd(nc, [arrays], core_ids=[0])
    return r.results[0]["out_dram"]
```
